# Optimizing a Trainium2 kernel written in Bass

```python
import numpy as np
import jax
import jax.numpy as jnp

def _softmax(x, axis=-1):
    return jax.nn.softmax(x, axis=axis)

def _gelu(x):
    return jax.nn.gelu(x, approximate=True)

def _silu(x):
    return jax.nn.silu(x)

def _sigmoid(x):
    return jax.nn.sigmoid(x)

def _layernorm(x, axis=-1, eps=1e-05):
    m = jnp.mean(x, axis=axis, keepdims=True)
    v = jnp.var(x, axis=axis, keepdims=True)
    return (x - m) / jnp.sqrt(v + eps)

def _scatter_add(tgt, idx, src, axis=0):
    return tgt.at[idx].add(src)

def _segment_sum(src, seg, n):
    return jax.ops.segment_sum(src, seg, n)
kernel_name = 'mk_prb_d1_jaxref_r8_f80d06'

def setup_inputs(seed: int=0):
    np.random.seed(seed)
    _w = jnp.asarray

    def _L0_attn_setup():
        import jax, jax.numpy as jnp
        import numpy as np
        B, T, DIM, H = (4, 128, 128, 16)
        D = DIM // H

        def _lin(x, Wt, bias):
            return x @ Wt.T + bias

        def _l2norm(x, eps=1e-12):
            n = jnp.sqrt(jnp.sum(x * x, axis=-1, keepdims=True))
            return x / jnp.maximum(n, eps)
        key = jax.random.key(seed)
        ks = jax.random.split(key, 18)
        W = lambda k: jax.random.normal(k, (DIM, DIM), jnp.float32) * 0.02
        b = lambda k: jax.random.normal(k, (DIM,), jnp.float32) * 0.02
        return {'x': jax.random.normal(ks[0], (B, T, DIM), jnp.float32), 'Wsq': W(ks[1]), 'bsq': b(ks[2]), 'Wsk': W(ks[3]), 'bsk': b(ks[4]), 'Wsv': W(ks[5]), 'bsv': b(ks[6]), 'Wg': jax.random.normal(ks[7], (H, DIM), jnp.float32) * 0.02, 'bg': jax.random.normal(ks[8], (H,), jnp.float32) * 0.02, 'Wq': W(ks[9]), 'bq': b(ks[10]), 'Wk': W(ks[11]), 'bk': b(ks[12]), 'Wv': W(ks[13]), 'bv': b(ks[14]), 'Wo': W(ks[15]), 'bo': b(ks[16]), 'temp': jnp.ones((1, H, 1, 1), jnp.float32)}
    _L0_attn_in = _L0_attn_setup()

    def _L0_ffn_setup():
        import jax, jax.numpy as jnp
        import numpy as np
        L, H, NH, NKV, HD, FF, E, K = (4, 128, 16, 4, 64, 256, 8, 2)
        B, S = (2, 256)
        THETA, EPS = (10000.0, 1e-05)

        def _rms(x, w):
            return x * jax.lax.rsqrt(jnp.mean(x * x, axis=-1, keepdims=True) + EPS) * w

        def _rope_cos_sin(seq_len, head_dim, theta):
            inv = 1.0 / theta ** (jnp.arange(0, head_dim, 2, dtype=jnp.float32) / head_dim)
            f = jnp.arange(seq_len, dtype=jnp.float32)[:, None] * inv
            emb = jnp.concatenate([f, f], axis=-1)
            return (jnp.cos(emb), jnp.sin(emb))

        def _rot_half(x):
            h = x.shape[-1] // 2
            return jnp.concatenate([-x[..., h:], x[..., :h]], axis=-1)

        def _attention(x, wq, wk, wv, wo, cos, sin, causal_bias):
            b, s, _ = x.shape
            q = (x @ wq).reshape(b, s, NH, HD).transpose(0, 2, 1, 3)
            k = (x @ wk).reshape(b, s, NKV, HD).transpose(0, 2, 1, 3)
            v = (x @ wv).reshape(b, s, NKV, HD).transpose(0, 2, 1, 3)
            c = cos[None, None]
            sn = sin[None, None]
            q = q * c + _rot_half(q) * sn
            k = k * c + _rot_half(k) * sn
            rep = NH // NKV
            k = jnp.repeat(k, rep, axis=1)
            v = jnp.repeat(v, rep, axis=1)
            scores = jnp.einsum('bhqd,bhkd->bhqk', q, k) / jnp.sqrt(jnp.asarray(HD, x.dtype))
            scores = scores + causal_bias
            attn = jax.nn.softmax(scores, axis=-1)
            out = jnp.einsum('bhqk,bhkd->bhqd', attn, v)
            out = out.transpose(0, 2, 1, 3).reshape(b, s, NH * HD)
            return out @ wo

        def _moe(x, wr, wg, wu, wd):
            logits = x @ wr
            probs = jax.nn.softmax(logits, axis=-1)
            topv, topi = jax.lax.top_k(probs, K)
            topv = topv / jnp.sum(topv, axis=-1, keepdims=True)
            comb = jnp.sum(jax.nn.one_hot(topi, E, dtype=x.dtype) * topv[..., None], axis=-2)
            out = jnp.zeros_like(x)
            for e in range(E):
                h = jax.nn.silu(x @ wg[e]) * (x @ wu[e])
                out = out + comb[..., e:e + 1] * (h @ wd[e])
            return out
        key = jax.random.key(seed)
        ks = jax.random.split(key, 12)
        sc = 0.02
        inp = {'hidden_states': jax.random.normal(ks[0], (B, S, H), jnp.float32), 'ln1_w': jnp.ones((L, H), jnp.float32), 'ln2_w': jnp.ones((L, H), jnp.float32), 'wq': jax.random.normal(ks[1], (L, H, NH * HD), jnp.float32) * sc, 'wk': jax.random.normal(ks[2], (L, H, NKV * HD), jnp.float32) * sc, 'wv': jax.random.normal(ks[3], (L, H, NKV * HD), jnp.float32) * sc, 'wo': jax.random.normal(ks[4], (L, NH * HD, H), jnp.float32) * sc, 'wr': jax.random.normal(ks[5], (L, H, E), jnp.float32) * sc, 'wg': jax.random.normal(ks[6], (L, E, H, FF), jnp.float32) * sc, 'wu': jax.random.normal(ks[7], (L, E, H, FF), jnp.float32) * sc, 'wd': jax.random.normal(ks[8], (L, E, FF, H), jnp.float32) * sc}
        return inp
    _L0_ffn_in = _L0_ffn_setup()
    _d = {'L0_attn_x': _L0_attn_in['x'], 'L0_attn_Wsq': _L0_attn_in['Wsq'], 'L0_attn_bsq': _L0_attn_in['bsq'], 'L0_attn_Wsk': _L0_attn_in['Wsk'], 'L0_attn_bsk': _L0_attn_in['bsk'], 'L0_attn_Wsv': _L0_attn_in['Wsv'], 'L0_attn_bsv': _L0_attn_in['bsv'], 'L0_attn_Wg': _L0_attn_in['Wg'], 'L0_attn_bg': _L0_attn_in['bg'], 'L0_attn_Wq': _L0_attn_in['Wq'], 'L0_attn_bq': _L0_attn_in['bq'], 'L0_attn_Wk': _L0_attn_in['Wk'], 'L0_attn_bk': _L0_attn_in['bk'], 'L0_attn_Wv': _L0_attn_in['Wv'], 'L0_attn_bv': _L0_attn_in['bv'], 'L0_attn_Wo': _L0_attn_in['Wo'], 'L0_attn_bo': _L0_attn_in['bo'], 'L0_attn_temp': _L0_attn_in['temp'], 'L0_ffn_ln1_w': _L0_ffn_in['ln1_w'], 'L0_ffn_ln2_w': _L0_ffn_in['ln2_w'], 'L0_ffn_wq': _L0_ffn_in['wq'], 'L0_ffn_wk': _L0_ffn_in['wk'], 'L0_ffn_wv': _L0_ffn_in['wv'], 'L0_ffn_wo': _L0_ffn_in['wo'], 'L0_ffn_wr': _L0_ffn_in['wr'], 'L0_ffn_wg': _L0_ffn_in['wg'], 'L0_ffn_wu': _L0_ffn_in['wu'], 'L0_ffn_wd': _L0_ffn_in['wd']}
    _x0 = _d['L0_attn_x']
    _d['L0_attn_x'] = jax.random.normal(jax.random.fold_in(jax.random.key(seed), 1), (2, 1024, 128), dtype=_x0.dtype)
    del _x0
    return _d

def reference(L0_attn_x, L0_attn_Wsq, L0_attn_bsq, L0_attn_Wsk, L0_attn_bsk, L0_attn_Wsv, L0_attn_bsv, L0_attn_Wg, L0_attn_bg, L0_attn_Wq, L0_attn_bq, L0_attn_Wk, L0_attn_bk, L0_attn_Wv, L0_attn_bv, L0_attn_Wo, L0_attn_bo, L0_attn_temp, L0_ffn_ln1_w, L0_ffn_ln2_w, L0_ffn_wq, L0_ffn_wk, L0_ffn_wv, L0_ffn_wo, L0_ffn_wr, L0_ffn_wg, L0_ffn_wu, L0_ffn_wd):

    def _L0_attn_ref(x, Wsq, bsq, Wsk, bsk, Wsv, bsv, Wg, bg, Wq, bq, Wk, bk, Wv, bv, Wo, bo, temp):
        import jax, jax.numpy as jnp
        import numpy as np
        B, T, DIM, H = (4, 128, 128, 16)
        D = DIM // H

        def _lin(x, Wt, bias):
            return x @ Wt.T + bias

        def _l2norm(x, eps=1e-12):
            n = jnp.sqrt(jnp.sum(x * x, axis=-1, keepdims=True))
            return x / jnp.maximum(n, eps)
        Bx, Tx, C = x.shape
        nh, hd = (H, C // H)
        sq = _lin(x, Wsq, bsq).reshape(Bx, Tx, nh, hd)
        sk = _lin(x, Wsk, bsk).reshape(Bx, Tx, nh, hd)
        sv = _lin(x, Wsv, bsv).reshape(Bx, Tx, nh, hd)
        g = jnp.exp(-jax.nn.softplus(_lin(x, Wg, bg)))

        def step(M, inp):
            g_t, k_t, v_t, q_t = inp
            M = g_t[..., None, None] * M + k_t[..., None] * v_t[..., None, :]
            h = jnp.einsum('bhd,bhde->bhe', q_t, M)
            return (M, h)
        xs = (g.transpose(1, 0, 2), sk.transpose(1, 0, 2, 3), sv.transpose(1, 0, 2, 3), sq.transpose(1, 0, 2, 3))
        M0 = jnp.zeros((Bx, nh, hd, hd), x.dtype)
        _, hs = jax.lax.scan(step, M0, xs)
        Hseq = hs.transpose(1, 0, 2, 3).reshape(Bx, Tx, C)
        Q = _lin(Hseq, Wq, bq).reshape(Bx, Tx, nh, hd).transpose(0, 2, 1, 3)
        K = _lin(Hseq, Wk, bk).reshape(Bx, Tx, nh, hd).transpose(0, 2, 1, 3)
        V = _lin(x, Wv, bv).reshape(Bx, Tx, nh, hd).transpose(0, 2, 1, 3)
        Q = _l2norm(Q)
        K = _l2norm(K)
        scores = jnp.einsum('bhqd,bhkd->bhqk', Q, K) * jax.nn.softplus(temp)
        attn = jax.nn.softmax(scores, axis=-1)
        out = jnp.einsum('bhqk,bhkd->bhqd', attn, V).transpose(0, 2, 1, 3).reshape(Bx, Tx, C)
        return _lin(out, Wo, bo)

    def _L0_ffn_ref(hidden_states, ln1_w, ln2_w, wq, wk, wv, wo, wr, wg, wu, wd):
        import jax, jax.numpy as jnp
        import numpy as np
        L, H, NH, NKV, HD, FF, E, K = (4, 128, 16, 4, 64, 256, 8, 2)
        B, S = (2, 256)
        THETA, EPS = (10000.0, 1e-05)

        def _rms(x, w):
            return x * jax.lax.rsqrt(jnp.mean(x * x, axis=-1, keepdims=True) + EPS) * w

        def _rope_cos_sin(seq_len, head_dim, theta):
            inv = 1.0 / theta ** (jnp.arange(0, head_dim, 2, dtype=jnp.float32) / head_dim)
            f = jnp.arange(seq_len, dtype=jnp.float32)[:, None] * inv
            emb = jnp.concatenate([f, f], axis=-1)
            return (jnp.cos(emb), jnp.sin(emb))

        def _rot_half(x):
            h = x.shape[-1] // 2
            return jnp.concatenate([-x[..., h:], x[..., :h]], axis=-1)

        def _attention(x, wq, wk, wv, wo, cos, sin, causal_bias):
            b, s, _ = x.shape
            q = (x @ wq).reshape(b, s, NH, HD).transpose(0, 2, 1, 3)
            k = (x @ wk).reshape(b, s, NKV, HD).transpose(0, 2, 1, 3)
            v = (x @ wv).reshape(b, s, NKV, HD).transpose(0, 2, 1, 3)
            c = cos[None, None]
            sn = sin[None, None]
            q = q * c + _rot_half(q) * sn
            k = k * c + _rot_half(k) * sn
            rep = NH // NKV
            k = jnp.repeat(k, rep, axis=1)
            v = jnp.repeat(v, rep, axis=1)
            scores = jnp.einsum('bhqd,bhkd->bhqk', q, k) / jnp.sqrt(jnp.asarray(HD, x.dtype))
            scores = scores + causal_bias
            attn = jax.nn.softmax(scores, axis=-1)
            out = jnp.einsum('bhqk,bhkd->bhqd', attn, v)
            out = out.transpose(0, 2, 1, 3).reshape(b, s, NH * HD)
            return out @ wo

        def _moe(x, wr, wg, wu, wd):
            logits = x @ wr
            probs = jax.nn.softmax(logits, axis=-1)
            topv, topi = jax.lax.top_k(probs, K)
            topv = topv / jnp.sum(topv, axis=-1, keepdims=True)
            comb = jnp.sum(jax.nn.one_hot(topi, E, dtype=x.dtype) * topv[..., None], axis=-2)
            out = jnp.zeros_like(x)
            for e in range(E):
                h = jax.nn.silu(x @ wg[e]) * (x @ wu[e])
                out = out + comb[..., e:e + 1] * (h @ wd[e])
            return out
        s = hidden_states.shape[1]
        cos, sin = _rope_cos_sin(s, HD, THETA)
        causal_bias = jnp.where(jnp.tril(jnp.ones((s, s), bool))[None, None], 0.0, -1000000000.0).astype(hidden_states.dtype)
        x = hidden_states
        for l in range(L):
            res = x
            h = _rms(x, ln1_w[l])
            h = _attention(h, wq[l], wk[l], wv[l], wo[l], cos, sin, causal_bias)
            x = jnp.clip(res + h, -100.0, 100.0)
            res = x
            h = _rms(x, ln2_w[l])
            h = _moe(h, wr[l], wg[l], wu[l], wd[l])
            x = jnp.clip(res + h, -100.0, 100.0)
        return x
    x = L0_attn_x
    xn = _layernorm(x, axis=-1)
    x = x + _L0_attn_ref(xn, L0_attn_Wsq, L0_attn_bsq, L0_attn_Wsk, L0_attn_bsk, L0_attn_Wsv, L0_attn_bsv, L0_attn_Wg, L0_attn_bg, L0_attn_Wq, L0_attn_bq, L0_attn_Wk, L0_attn_bk, L0_attn_Wv, L0_attn_bv, L0_attn_Wo, L0_attn_bo, L0_attn_temp) + _L0_ffn_ref(xn, L0_ffn_ln1_w, L0_ffn_ln2_w, L0_ffn_wq, L0_ffn_wk, L0_ffn_wv, L0_ffn_wo, L0_ffn_wr, L0_ffn_wg, L0_ffn_wu, L0_ffn_wd)
    return x

_drawn_inputs = setup_inputs


def setup_inputs(seed=0):
    import zlib

    import numpy as np

    out = dict(_drawn_inputs(seed))
    spreads = {'L0_attn_temp': (1.0, 0.6), 'L0_ffn_ln1_w': (1.0, 0.6), 'L0_ffn_ln2_w': (1.0, 0.6)}
    factors = {'L0_attn_Wsq': 64.0,
     'L0_attn_bsq': 200.0,
     'L0_attn_Wsk': 64.0,
     'L0_attn_bsk': 200.0,
     'L0_attn_Wsv': 64.0,
     'L0_attn_bsv': 200.0,
     'L0_attn_Wg': 64.0,
     'L0_attn_bg': 200.0,
     'L0_attn_Wq': 64.0,
     'L0_attn_bq': 200.0,
     'L0_attn_Wk': 64.0,
     'L0_attn_bk': 200.0,
     'L0_attn_Wv': 64.0,
     'L0_attn_bv': 33.747,
     'L0_attn_Wo': 29.834,
     'L0_attn_bo': 43.8,
     'L0_ffn_wq': 8.0,
     'L0_ffn_wk': 8.0,
     'L0_ffn_wv': 4.085,
     'L0_ffn_wo': 4.152,
     'L0_ffn_wr': 8.0,
     'L0_ffn_wg': 8.0,
     'L0_ffn_wu': 8.0,
     'L0_ffn_wd': 8.0}
    for name, (base, spread) in spreads.items():
        noise = np.random.default_rng([zlib.crc32(name.encode()), seed]).standard_normal(out[name].shape)
        drawn = base * np.exp(spread * noise) if base else spread * noise
        out[name] = jnp.asarray(drawn.astype(out[name].dtype))
    for name, factor in factors.items():
        out[name] = (out[name] * factor).astype(out[name].dtype)
    return out
```

```python
import math
from contextlib import ExitStack

import numpy as np

import concourse.bass as bass
import concourse.mybir as mybir

F32 = mybir.dt.float32
F32R = mybir.dt.float32r
BF16 = mybir.dt.bfloat16
ALU = mybir.AluOpType
ACT = mybir.ActivationFunctionType
AX = mybir.AxisListType

P = 128
BATCH, T, C = 2, 1024, 128
TT = T // P
HALF = 512
LAYERS = 4
NH, NKV, HD = 16, 4, 64
REP = NH // NKV
GW = REP * HD + 2 * HD
ROT = REP * HD + HD
FF, EXPERTS = 256, 8
FCH = FF // P
EPS = 1e-5
RAW = 4
WRING = 4
AH, AD = 16, 8
STATES = AH * AD * AD
STATE_TILES = STATES // P
TALL = 80.0
LIMIT = 100.0
FAR = -1e9
MROW = 64
KROWS = 96



def attention_steps():
    steps = []
    for g in range(NKV):
        for h in range(REP):
            for qc in range(2):
                for pair in range(2 * (qc + 1)):
                    local = pair - 2 * qc
                    steps.append((g, h, qc, 2 * pair, 256 if local == 1 else 0, local >= 0))
    return steps


def preparation_units(g):
    units = [("project", g, tt) for tt in range(TT)]
    units += [("turn", g, REP, half) for half in range(2)]
    for pair in range(REP // 2):
        units += [("turn", g, 2 * pair, half) for half in range(2)]
        for j in (2 * pair, 2 * pair + 1):
            for qb in range(TT):
                keys = (qb + 1) * P
                units.append(("coarse", g, j, qb, 0, min(keys, HALF)))
                if keys > HALF:
                    units.append(("coarse", g, j, qb, HALF, keys - HALF))
    units.append(("maxima", g))
    return units


STEPS = attention_steps()
UNITS = [u for g in range(NKV) for u in preparation_units(g)]
PER_GROUP = len(UNITS) // NKV
STEPS_PER_GROUP = len(STEPS) // NKV


def units_at(s):
    g, i = divmod(s, STEPS_PER_GROUP)
    if g + 1 == NKV:
        return []
    span = STEPS_PER_GROUP - 2
    a, b = (min(PER_GROUP, math.ceil(k * PER_GROUP / span)) for k in (i, i + 1))
    return list(range((g + 1) * PER_GROUP + a, (g + 1) * PER_GROUP + b))


def ordinal(kind, n):
    return sum(u[0] == kind for u in UNITS[:n + 1])


CHUNK_END = [s for s, st in enumerate(STEPS) if st[3] == (2 if st[2] == 0 else 6)]
CHUNKS = len(CHUNK_END)


class Core:

    def __init__(self, nc, ctx):
        self.nc, self.ctx = nc, ctx
        self.sems = []

    def sb(self, name, shape, dt=F32):
        return self.ctx.enter_context(self.nc.sbuf_tensor(name, shape, dt))

    def psum(self, name, shape, dt=F32):
        return self.ctx.enter_context(self.nc.psum_tensor(name, shape, dt))

    def sem(self, name):
        s = self.ctx.enter_context(self.nc.semaphore(name))
        self.sems.append(s)
        return s

    def clear_semaphores(self):
        numbers = [s.num for s in self.sems]
        self.nc.sync.sem_clear(range(min(numbers), max(numbers) + 1))
        self.nc.all_engine_barrier()


def first_constants(nc, m, d):
    with nc.Block() as block:
        @block.sync
        def _(sp):
            sp.dma_start(m.cos[:, :, :], d["cos"].rearrange("(t p) f -> p t f", p=P)).then_inc(m.s_load, 16)
            sp.dma_start(m.sin[:, :, :], d["sin"].rearrange("(t p) f -> p t f", p=P)).then_inc(m.s_load, 16)
            sp.wait_ge(m.s_load, 32)

        @block.gpsimd
        def _(pool):
            pool.memset(m.ident[:, :], 0.0).then_inc(m.s_set, 1)
            pool.memset(m.later[:, :], 0.0).then_inc(m.s_set, 1)
            pool.wait_ge(m.s_set, 2)
            pool.affine_select(out=m.ident[:, :], in_=m.ident[:, :], compare_op=ALU.not_equal, fill=1.0, base=0,
                               pattern=[[-1, P]], channel_multiplier=1).then_inc(m.s_set, 1)
            pool.affine_select(out=m.later[:, :], in_=m.later[:, :], compare_op=ALU.is_ge, fill=FAR, base=0,
                               pattern=[[-1, P]], channel_multiplier=1).then_inc(m.s_set, 1)
            pool.wait_ge(m.s_set, 4)
            pool.tensor_copy(m.ident16[:, :], m.ident[:, :]).then_inc(m.s_set, 1)
            pool.tensor_copy(m.later16[:, :], m.later[:, :]).then_inc(m.s_set, 1)
            pool.wait_ge(m.s_set, 6)

        @block.vector
        def _(dve):
            dve.memset(m.eps[:, :], EPS).then_inc(m.s_ones, 1)
            dve.wait_ge(m.s_ones, 1)
    m.clear_semaphores()


def decoder_constants(nc, m):
    with nc.Block() as block:
        @block.vector
        def _(dve):
            for v in m.vones:
                dve.memset(v[:, :, :], 1.0).then_inc(m.s_ones, 1)
            for q in m.q_shift:
                dve.memset(q[MROW:KROWS, :, :].bitcast(F32), 0.0).then_inc(m.s_ones, 1)
            for k in m.k_rest:
                dve.memset(k[MROW:KROWS, :].bitcast(F32), 0.0).then_inc(m.s_ones, 1)
            dve.wait_ge(m.s_ones, 6)
            for k in m.k_rest:
                dve.memset(k[MROW:MROW + 1, :].bitcast(F32), 1.0).then_inc(m.s_ones, 1)
            for e in range(EXPERTS):
                dve.memset(m.expert_no[:, :, e:e + 1], float(e)).then_inc(m.s_ones, 1)
            dve.wait_ge(m.s_ones, 8 + EXPERTS)
    m.clear_semaphores()


def load_expert(sp, m, d, layer, e):
    i = e % WRING
    sp.dma_start(m.wg[:, i, :], d["wg"][layer, e]).then_inc(m.s_expert[i], 16)
    sp.dma_start(m.wu[:, i, :], d["wu"][layer, e]).then_inc(m.s_expert[i], 16)
    sp.dma_start(m.wd[:, i, :, :], d["wd"][layer, e].rearrange("(j p) c -> p j c", p=P)).then_inc(m.s_expert[i], 16)


def attention_block(nc, m, d, layer):
    scores, heads, aux = m.pair_bank, m.bank[4:6], m.bank[6:8]
    with nc.Block() as block:
        @block.sync
        def _(sp):
            sp.dma_start(m.ln1[:, :], d["ln1_w"][layer].rearrange("(c o) -> c o", o=1)).then_inc(m.s_load, 16)
            sp.dma_start(m.wqkv[:, :, 0:REP * HD], d["wq"][layer].rearrange("c (g n) -> c g n", g=NKV)).then_inc(m.s_load, 16)
            sp.dma_start(m.wqkv[:, :, REP * HD:ROT], d["wk"][layer].rearrange("c (g n) -> c g n", g=NKV)).then_inc(m.s_load, 16)
            sp.dma_start(m.wqkv[:, :, ROT:GW], d["wv"][layer].rearrange("c (g n) -> c g n", g=NKV)).then_inc(m.s_load, 16)
            sp.dma_start(m.wo[:, :, :], d["wo"][layer].rearrange("(j p) c -> p j c", p=P)).then_inc(m.s_load_wo, 16)
            sp.dma_start(m.ln2[:, :], d["ln2_w"][layer].rearrange("(c o) -> c o", o=1)).then_inc(m.s_load_moe, 16)
            sp.dma_start(m.wr[:, :], d["wr"][layer]).then_inc(m.s_load_moe, 16)
            for e in range(WRING):
                load_expert(sp, m, d, layer, e)
            for g in range(NKV):
                sp.wait_ge(m.s_maxrow, g + 1)
                sp.dma_start(m.scratch[g % 2], m.maxrow[g % 2][:, :].bitcast(F32)).then_inc(m.s_scratch[g % 2], 16)
                sp.wait_ge(m.s_scratch[g % 2], 16 * (g // 2 + 1))
                if g >= 2:
                    sp.wait_ge(m.s_pv, (g - 1) * STEPS_PER_GROUP)
                sp.dma_start(m.q_shift[g % 2][MROW:MROW + 1, :, :].rearrange("o h (b c) -> o (h b) c", c=P).bitcast(F32),
                             m.scratch[g % 2].unsqueeze(0)).then_inc(m.s_shift[g % 2], 16)
            sp.wait_ge(m.s_load_moe, 2 * 16)
            for e in range(WRING):
                sp.wait_ge(m.s_expert[e], 3 * 16)

        @block.vector
        def _(dve):
            dve.tensor_tensor(m.square[:, :, :], m.x[:, :, :], m.x[:, :, :], ALU.mult).then_inc(m.s_norm_v, 1)
            dve.wait_ge(m.s_norm_v, 1)
            dve.reduce_sum(m.stat[:, 0, :], m.square[:, :, :], AX.X).then_inc(m.s_norm_v, 1)
            dve.wait_ge(m.s_norm_a, 2)
            dve.tensor_tensor(m.square[:, :, :], m.x[:, :, :], m.stat[:, 2, :].unsqueeze(2).broadcast_to([P, TT, P]),
                              ALU.mult).then_inc(m.s_norm_v, 1)
            stored = 0

            def unit(n):
                kind, g = UNITS[n][0:2]
                buf = g % 2
                if kind == "project":
                    tt = UNITS[n][2]
                    if tt % 2 == 0:
                        return
                    dve.wait_ge(m.s_raw, g * TT + tt + 1)
                    a = slice(tt - 1, tt + 1)
                    r = slice((tt - 1) % RAW, (tt - 1) % RAW + 2)
                    dve.tensor_tensor(m.rotated[:, a, :, :], m.raw[:, r, :, :],
                                      m.cos[:, a, :].unsqueeze(2).broadcast_to([P, 2, REP + 1, HD]),
                                      ALU.mult).then_inc(m.s_cos, 1)
                    i = g * TT // 2 + tt // 2 + 1
                    dve.wait_ge(m.s_sin, i)
                    dve.wait_ge(m.s_cos, i)
                    dve.tensor_tensor(m.rotated[:, a, :, :], m.rotated[:, a, :, :], m.swapped[:, r, :, :],
                                      ALU.add).then_inc(m.s_rotated, 1)
                elif kind == "turn":
                    j, half = UNITS[n][2:4]
                    cols = slice(half * HALF, (half + 1) * HALF)
                    dve.wait_ge(m.s_high, ordinal("turn", n))
                    if j == REP:
                        dve.tensor_tensor(m.k_rest[buf][0:HD, cols], aux[n % 2][0:HD, :],
                                          m.k_twice[buf][0:HD, cols].bitcast(F32), ALU.subtract).then_inc(m.s_low, 1)
                    else:
                        for i in range(2):
                            dve.tensor_tensor(m.q_full[buf][HD:P, j + i, cols], aux[n % 2][i * HD:(i + 1) * HD, :],
                                              m.q_full[buf][0:HD, j + i, cols].bitcast(F32),
                                              ALU.subtract).then_inc(m.s_low if i else m.s_low0, 1)
                elif kind == "coarse":
                    j, qb, k0, keys = UNITS[n][2:6]
                    dve.wait_ge(m.s_unit, n + 1)
                    if g >= 2 and j == 0 and qb == 0:
                        dve.wait_ge(m.s_maxrow, g - 1)
                    to = m.maxima if k0 == 0 else m.maxima2
                    dve.reduce_max(to[buf][:, j, qb:qb + 1], aux[n % 2][:, 0:keys], AX.X).then_inc(m.s_max, 1)
                else:
                    dve.wait_ge(m.s_max, ordinal("coarse", n))
                    dve.tensor_tensor(m.maxima[buf][:, :, TT // 2:TT], m.maxima[buf][:, :, TT // 2:TT],
                                      m.maxima2[buf][:, :, TT // 2:TT], ALU.max).then_inc(m.s_rowmax, 1)

            def store(ch):
                g, h, qc = STEPS[CHUNK_END[ch]][0:3]
                head = g * REP + h
                dve.wait_ge(m.s_recip, ch + 1)
                dve.tensor_tensor(m.mixed[(head % 2) * HD:(head % 2 + 1) * HD, head // 2, qc * HALF:(qc + 1) * HALF],
                                  heads[ch % 2][0:HD, :], m.recip[ch % 2][:, :], ALU.mult).then_inc(m.s_stored, 1)

            for n in range(PER_GROUP):
                unit(n)
            for s in range(len(STEPS) + 4):
                if stored < CHUNKS and CHUNK_END[stored] + 3 <= s:
                    store(stored)
                    stored += 1
                for n in (units_at(s) if s < len(STEPS) else ()):
                    unit(n)
            dve.wait_ge(m.s_wo, 2)
            for i in range(2):
                a = slice(i * TT // 2, (i + 1) * TT // 2)
                dve.tensor_tensor(m.x[:, a, :], m.bank[i][:, :].rearrange("p (t c) -> p t c", c=C), m.x[:, a, :],
                                  ALU.add).then_inc(m.s_sum, 1)
            dve.wait_ge(m.s_sum, 2)
            dve.tensor_scalar(m.x[:, :, :], m.x[:, :, :], -LIMIT, LIMIT, ALU.max, ALU.min).then_inc(m.s_sum, 1)
            dve.wait_ge(m.s_sum, 3)

        @block.gpsimd
        def _(pool):
            def swap(n):
                kind, g, tt = UNITS[n][0:3]
                if tt % 2 == 0:
                    return
                a = slice(tt - 1, tt + 1)
                r = slice((tt - 1) % RAW, (tt - 1) % RAW + 2)
                i = g * TT // 2 + tt // 2
                pool.wait_ge(m.s_raw, g * TT + tt + 1)
                if i >= RAW // 2:
                    pool.wait_ge(m.s_rotated, i + 1 - RAW // 2)
                for f in range(2):
                    pool.tensor_tensor(m.swapped[:, r, :, f * 32:f * 32 + 32], m.raw[:, r, :, 32 - f * 32:64 - f * 32],
                                       m.sin[:, a, f * 32:f * 32 + 32].unsqueeze(2).broadcast_to([P, 2, REP + 1, 32]),
                                       ALU.mult).then_inc(m.s_sin if f else m.s_sin0, 1)

            def mask(s):
                g, h, qc, kb, q0, diagonal = STEPS[s]
                if not diagonal:
                    return
                pool.wait_ge(m.s_probs, s + 1)
                v = m.probs[s % 3][:, :, q0:q0 + 256]
                pool.affine_select(out=v, in_=v, compare_op=ALU.is_ge, fill=0.0,
                                   base=qc * HALF + q0 - kb * P, pattern=[[-P, 2], [1, 256]],
                                   channel_multiplier=-1).then_inc(m.s_masked, 1)

            for n in range(PER_GROUP):
                if UNITS[n][0] == "project":
                    swap(n)
            for s in range(len(STEPS)):
                mask(s)
                for n in units_at(s):
                    if UNITS[n][0] == "project":
                        swap(n)

        @block.scalar
        def _(act):
            act.preload_act_table_set("natural_log_exp_and_others")
            act.wait_ge(m.s_norm_v, 2)
            act.activation(m.stat[:, 1, :], m.stat[:, 0, :], ACT.Ln, bias=m.eps[:, 0:1], scale=1.0 / C).then_inc(m.s_norm_a, 1)
            act.wait_ge(m.s_norm_a, 1)
            act.activation(m.stat[:, 2, :], m.stat[:, 1, :], ACT.Exp, scale=-0.5).then_inc(m.s_norm_a, 1)
            act.wait_ge(m.s_load, 4 * 16)
            for i in range(2):
                act.wait_ge(m.s_turn_x, i + 1)
                act.mul(m.hT[:, i * HALF:(i + 1) * HALF], m.bank[i][:, :], m.ln1[:, 0:1]).then_inc(m.s_hT, 1)

            def unit(n):
                kind, g = UNITS[n][0:2]
                buf = g % 2
                if kind == "project":
                    tt = UNITS[n][2]
                    act.wait_ge(m.s_unit, n + 1)
                    if g >= 2:
                        act.wait_ge(m.s_pv, (g - 1) * STEPS_PER_GROUP)
                    act.copy(m.vones[buf][:, tt, 0:HD], aux[n % 2][:, ROT:GW]).then_inc(m.s_value, 1)
                    before = (g * TT + tt - RAW) // 2 + 1
                    if before > 0:
                        act.wait_ge(m.s_cos, before)
                        act.wait_ge(m.s_sin, before)
                    act.copy(m.raw[:, tt % RAW, :, :], aux[n % 2][:, 0:ROT].rearrange("p (h e) -> p h e", e=HD)).then_inc(m.s_raw, 1)
                elif kind == "turn":
                    j, half = UNITS[n][2:4]
                    cols = slice(half * HALF, (half + 1) * HALF)
                    act.wait_ge(m.s_unit, n + 1)
                    if g >= 2:
                        act.wait_ge(m.s_pv, (g - 1) * STEPS_PER_GROUP)
                    if j == REP:
                        act.copy(m.k_twice[buf][HD:P, cols], aux[n % 2][0:HD, :]).then_inc(m.s_high0, 1)
                        act.copy(m.k_twice[buf][0:HD, cols], aux[n % 2][0:HD, :]).then_inc(m.s_high, 1)
                    else:
                        for i in range(2):
                            half_rows = aux[n % 2][i * HD:(i + 1) * HD, :]
                            act.copy(m.q_shift[buf][0:HD, j + i, cols], half_rows).then_inc(m.s_high0, 1)
                            act.copy(m.q_full[buf][0:HD, j + i, cols], half_rows).then_inc(m.s_high if i else m.s_high0, 1)
                elif kind == "maxima":
                    act.wait_ge(m.s_unit, n + 1)
                    if g >= 2:
                        act.wait_ge(m.s_shift[buf], 16)
                    act.mul(m.maxrow[buf][:, :], aux[n % 2][0:REP * TT, 0:P], -1.0).then_inc(m.s_maxrow, 1)

            def exponentials(s):
                q0 = STEPS[s][4]
                act.wait_ge(m.s_scores, s + 1)
                if s >= 3:
                    act.wait_ge(m.s_pv, s - 2)
                act.activation(m.probs[s % 3][:, :, q0:HALF],
                               scores[s % 2][:, :].rearrange("p (k q) -> p k q", k=2)[:, :, q0:HALF],
                               ACT.Exp, scale=1.0 / math.sqrt(HD)).then_inc(m.s_probs, 1)

            def reciprocals(ch):
                act.wait_ge(m.s_pv, CHUNK_END[ch] + 1)
                if ch >= 2:
                    act.wait_ge(m.s_stored, ch - 1)
                act.activation(m.recip[ch % 2][:, :], heads[ch % 2][HD:P, :], ACT.Ln).then_inc(m.s_logden, 1)
                act.wait_ge(m.s_logden, ch + 1)
                act.activation(m.recip[ch % 2][:, :], m.recip[ch % 2][:, :], ACT.Exp, scale=-1.0).then_inc(m.s_recip, 1)

            for n in range(PER_GROUP):
                unit(n)
            done = 0
            for s in range(len(STEPS) + 3):
                if s < len(STEPS):
                    exponentials(s)
                    for n in units_at(s):
                        unit(n)
                if done < CHUNKS and CHUNK_END[done] + 2 <= s:
                    reciprocals(done)
                    done += 1

        @block.tensor
        def _(pe):
            pe.wait_ge(m.s_norm_v, 3)
            for tt in range(TT):
                mm = pe.transpose(m.bank[tt // 4][:, (tt % 4) * P:(tt % 4 + 1) * P], m.square[:, tt, :], m.ident[:, :])
                if tt % 4 == 3:
                    mm.then_inc(m.s_turn_x, 1)

            def released(n):
                kind = UNITS[n][0]
                sem = {"project": m.s_raw, "turn": m.s_low, "coarse": m.s_max, "maxima": m.s_maxrow}[kind]
                pe.wait_ge(sem, ordinal(kind, n))

            def unit(n):
                kind, g = UNITS[n][0:2]
                buf, to = g % 2, aux[n % 2]
                if n >= 2:
                    released(n - 2)
                if kind == "project":
                    tt = UNITS[n][2]
                    if n < TT:
                        pe.wait_ge(m.s_hT, tt // 4 + 1)
                    mm = pe.matmul(to[:, 0:GW], m.hT[:, tt * P:(tt + 1) * P], m.wqkv[:, g, :], start=True, stop=True)
                    mm.then_inc(m.s_unit, 1)
                elif kind == "turn":
                    j, half = UNITS[n][2:4]
                    pe.wait_ge(m.s_rotated, (g * TT + half * 4) // 2 + 2)
                    heads_here = slice(j, j + (1 if j == REP else 2))
                    for i in range(4):
                        rows = m.rotated[:, half * 4 + i, heads_here, :].rearrange("p h e -> p (h e)")
                        mm = pe.transpose(to[0:rows.shape[1], i * P:(i + 1) * P], rows, m.ident[:, :])
                    mm.then_inc(m.s_unit, 1)
                elif kind == "coarse":
                    j, qb, k0, keys = UNITS[n][2:6]
                    if k0 == 0:
                        pe.wait_ge(m.s_low, ordinal("turn", n) if qb >= 4 else ordinal("turn", n) - 1)
                    diagonal = k0 + keys == (qb + 1) * P
                    mm = pe.matmul(to[:, 0:keys], m.q_full[buf][:, j, qb * P:(qb + 1) * P], m.k_twice[buf][:, k0:k0 + keys],
                                   start=True, stop=not diagonal)
                    if diagonal:
                        mm = pe.matmul(to[:, keys - P:keys], m.ident16[:, :], m.later16[:, :], start=False, stop=True)
                    mm.then_inc(m.s_unit, 1)
                else:
                    pe.wait_ge(m.s_rowmax, g + 1)
                    mm = pe.transpose(to[0:REP * TT, 0:P], m.maxima[buf][:, :, :], m.ident[:, :])
                    mm.then_inc(m.s_unit, 1)

            def score(s):
                g, h, qc, kb, q0, _ = STEPS[s]
                buf = g % 2
                if s % STEPS_PER_GROUP == 0:
                    last = (g + 1) * PER_GROUP - 1
                    pe.wait_ge(m.s_low, ordinal("turn", last))
                    pe.wait_ge(m.s_value, TT * (g + 1))
                    pe.wait_ge(m.s_shift[buf], 16 * (g // 2 + 1))
                if s >= 2:
                    pe.wait_ge(m.s_probs, s - 1)
                cols = slice(qc * HALF + q0, (qc + 1) * HALF)
                for i in range(2):
                    keys = slice((kb + i) * P, (kb + i + 1) * P)
                    to = scores[s % 2][:, i * HALF + q0:(i + 1) * HALF]
                    pe.matmul(to, m.k_twice[buf][:, keys], m.q_full[buf][:, h, cols], start=True, stop=False)
                    mm = pe.matmul(to, m.k_rest[buf][:, keys], m.q_shift[buf][:, h, cols], start=False, stop=True)
                mm.then_inc(m.s_scores, 1)

            def mix(s):
                g, h, qc, kb, q0, diagonal = STEPS[s]
                ch = sum(e < s for e in CHUNK_END)
                if diagonal:
                    pe.wait_ge(m.s_masked, sum(st[5] for st in STEPS[:s + 1]))
                else:
                    pe.wait_ge(m.s_probs, s + 1)
                if kb == 0 and ch >= 2:
                    pe.wait_ge(m.s_stored, ch - 1)
                for i in range(2):
                    mm = pe.matmul(heads[ch % 2][:, q0:HALF], m.vones[g % 2][:, kb + i, :], m.probs[s % 3][:, i, q0:HALF],
                                   start=(kb + i == 0), stop=(s == CHUNK_END[ch] and i == 1))
                mm.then_inc(m.s_pv, 1)

            for n in range(PER_GROUP):
                unit(n)
            for s in range(len(STEPS)):
                score(s)
                if s:
                    mix(s - 1)
                for n in units_at(s):
                    unit(n)
            mix(len(STEPS) - 1)

            pe.wait_ge(m.s_load_wo, 16)
            pe.wait_ge(m.s_stored, CHUNKS)
            pe.wait_ge(m.s_probs, len(STEPS))
            for tt in range(TT):
                for j in range(NH // 2):
                    mm = pe.matmul(m.bank[tt // 4][:, (tt % 4) * C:(tt % 4 + 1) * C], m.mixed[:, j, tt * P:(tt + 1) * P],
                                   m.wo[:, j, :], start=(j == 0), stop=(j == NH // 2 - 1))
                if tt % 4 == 3:
                    mm.then_inc(m.s_wo, 1)
    m.clear_semaphores()


def moe_block(nc, m, d, layer):
    with nc.Block() as block:
        @block.sync
        def _(sp):
            for e in range(WRING, EXPERTS):
                sp.wait_ge(m.s_down_unit, FCH * (e - WRING + 1))
                load_expert(sp, m, d, layer, e)

        @block.vector
        def _(dve):
            dve.tensor_tensor(m.square[:, :, :], m.x[:, :, :], m.x[:, :, :], ALU.mult).then_inc(m.s_norm_v, 1)
            dve.wait_ge(m.s_norm_v, 1)
            dve.reduce_sum(m.stat[:, 0, :], m.square[:, :, :], AX.X).then_inc(m.s_norm_v, 1)
            dve.wait_ge(m.s_norm_a, 2)
            dve.tensor_tensor(m.square[:, :, :], m.x[:, :, :], m.stat[:, 2, :].unsqueeze(2).broadcast_to([P, TT, P]),
                              ALU.mult).then_inc(m.s_norm_v, 1)

            pick, k = m.pick, 0

            def wide(a):
                return a.unsqueeze(2).broadcast_to([P, TT, EXPERTS])

            def then(ins):
                nonlocal k
                k += 1
                ins.then_inc(m.s_pick, 1)
                dve.wait_ge(m.s_pick, k)

            def hot(values, to, largest, first):
                then(dve.reduce_max(largest, values, AX.X))
                then(dve.tensor_tensor(to, values, wide(largest), ALU.is_equal))
                then(dve.tensor_scalar(m.rank[:, :, :], m.expert_no[:, :, :], -1.0, float(EXPERTS), ALU.mult, ALU.add))
                then(dve.tensor_tensor(m.rank[:, :, :], m.rank[:, :, :], to, ALU.mult))
                then(dve.reduce_max(first, m.rank[:, :, :], AX.X))
                then(dve.tensor_tensor(to, m.rank[:, :, :], wide(first), ALU.is_equal))

            dve.wait_ge(m.s_router, 1)
            logits = m.bank[4][:, 0:TT * EXPERTS].rearrange("p (t e) -> p t e", e=EXPERTS)
            then(dve.reduce_max(m.top[:, 0, :], logits, AX.X))
            then(dve.tensor_tensor(pick[:, 0, :, :], logits, wide(m.top[:, 0, :]), ALU.subtract))
            dve.wait_ge(m.s_routed, 1)
            hot(pick[:, 1, :, :], pick[:, 2, :, :], m.top[:, 1, :], m.top[:, 2, :])
            then(dve.scalar_tensor_tensor(pick[:, 3, :, :], pick[:, 1, :, :], 1.0, pick[:, 2, :, :], ALU.add, ALU.mult))
            then(dve.tensor_tensor(pick[:, 3, :, :], pick[:, 1, :, :], pick[:, 3, :, :], ALU.subtract))
            hot(pick[:, 3, :, :], pick[:, 4, :, :], m.top[:, 3, :], m.top[:, 4, :])
            then(dve.tensor_tensor(pick[:, 4, :, :], pick[:, 4, :, :], pick[:, 2, :, :], ALU.add))
            then(dve.tensor_tensor(pick[:, 4, :, :], pick[:, 4, :, :], pick[:, 1, :, :], ALU.mult))
            then(dve.reduce_sum(m.top[:, 5, :], pick[:, 4, :, :], AX.X))
            then(dve.reciprocal(m.top[:, 6, :], m.top[:, 5, :]))
            then(dve.tensor_tensor(m.share[:, :, :], pick[:, 4, :, :], wide(m.top[:, 6, :]), ALU.mult))

            def gated(i):
                dve.wait_ge(m.s_silu, i + 1)
                dve.wait_ge(m.s_up, i + 1)
                if i >= 2:
                    dve.wait_ge(m.s_down_unit, i - 1)
                dve.tensor_tensor(m.act_in[i % 2][:, :], m.up_bank[:, :], m.silu[i % 2][:, :], ALU.mult).then_inc(m.s_gated, 1)

            def weigh(e):
                dve.wait_ge(m.s_down_unit, FCH * (e + 1))
                for tt in range(TT):
                    if tt == 0 and e:
                        dve.wait_ge(m.s_weighed, TT * e)
                    dve.scalar_tensor_tensor(m.moe[:, tt, :],
                                             m.bank[6 + tt // 4][:, (tt % 4) * C:(tt % 4 + 1) * C],
                                             m.share[:, tt, e:e + 1], m.moe[:, tt, :] if e else m.x[:, tt, :],
                                             ALU.mult, ALU.add).then_inc(m.s_weighed, 1)

            for e in range(EXPERTS):
                for f in range(FCH):
                    gated(e * FCH + f)
                    if f == 0 and e:
                        weigh(e - 1)
            weigh(EXPERTS - 1)
            dve.wait_ge(m.s_weighed, TT * EXPERTS)
            dve.tensor_scalar(m.x[:, :, :], m.moe[:, :, :], -LIMIT, LIMIT, ALU.max, ALU.min).then_inc(m.s_sum, 1)
            dve.wait_ge(m.s_sum, 1)

        @block.scalar
        def _(act):
            act.preload_act_table_set("natural_log_exp_and_others")
            act.wait_ge(m.s_norm_v, 2)
            act.activation(m.stat[:, 1, :], m.stat[:, 0, :], ACT.Ln, bias=m.eps[:, 0:1], scale=1.0 / C).then_inc(m.s_norm_a, 1)
            act.wait_ge(m.s_norm_a, 1)
            act.activation(m.stat[:, 2, :], m.stat[:, 1, :], ACT.Exp, scale=-0.5).then_inc(m.s_norm_a, 1)
            for i in range(2):
                act.wait_ge(m.s_turn_x, i + 1)
                act.mul(m.hT[:, i * HALF:(i + 1) * HALF], m.bank[i][:, :], m.ln2[:, 0:1]).then_inc(m.s_hT, 1)
            act.wait_ge(m.s_pick, 2)
            act.activation(m.pick[:, 1, :, :], m.pick[:, 0, :, :], ACT.Exp).then_inc(m.s_routed, 1)
            for i in range(EXPERTS * FCH):
                act.wait_ge(m.s_gate, i + 1)
                if i >= 2:
                    act.wait_ge(m.s_gated, i - 1)
                act.activation(m.silu[i % 2][:, :], m.gate_bank[:, :], ACT.Silu).then_inc(m.s_silu, 1)

        @block.tensor
        def _(pe):
            pe.wait_ge(m.s_norm_v, 3)
            for tt in range(TT):
                mm = pe.transpose(m.bank[tt // 4][:, (tt % 4) * P:(tt % 4 + 1) * P], m.square[:, tt, :], m.ident[:, :])
                if tt % 4 == 3:
                    mm.then_inc(m.s_turn_x, 1)
            pe.wait_ge(m.s_hT, 2)
            for tt in range(TT):
                mm = pe.matmul(m.bank[4][:, tt * EXPERTS:(tt + 1) * EXPERTS], m.hT[:, tt * P:(tt + 1) * P], m.wr[:, :],
                               start=True, stop=True)
            mm.then_inc(m.s_router, 1)

            def hidden(i):
                e, f = divmod(i, FCH)
                w = e % WRING
                cols = slice(f * P, (f + 1) * P)
                if e >= WRING and f == 0:
                    pe.wait_ge(m.s_expert[w], 3 * 16)
                if i >= 1:
                    pe.wait_ge(m.s_silu, i)
                for half in range(2):
                    t = slice(half * HALF, (half + 1) * HALF)
                    mm = pe.matmul(m.gate_bank[:, t], m.wg[:, w, cols], m.hT[:, t], start=True, stop=True)
                mm.then_inc(m.s_gate, 1)
                if i >= 1:
                    pe.wait_ge(m.s_gated, i)
                for half in range(2):
                    t = slice(half * HALF, (half + 1) * HALF)
                    mm = pe.matmul(m.up_bank[:, t], m.wu[:, w, cols], m.hT[:, t], start=True, stop=True)
                mm.then_inc(m.s_up, 1)

            def down(i):
                e, f = divmod(i, FCH)
                pe.wait_ge(m.s_gated, i + 1)
                if f == 0 and e:
                    pe.wait_ge(m.s_weighed, TT * e)
                for tt in range(TT):
                    mm = pe.matmul(m.bank[6 + tt // 4][:, (tt % 4) * C:(tt % 4 + 1) * C], m.act_in[i % 2][:, tt * P:(tt + 1) * P],
                                   m.wd[:, e % WRING, f, :], start=(f == 0 and tt % 4 == 0), stop=(f == FCH - 1),
                                   skip_group_check=True)
                mm.then_inc(m.s_down_unit, 1)

            for i in range(EXPERTS * FCH):
                hidden(i)
                if i:
                    down(i - 1)
            down(EXPERTS * FCH - 1)
    m.clear_semaphores()


def decoder_tensors(m):
    m.q_full = [m.sb(f"q_full{i}", [P, REP, T], F32R) for i in range(2)]
    m.q_shift = [m.sb(f"q_shift{i}", [KROWS, REP, T], F32R) for i in range(2)]
    m.k_twice = [m.sb(f"k_twice{i}", [P, T], F32R) for i in range(2)]
    m.k_rest = [m.sb(f"k_rest{i}", [KROWS, T], F32R) for i in range(2)]
    m.vones = [m.sb(f"vones{i}", [P, TT, 2 * HD]) for i in range(2)]
    m.raw = m.sb("raw", [P, RAW, REP + 1, HD])
    m.swapped = m.sb("swapped", [P, RAW, REP + 1, HD])
    m.rotated = m.sb("rotated", [P, TT, REP + 1, HD])
    m.probs = [m.sb(f"probs{i}", [P, 2, HALF]) for i in range(3)]
    m.mixed = m.sb("mixed", [P, NH // 2, T])
    m.silu = [m.mixed[:, i, :] for i in range(2)]
    m.act_in = [m.mixed[:, 2 + i, :] for i in range(2)]
    m.moe = m.mixed[:, 4, :].rearrange("p (t c) -> p t c", c=C)
    m.recip = [m.sb(f"recip{i}", [HD, HALF]) for i in range(2)]
    m.maxima = [m.sb(f"maxima{i}", [P, REP, TT]) for i in range(2)]
    m.maxima2 = [m.sb(f"maxima2{i}", [P, REP, TT]) for i in range(2)]
    m.maxrow = [m.sb(f"maxrow{i}", [REP * TT, P], F32R) for i in range(2)]
    m.hT = m.sb("hT", [C, T])
    m.stat = m.sb("stat", [P, 3, TT])
    m.ln1, m.ln2 = m.sb("ln1", [C, 1]), m.sb("ln2", [C, 1])
    m.wqkv = m.sb("wqkv", [C, NKV, GW])
    m.wo = m.sb("wo", [P, NH // 2, C])
    m.wr = m.sb("wr", [C, EXPERTS])
    m.wg, m.wu = m.sb("wg", [C, WRING, FF]), m.sb("wu", [C, WRING, FF])
    m.wd = m.sb("wd", [P, WRING, FCH, C])
    m.expert_no = m.sb("expert_no", [P, TT, EXPERTS])
    m.rank = m.sb("rank", [P, TT, EXPERTS])
    m.share = m.sb("share", [P, TT, EXPERTS])
    m.pick = m.sb("pick", [P, 5, TT, EXPERTS])
    m.top = m.sb("top", [P, 7, TT])



def branch_tensors(m):
    m.same_head = m.sb("same_head", [P, P])
    m.stacker = m.sb("stacker", [P, 4, P])
    m.head_mask = m.sb("head_mask", [P, 4])
    m.w_turned = m.sb("w_turned", [C, 4, C])
    m.b_col = m.sb("b_col", [P, 2])
    m.b_row = m.sb("b_row", [P, 2, C])
    m.temp_col, m.temp_row = m.sb("temp_col", [P, 1]), m.sb("temp_row", [P, AH])
    m.scale_work = m.sb("scale_work", [P, 4, 1 + AH])
    m.scale = m.sb("scale", [P, 1 + AH])
    m.shift = m.sb("shift", [P, AH])
    m.xT = m.sb("xT", [C, T])
    m.seqT = m.sb("seqT", [P, T])
    m.qk = [m.sb(f"qk{i}", [P, T]) for i in range(2)]
    m.qk_square = [m.sb(f"qk_square{i}", [P, T]) for i in range(2)]
    m.qk_norm = [m.sb(f"qk_norm{i}", [P, T]) for i in range(2)]
    m.q_stack = [m.sb(f"q_stack{i}", [P, T], F32R) for i in range(4)]
    m.key_stack = [m.sb(f"key_stack{i}", [P, T], F32R) for i in range(4)]


def recurrence_tensors(m):
    m.w_wide = m.sb("w_wide", [C, 4, STATES])
    m.b_wide = m.sb("b_wide", [P, 4, STATE_TILES])
    m.sum_rows = m.sb("sum_rows", [P, STATE_TILES, P])
    m.key_wide = [m.sb(f"key_wide{i}", [P, HALF]) for i in range(2)]
    m.decay = [m.sb(f"decay{i}", [P, HALF]) for i in range(2)]
    m.outer = [m.sb(f"outer{i}", [P, HALF]) for i in range(2)]
    m.read = [m.sb(f"read{i}", [P, HALF]) for i in range(2)]
    m.state = m.sb("state", [P, STATE_TILES, 2, HALF])


def attention_tensors(m):
    m.key_head = [m.sb(f"key_head{i}", [P, T], F32R) for i in range(AH // 2)]
    m.weights = [m.sb(f"weights{i}", [P, 2, HALF]) for i in range(4)]
    m.recip_a = [m.sb(f"recip_a{i}", [32, HALF]) for i in range(2)]
    m.mixedT = m.sb("mixedT", [P, T])
    m.v_wide = m.sb("v_wide", [P, TT, AH, 64])


def recurrence_block(nc, m, d):
    kinds = 4

    with nc.Block() as block:
        @block.sync
        def _(sp):
            sp.dma_start(m.w_wide[:, :, :], d["w_wide"].rearrange("k c n -> c k n")).then_inc(m.s_load, 16)
            sp.dma_start(m.b_wide[:, :, :], d["b_wide"].rearrange("k p j -> p k j")).then_inc(m.s_load, 16)
            sp.dma_start(m.sum_rows[:, :, :], d["sum_rows"].rearrange("j p n -> p j n")).then_inc(m.s_load, 16)
            sp.dma_start(m.same_head[:, :], d["same_head"]).then_inc(m.s_load_wo, 16)
            sp.dma_start(m.stacker[:, :, :], d["stacker"].rearrange("g p n -> p g n")).then_inc(m.s_load_wo, 16)
            sp.dma_start(m.head_mask[:, :], d["head_mask"]).then_inc(m.s_load_wo, 16)
            sp.dma_start(m.w_turned[:, :, :], d["w_turned"].rearrange("k c n -> c k n")).then_inc(m.s_load_wo, 16)
            sp.dma_start(m.b_col[:, :], d["b_col"]).then_inc(m.s_load_wo, 16)
            sp.dma_start(m.b_row[:, :, :], d["b_row"].unsqueeze(0).broadcast_to([P, 2, C])).then_inc(m.s_load_wo, 16)
            sp.dma_start(m.scale_work[:, 0, 0:1], d["temp_col"]).then_inc(m.s_load_moe, 16)
            sp.dma_start(m.scale_work[:, 0, 1:1 + AH], d["temp_row"].unsqueeze(0).broadcast_to([P, AH])).then_inc(m.s_load_moe, 16)
            sp.wait_ge(m.s_load_wo, 6 * 16)

        @block.tensor
        def _(pe):
            for tt in range(TT):
                mm = pe.transpose(m.bank[tt // 4][:, (tt % 4) * P:(tt % 4 + 1) * P], m.x[:, tt, :], m.ident[:, :])
                if tt % 4 == 3:
                    mm.then_inc(m.s_turn_x, 1)
            pe.wait_ge(m.s_load, 3 * 16)
            pe.wait_ge(m.s_hT, 2)

            def project(n):
                i, kind = divmod(n, kinds)
                half, j = divmod(i, STATE_TILES)
                if n >= 6:
                    sem = (m.s_key_wide, m.s_decay, m.s_outer, m.s_read)[(n - 6) % kinds]
                    pe.wait_ge(sem, (n - 6) // kinds + 1)
                pe.matmul(m.bank[n % 6][:, :], m.w_wide[:, kind, j * P:(j + 1) * P], m.xT[:, half * HALF:(half + 1) * HALF],
                          start=True, stop=True).then_inc(m.s_unit, 1)

            def gather(i):
                half, j = divmod(i, STATE_TILES)
                pe.wait_ge(m.s_read, i + 1)
                pe.matmul(m.bank[6 + half][:, :], m.sum_rows[:, j, :], m.read[i % 2][:, :],
                          start=(j == 0), stop=(j == STATE_TILES - 1)).then_inc(m.s_gathered, 1)

            for i in range(2 * STATE_TILES):
                for kind in range(kinds):
                    project(i * kinds + kind)
                if i:
                    gather(i - 1)
            gather(2 * STATE_TILES - 1)

        @block.scalar
        def _(act):
            for i in range(2):
                act.wait_ge(m.s_turn_x, i + 1)
                act.copy(m.xT[:, i * HALF:(i + 1) * HALF], m.bank[i][:, :]).then_inc(m.s_hT, 1)
            act.wait_ge(m.s_norm_v, 1)
            for i in range(2 * STATE_TILES):
                j = i % STATE_TILES
                act.wait_ge(m.s_unit, kinds * i + 1)
                if i >= 2:
                    act.wait_ge(m.s_outer, i - 1)
                act.activation(m.key_wide[i % 2][:, :], m.bank[(kinds * i) % 6][:, :], ACT.Identity,
                               bias=m.b_wide[:, 0, j:j + 1]).then_inc(m.s_key_wide, 1)
                act.wait_ge(m.s_unit, kinds * i + 2)
                if i >= 2:
                    act.wait_ge(m.s_state, i - 1)
                act.activation(m.decay[i % 2][:, :], m.bank[(kinds * i + 1) % 6][:, :], ACT.Sigmoid,
                               bias=m.b_wide[:, 1, j:j + 1], scale=-1.0).then_inc(m.s_decay, 1)
            for half in range(2):
                act.wait_ge(m.s_gathered, (half + 1) * STATE_TILES)
                act.copy(m.seqT[:, half * HALF:(half + 1) * HALF], m.bank[6 + half][:, :]).then_inc(m.s_hT, 1)
            act.wait_ge(m.s_scale, 2)
            act.activation(m.scale_work[:, 2, :], m.scale_work[:, 1, :], ACT.Exp, scale=-1.0).then_inc(m.s_norm_a, 1)
            act.wait_ge(m.s_norm_a, 1)
            act.activation(m.scale_work[:, 3, :], m.scale_work[:, 2, :], ACT.Ln, bias=1.0).then_inc(m.s_norm_a, 1)

        @block.vector
        def _(dve):
            dve.wait_ge(m.s_load, 3 * 16)
            dve.tensor_scalar(m.b_wide[:, 1, :], m.b_wide[:, 1, :], -1.0, None, ALU.mult).then_inc(m.s_norm_v, 1)
            dve.wait_ge(m.s_load_moe, 2 * 16)
            dve.tensor_scalar(m.scale_work[:, 1, :], m.scale_work[:, 0, :], -1.0, None, ALU.mult).then_inc(m.s_scale, 1)
            dve.wait_ge(m.s_scale, 1)
            dve.tensor_tensor(m.scale_work[:, 1, :], m.scale_work[:, 1, :], m.scale_work[:, 0, :], ALU.max).then_inc(m.s_scale, 1)

            def read_out(i):
                j = i % STATE_TILES
                dve.wait_ge(m.s_unit, kinds * i + 4)
                if i >= 2:
                    dve.wait_ge(m.s_gathered, i - 1)
                dve.scalar_tensor_tensor(m.read[i % 2][:, :], m.bank[(kinds * i + 3) % 6][:, :], m.b_wide[:, 3, j:j + 1],
                                         m.state[:, j, i // STATE_TILES, :], ALU.add, ALU.mult).then_inc(m.s_read, 1)

            for i in range(2 * STATE_TILES):
                half, j = divmod(i, STATE_TILES)
                dve.wait_ge(m.s_unit, kinds * i + 3)
                dve.wait_ge(m.s_key_wide, i + 1)
                if i >= 2:
                    dve.wait_ge(m.s_state, i - 1)
                dve.scalar_tensor_tensor(m.outer[i % 2][:, :], m.bank[(kinds * i + 2) % 6][:, :], m.b_wide[:, 2, j:j + 1],
                                         m.key_wide[i % 2][:, :], ALU.add, ALU.mult).then_inc(m.s_outer, 1)
                dve.wait_ge(m.s_decay, i + 1)
                dve.wait_ge(m.s_outer, i + 1)
                dve.tensor_tensor_scan(m.state[:, j, half, :], m.decay[i % 2][:, :], m.outer[i % 2][:, :],
                                       m.state[:, j, 0, HALF - 1:HALF] if half else 0.0,
                                       ALU.mult, ALU.add).then_inc(m.s_state, 1)
                dve.wait_ge(m.s_state, i + 1)
                read_out(i)
            dve.wait_ge(m.s_norm_a, 2)
            dve.scalar_tensor_tensor(m.scale[:, :], m.scale_work[:, 0, :], 0.0, m.scale_work[:, 3, :], ALU.max,
                                     ALU.add).then_inc(m.s_scale, 1)
            dve.wait_ge(m.s_scale, 3)
            dve.tensor_scalar(m.shift[:, :], m.scale[:, 1:1 + AH], -TALL, 0.0, ALU.add, ALU.max).then_inc(m.s_scale, 1)
            dve.wait_ge(m.s_scale, 4)
            dve.tensor_scalar(m.shift[:, :], m.shift[:, :], -1.0, None, ALU.mult).then_inc(m.s_scale, 1)
            dve.wait_ge(m.s_scale, 5)
    m.clear_semaphores()


def heads_block(nc, m):
    q, k = 0, 1
    with nc.Block() as block:
        @block.tensor
        def _(pe):
            for i in (q, k):
                for half in range(2):
                    t = slice(half * HALF, (half + 1) * HALF)
                    mm = pe.matmul(m.pair_bank[i][:, t], m.w_turned[:, i, :], m.seqT[:, t], start=True, stop=True)
                mm.then_inc(m.s_unit, 1)
            for tt in range(TT):
                mm = pe.matmul(m.pair_bank[2][:, tt * C:(tt + 1) * C], m.xT[:, tt * P:(tt + 1) * P], m.w_turned[:, 2, :],
                               start=True, stop=True)
            mm.then_inc(m.s_unit, 1)
            for i in (q, k):
                pe.wait_ge(m.s_square, i + 1)
                if i == k:
                    pe.wait_ge(m.s_value, 5)
                for half in range(2):
                    t = slice(half * HALF, (half + 1) * HALF)
                    mm = pe.matmul(m.pair_bank[3 - i][:, t], m.same_head[:, :], m.qk_square[i][:, t], start=True, stop=True)
                mm.then_inc(m.s_sumsq, 1)
            for n in range(8):
                i, g = divmod(n, 4)
                pe.wait_ge(m.s_unit_length, i + 1)
                if n >= 2:
                    pe.wait_ge(m.s_low, n - 1)
                for half in range(2):
                    t = slice(half * HALF, (half + 1) * HALF)
                    mm = pe.matmul(m.pair_bank[n % 2][:, t], m.stacker[:, g, :], m.qk[i][:, t], start=True, stop=True)
                mm.then_inc(m.s_stacked, 1)

        @block.scalar
        def _(act):
            for i in (q, k):
                act.wait_ge(m.s_unit, i + 1)
                act.activation(m.qk[i][:, :], m.pair_bank[i][:, :], ACT.Identity, bias=m.b_col[:, i:i + 1]).then_inc(m.s_qk, 1)
            for i in (q, k):
                act.wait_ge(m.s_sumsq, i + 1)
                act.activation(m.qk_norm[i][:, :], m.pair_bank[3 - i][:, :], ACT.Sqrt).then_inc(m.s_norm_a, 1)
            for n in range(8):
                act.wait_ge(m.s_stacked, n + 1)
                to = (m.q_stack if n < 4 else m.key_stack)[n % 4]
                act.copy(to[:, :], m.pair_bank[n % 2][:, :]).then_inc(m.s_high, 1)

        @block.vector
        def _(dve):
            dve.memset(m.v_wide[:, :, :, :], 0.0).then_inc(m.s_value, 1)
            dve.wait_ge(m.s_value, 1)
            v_wide = m.v_wide[:, :, :, :].rearrange("p t (g j) e -> p t g j e", j=4)
            dve.wait_ge(m.s_unit, 3)
            for j in range(4):
                cols = m.pair_bank[2][:, :].rearrange("p (t g n) -> p t g n", t=TT, g=4)[:, :, :, 8 * j:8 * j + 8]
                bias = m.b_row[:, 0, :].rearrange("p (g n) -> p g n", g=4)[:, :, 8 * j:8 * j + 8]
                dve.tensor_tensor(v_wide[:, :, :, j, 8 * j:8 * j + 8], cols,
                                  bias.unsqueeze(1).broadcast_to([P, TT, 4, 8]), ALU.add).then_inc(m.s_value, 1)
            for j in range(4):
                dve.memset(v_wide[:, :, :, j, 32 + 8 * j:40 + 8 * j], 1.0).then_inc(m.s_ones, 1)
            for i in (q, k):
                dve.wait_ge(m.s_qk, i + 1)
                dve.tensor_tensor(m.qk_square[i][:, :], m.qk[i][:, :], m.qk[i][:, :], ALU.mult).then_inc(m.s_square, 1)
            for i in (q, k):
                dve.wait_ge(m.s_norm_a, i + 1)
                dve.tensor_scalar(m.qk_norm[i][:, :], m.qk_norm[i][:, :], 1e-12, None, ALU.max).then_inc(m.s_norm_v, 1)
                dve.wait_ge(m.s_norm_v, 2 * i + 1)
                dve.reciprocal(m.qk_square[i][:, :], m.qk_norm[i][:, :]).then_inc(m.s_norm_v, 1)
                dve.wait_ge(m.s_norm_v, 2 * i + 2)
                if i == q:
                    dve.scalar_tensor_tensor(m.qk[i][:, :], m.qk[i][:, :], m.scale[:, 0:1], m.qk_square[i][:, :],
                                             ALU.mult, ALU.mult).then_inc(m.s_unit_length, 1)
                else:
                    dve.tensor_tensor(m.qk[i][:, :], m.qk[i][:, :], m.qk_square[i][:, :], ALU.mult).then_inc(m.s_unit_length, 1)
            for n in range(8):
                dve.wait_ge(m.s_high, n + 1)
                to = (m.q_stack if n < 4 else m.key_stack)[n % 4]
                parts = ((32, 64), (96, 128)) if n < 4 else ((64, 128),)
                for x, (a, b) in enumerate(parts):
                    dve.tensor_tensor(to[a:b, :], m.pair_bank[n % 2][a:b, :], to[a:b, :].bitcast(F32), ALU.subtract)\
                       .then_inc(m.s_low if x == len(parts) - 1 else m.s_low0, 1)
            dve.wait_ge(m.s_low, 8)
            dve.wait_ge(m.s_ones, 4)
    m.clear_semaphores()


def full_attention_steps():
    return [(gp, qc, j, 2 * kp, side) for gp in range(2) for qc in range(2) for j in range(4)
            for kp in range(TT // 2) for side in range(2)]


def full_attention_block(nc, m):
    steps = full_attention_steps()
    per_chunk = len(steps) // 4
    s_tile = m.pair_bank[0:3]
    heads_per_pair = AH // 2
    with nc.Block() as block:
        @block.vector
        def _(dve):
            def key_heads(gp):
                for j in range(4):
                    for side in range(2):
                        n = j * 2 + side
                        if gp:
                            dve.wait_ge(m.s_scores, per_chunk + (j + 1) * TT - 1 + side)
                        dve.tensor_scalar(m.key_head[n][:, :], m.key_stack[2 * gp + side][:, :].bitcast(F32),
                                          m.head_mask[:, j:j + 1], None, ALU.mult).then_inc(m.s_key_head, 1)

            def store(ch):
                gp, qc = divmod(ch, 2)
                o = m.bank[6 + ch % 2]
                dve.wait_ge(m.s_pv, (ch + 1) * per_chunk // 2)
                for side in range(2):
                    n = 2 * ch + side
                    if ch:
                        dve.wait_ge(m.s_stored, n - 1)
                    dve.reciprocal(m.recip_a[side][:, :], o[64 * side + 32:64 * side + 64, :]).then_inc(m.s_recip, 1)
                    dve.wait_ge(m.s_recip, n + 1)
                    g = 2 * gp + side
                    dve.tensor_tensor(m.mixedT[32 * g:32 * g + 32, qc * HALF:(qc + 1) * HALF], o[64 * side:64 * side + 32, :],
                                      m.recip_a[side][:, :], ALU.mult).then_inc(m.s_stored, 1)

            dve.tensor_tensor(m.total[:, :, :], m.total[:, :, :], m.b_row[:, 1, :].unsqueeze(1).broadcast_to([P, TT, C]),
                              ALU.add).then_inc(m.s_sum, 1)
            key_heads(0)
            store(0)
            key_heads(1)
            store(1)
            store(2)
            store(3)
            dve.wait_ge(m.s_sum, 1)
            dve.wait_ge(m.s_wo, 1)
            dve.tensor_tensor(m.total[:, :, :], m.pair_bank[0][:, :].rearrange("p (t c) -> p t c", c=C), m.total[:, :, :],
                              ALU.add).then_inc(m.s_sum, 1)
            dve.wait_ge(m.s_sum, 2)

        @block.scalar
        def _(act):
            for s, (gp, qc, j, kb, side) in enumerate(steps):
                head = 4 * (2 * gp + side) + j
                act.wait_ge(m.s_scores, s + 1)
                if s >= 4:
                    act.wait_ge(m.s_pv, (s - 4) // 2 + 1)
                act.activation(m.weights[s % 4][:, :, :], s_tile[s % 3][:, :].rearrange("p (k q) -> p k q", k=2),
                               ACT.Exp, bias=m.shift[:, head:head + 1]).then_inc(m.s_probs, 1)

        @block.tensor
        def _(pe):
            def score(s):
                gp, qc, j, kb, side = steps[s]
                n = j * 2 + side
                if kb == 0 and qc == 0:
                    pe.wait_ge(m.s_key_head, gp * heads_per_pair + n + 1)
                if s >= 3:
                    pe.wait_ge(m.s_probs, s - 2)
                for i in range(2):
                    mm = pe.matmul(s_tile[s % 3][:, i * HALF:(i + 1) * HALF], m.key_head[n][:, (kb + i) * P:(kb + i + 1) * P],
                                   m.q_stack[2 * gp + side][:, qc * HALF:(qc + 1) * HALF], start=True, stop=True)
                mm.then_inc(m.s_scores, 1)

            def mix(pair):
                gp, qc, j, kb, _ = steps[2 * pair]
                ch = 2 * gp + qc
                pe.wait_ge(m.s_probs, 2 * pair + 2)
                if j == 0 and kb == 0 and ch >= 2:
                    pe.wait_ge(m.s_stored, 2 * (ch - 1))
                for i in range(2):
                    for side in range(2):
                        head = 4 * (2 * gp + side) + j
                        mm = pe.matmul(m.bank[6 + ch % 2][64 * side:64 * side + 64, :], m.v_wide[:, kb + i, head, :],
                                       m.weights[(2 * pair + side) % 4][:, i, :],
                                       start=(j == 0 and kb + i == 0), stop=(j == 3 and kb + i == TT - 1))
                mm.then_inc(m.s_pv, 1)

            for pair in range(len(steps) // 2):
                score(2 * pair)
                score(2 * pair + 1)
                if pair:
                    mix(pair - 1)
            mix(len(steps) // 2 - 1)
            pe.wait_ge(m.s_stored, 8)
            pe.wait_ge(m.s_probs, len(steps))
            for tt in range(TT):
                mm = pe.matmul(m.pair_bank[0][:, tt * C:(tt + 1) * C], m.mixedT[:, tt * P:(tt + 1) * P], m.w_turned[:, 3, :],
                               start=True, stop=True)
            mm.then_inc(m.s_wo, 1)
    m.clear_semaphores()


def semaphores(m):
    m.s_load = m.sem("load")
    m.s_key_wide = m.sem("key_wide")
    m.s_decay = m.sem("decay")
    m.s_outer = m.sem("outer")
    m.s_read = m.sem("read")
    m.s_gathered = m.sem("gathered")
    m.s_state = m.sem("state")
    m.s_scale = m.sem("scale")
    m.s_square = m.sem("square")
    m.s_qk = m.sem("qk")
    m.s_sumsq = m.sem("sumsq")
    m.s_unit_length = m.sem("unit_length")
    m.s_stacked = m.sem("stacked")
    m.s_key_head = m.sem("key_head")
    m.s_load_wo = m.sem("load_wo")
    m.s_load_moe = m.sem("load_moe")
    m.s_set = m.sem("set")
    m.s_ones = m.sem("ones")
    m.s_norm_v = m.sem("norm_v")
    m.s_norm_a = m.sem("norm_a")
    m.s_turn_x = m.sem("turn_x")
    m.s_hT = m.sem("hT")
    m.s_maxrow = m.sem("maxrow")
    m.s_pv = m.sem("pv")
    m.s_raw = m.sem("raw")
    m.s_cos = m.sem("cos")
    m.s_sin0 = m.sem("sin0")
    m.s_sin = m.sem("sin")
    m.s_rotated = m.sem("rotated")
    m.s_high = m.sem("high")
    m.s_high0 = m.sem("high0")
    m.s_low0 = m.sem("low0")
    m.s_low = m.sem("low")
    m.s_value = m.sem("value")
    m.s_max = m.sem("max")
    m.s_rowmax = m.sem("rowmax")
    m.s_unit = m.sem("unit")
    m.s_probs = m.sem("probs")
    m.s_scores = m.sem("scores")
    m.s_masked = m.sem("masked")
    m.s_recip = m.sem("recip")
    m.s_logden = m.sem("logden")
    m.s_stored = m.sem("stored")
    m.s_wo = m.sem("wo")
    m.s_sum = m.sem("sum")
    m.s_router = m.sem("router")
    m.s_routed = m.sem("routed")
    m.s_pick = m.sem("pick")
    m.s_silu = m.sem("silu")
    m.s_gate = m.sem("gate")
    m.s_up = m.sem("up")
    m.s_gated = m.sem("gated")
    m.s_down_unit = m.sem("down_unit")
    m.s_weighed = m.sem("weighed")
    m.s_shift = [m.sem(f"shift{i}") for i in range(2)]
    m.s_scratch = [m.sem(f"scratch{i}") for i in range(2)]
    m.s_expert = [m.sem(f"expert{i}") for i in range(WRING)]


def input_block(nc, m, d, b):
    with nc.Block() as block:
        @block.sync
        def _(sp):
            sp.dma_start(m.total[:, :, :], d["x"][b].rearrange("(t p) c -> p t c", p=P)).then_inc(m.s_load, 16)
            sp.wait_ge(m.s_load, 16)

        @block.vector
        def _(dve):
            dve.wait_ge(m.s_load, 16)
            for tt in range(TT):
                dve.bn_stats(m.bn[:, tt, :], m.total[:, tt, :]).then_inc(m.s_norm_v, 1)
            dve.wait_ge(m.s_norm_v, TT)
            for tt in range(TT):
                dve.bn_aggr(m.moments[:, tt, 0:2], m.bn[:, tt, :]).then_inc(m.s_norm_v, 1)
            dve.wait_ge(m.s_norm_v, 2 * TT)
            dve.tensor_tensor(m.square[:, :, :], m.total[:, :, :], m.moments[:, :, 0:1].broadcast_to([P, TT, C]),
                              ALU.subtract).then_inc(m.s_norm_v, 1)
            dve.wait_ge(m.s_norm_a, 2)
            dve.wait_ge(m.s_norm_v, 2 * TT + 1)
            dve.tensor_tensor(m.x[:, :, :], m.square[:, :, :], m.moments[:, :, 2:3].broadcast_to([P, TT, C]),
                              ALU.mult).then_inc(m.s_norm_v, 1)
            dve.wait_ge(m.s_norm_v, 2 * TT + 2)

        @block.scalar
        def _(act):
            act.wait_ge(m.s_norm_v, 2 * TT)
            act.activation(m.moments[:, :, 3:4], m.moments[:, :, 1:2], ACT.Ln, bias=m.eps[:, 0:1]).then_inc(m.s_norm_a, 1)
            act.wait_ge(m.s_norm_a, 1)
            act.activation(m.moments[:, :, 2:3], m.moments[:, :, 3:4], ACT.Exp, scale=-0.5).then_inc(m.s_norm_a, 1)
            act.wait_ge(m.s_norm_a, 2)
    m.clear_semaphores()


def output_block(nc, m, out, b):
    with nc.Block() as block:
        @block.vector
        def _(dve):
            dve.tensor_tensor(m.total[:, :, :], m.total[:, :, :], m.x[:, :, :], ALU.add).then_inc(m.s_sum, 1)

        @block.sync
        def _(sp):
            sp.wait_ge(m.s_sum, 1)
            sp.dma_start(out[b].rearrange("(t p) c -> p t c", p=P), m.total[:, :, :]).then_inc(m.s_load, 16)
            sp.wait_ge(m.s_load, 16)
    m.clear_semaphores()


def build_program(nc, d, out):
    with ExitStack() as ctx:
        m = Core(nc, ctx)
        semaphores(m)
        m.scratch = [nc.dram_tensor(f"maxima_turned{i}", (REP * TT, P), F32, kind="Internal").ap() for i in range(2)]
        banks = m.psum("banks", [P, 8, HALF])
        m.bank = [banks[:, i, :] for i in range(8)]
        m.pair_bank = [banks[:, 2 * i:2 * i + 2, :].rearrange("p k n -> p (k n)") for i in range(4)]
        m.gate_bank, m.up_bank = m.pair_bank[0:2]
        m.ident, m.ident16 = m.sb("ident", [P, P]), m.sb("ident16", [P, P], BF16)
        m.later, m.later16 = m.sb("later", [P, P]), m.sb("later16", [P, P], BF16)
        m.cos, m.sin = m.sb("cos", [P, TT, HD]), m.sb("sin", [P, TT, HD])
        m.eps = m.sb("eps", [P, 1])
        m.total, m.x, m.square = (m.sb(n, [P, TT, C]) for n in ("total", "x", "square"))
        m.bn, m.moments = m.sb("bn", [P, TT, 6]), m.sb("moments", [P, TT, 4])
        first_constants(nc, m, d)
        with nc.Fori(0, BATCH) as b:
            input_block(nc, m, d, b)
            with ExitStack() as inner:
                m.ctx = inner
                branch_tensors(m)
                with ExitStack() as m.ctx:
                    recurrence_tensors(m)
                    recurrence_block(nc, m, d)
                m.ctx = inner
                attention_tensors(m)
                heads_block(nc, m)
                full_attention_block(nc, m)
            with ExitStack() as inner:
                m.ctx = inner
                decoder_tensors(m)
                decoder_constants(nc, m)
                with nc.Fori(0, LAYERS) as layer:
                    attention_block(nc, m, d, layer)
                    moe_block(nc, m, d, layer)
            output_block(nc, m, out, b)


def rotary_tables():
    inverse = (np.float32(1.0) / (np.float32(10000.0) ** (np.arange(0, HD, 2, dtype=np.float32) / np.float32(HD)))).astype(np.float32)
    angles = np.arange(T, dtype=np.float32)[:, None] * inverse
    cos, sin = np.cos(angles), np.sin(angles)
    return np.concatenate([cos, cos], axis=1), np.concatenate([-sin, sin], axis=1)


def branch_constants():
    row = np.arange(P)
    state = np.arange(STATES)
    column = state // (AD * AD) * AD + state % AD
    sum_rows = (column[:, None] == row).astype(np.float32).reshape(STATE_TILES, P, P)
    same_head = (row[:, None] // AD == row // AD).astype(np.float32)
    stacker = np.stack([(row[:, None] == 32 * g + row % 32).astype(np.float32) for g in range(4)])
    head_mask = (row[:, None] % 32 // AD == np.arange(4)).astype(np.float32)
    return {"sum_rows": sum_rows, "same_head": same_head, "stacker": stacker, "head_mask": head_mask}


def laid_out(given):
    state = np.arange(STATES)
    head, d, e = state // (AD * AD), state // AD % AD, state % AD
    rows = [("Wsk", "bsk", head * AD + d), ("Wg", "bg", head), ("Wsv", "bsv", head * AD + e), ("Wsq", "bsq", head * AD + d)]
    return {
        "w_wide": np.stack([np.ascontiguousarray(given[w][i].T) for w, _, i in rows]),
        "b_wide": np.stack([np.ascontiguousarray(given[b][i].reshape(STATE_TILES, P).T) for _, b, i in rows]),
        "w_turned": np.stack([np.ascontiguousarray(given[w].T) for w in ("Wq", "Wk", "Wv", "Wo")]),
        "b_col": np.stack([given["bq"], given["bk"]], axis=1),
        "b_row": np.stack([given["bv"], given["bo"]]),
        "temp_row": given["temp"].reshape(AH),
        "temp_col": np.repeat(given["temp"].reshape(AH), AD).reshape(P, 1),
    }


DECODER = ("ln1_w", "ln2_w", "wq", "wk", "wv", "wo", "wr", "wg", "wu", "wd")


def arrays_of(inputs):
    given = {name: np.ascontiguousarray(inputs[full]) for name, full in _INS.items()}
    cos, sin = rotary_tables()
    return {"x": given["x"], "cos": cos, "sin": sin, **{n: given[n] for n in DECODER}, **branch_constants(), **laid_out(given)}


_INS = {
    "x": "L0_attn_x", "Wsq": "L0_attn_Wsq", "bsq": "L0_attn_bsq", "Wsk": "L0_attn_Wsk", "bsk": "L0_attn_bsk",
    "Wsv": "L0_attn_Wsv", "bsv": "L0_attn_bsv", "Wg": "L0_attn_Wg", "bg": "L0_attn_bg", "Wq": "L0_attn_Wq",
    "bq": "L0_attn_bq", "Wk": "L0_attn_Wk", "bk": "L0_attn_bk", "Wv": "L0_attn_Wv", "bv": "L0_attn_bv",
    "Wo": "L0_attn_Wo", "bo": "L0_attn_bo", "temp": "L0_attn_temp", "ln1_w": "L0_ffn_ln1_w",
    "ln2_w": "L0_ffn_ln2_w", "wq": "L0_ffn_wq", "wk": "L0_ffn_wk", "wv": "L0_ffn_wv", "wo": "L0_ffn_wo",
    "wr": "L0_ffn_wr", "wg": "L0_ffn_wg", "wu": "L0_ffn_wu", "wd": "L0_ffn_wd",
}


def kernel(**inputs):
    import numpy as _np
    import concourse.bacc as _bacc
    from concourse import mybir as _mybir
    from concourse.bass_utils import run_bass_kernel_spmd as _run

    nc = _bacc.Bacc("TRN2", target_bir_lowering=False, num_devices=1)
    arrays, dram = {}, {}
    for name, a in arrays_of(inputs).items():
        a = _np.ascontiguousarray(a)
        arrays[f"in_{name}_dram"] = a
        dram[name] = nc.dram_tensor(f"in_{name}_dram", a.shape, _mybir.dt.from_np(a.dtype), kind="ExternalInput").ap()
    out = nc.dram_tensor("out_0_dram", (BATCH, T, C), _mybir.dt.float32, kind="ExternalOutput").ap()
    build_program(nc, dram, out)
    r = _run(nc, [arrays], core_ids=[0])
    return r.results[0]["out_0_dram"]
```

```python
import math
from contextlib import ExitStack

import numpy as np

import concourse.bass as bass
import concourse.mybir as mybir

F32 = mybir.dt.float32
F32R = mybir.dt.float32r
BF16 = mybir.dt.bfloat16
ALU = mybir.AluOpType
ACT = mybir.ActivationFunctionType
AX = mybir.AxisListType

P = 128
BATCH, T, C = 2, 1024, 128
TT = T // P
HALF = 512
LAYERS = 4
NH, NKV, HD = 16, 4, 64
REP = NH // NKV
GW = REP * HD + 2 * HD
ROT = REP * HD + HD
FF, EXPERTS = 256, 8
FCH = FF // P
EPS = 1e-5
RAW = 4
WRING = 4
AH, AD = 16, 8
STATES = AH * AD * AD
STATE_TILES = STATES // P
TALL = 80.0
LIMIT = 100.0
FAR = -1e9
MROW = 64
KROWS = 96



GROUPS = BATCH * NKV


def attention_steps():
    return [(g, pair, qc, kt) for g in range(GROUPS) for pair in range(REP // 2) for qc in range(2)
            for kt in range(4 * (qc + 1))]


STEPS = attention_steps()
STEPS_PER_GROUP = len(STEPS) // GROUPS
CHUNK_END = [s for s, (_, _, qc, kt) in enumerate(STEPS) if kt == 4 * qc + 3]
CHUNKS = len(CHUNK_END)
BATCH_CHUNKS = CHUNKS // BATCH
MIX_LAG = 2
ADD_LAG = 2
DEN_LAG = ADD_LAG + 1
LAST_STEPS = 4
OUTPUT_STEP = len(STEPS) // BATCH + DEN_LAG
PROBS = 4
ALL_STEPS = len(STEPS) + DEN_LAG + 1


def is_diagonal(s):
    _, _, qc, kt = STEPS[s]
    return kt >= 4 * qc


def first_query(s):
    _, _, qc, kt = STEPS[s]
    return max(0, kt - 4 * qc) * P


def first_score(s):
    return min(first_query(s), HALF // 2)


def masks_until(s):
    return sum(is_diagonal(k) for k in range(s + 1))


def adds_until(s):
    return sum(STEPS[k][3] > 0 for k in range(s + 1))


def chunk_of(s):
    return sum(e < s for e in CHUNK_END)


def preparation_units(g):
    def coarse(j, qbs):
        for qb in qbs:
            keys = (qb + 1) * P
            yield ("coarse", g, j, qb, 0, min(keys, HALF))
            if keys > HALF:
                yield ("coarse", g, j, qb, HALF, keys - HALF)

    units = [("project", g, tt) for tt in range(TT)]
    units.insert(TT - 1, ("turn", g, REP, 0))
    units.append(("turn", g, 0, 0))
    early, late = range(TT // 2), range(TT // 2, TT)
    c = [*coarse(0, early), *coarse(1, early), *coarse(0, late), *coarse(1, late)]
    for place, unit in ((3, ("turn", g, REP, 1)), (6, ("turn", g, 0, 1)), (15, ("turn", g, 2, 0)), (20, ("turn", g, 2, 1))):
        c.insert(place, unit)
    return units + c + [*coarse(2, range(TT)), *coarse(3, range(TT))]


PARTS = 3
UNIT_TIME = {"norm": 1.5, "project": 1.2, "turn": 3.4, "coarse": 0.8}


def schedule():
    first = preparation_units(0) + [("maxima", 0)]
    at = [[[] for _ in range(PARTS)] for _ in range(ALL_STEPS)]
    for g in range(1, GROUPS):
        units = preparation_units(g)
        if g == NKV:
            units = [("norm", g, half) for half in range(2)] + units
        start = (g - 1) * STEPS_PER_GROUP
        slots = [(s, part) for s in range(start + MIX_LAG, start + STEPS_PER_GROUP - LAST_STEPS) for part in range(PARTS)]
        spans = [2 * (HALF - first_query(s - MIX_LAG)) if part == 2 else HALF - first_score(s) for s, part in slots]
        scale = sum(UNIT_TIME[u[0]] for u in units) / sum(spans)
        have, want = 0.0, 0.0
        for (s, part), span in zip(slots, spans):
            want += span * scale
            while units and have + UNIT_TIME[units[0][0]] / 2 <= want:
                have += UNIT_TIME[units[0][0]]
                at[s][part].append(units.pop(0))
        at[slots[-1][0]][-1] += units
        at[start + STEPS_PER_GROUP - LAST_STEPS + 1][0].append(("maxima", g))
    for ch, s in enumerate(CHUNK_END):
        at[s + DEN_LAG][-1].append(("denominators", STEPS[s][0], ch))
    for half in range(2):
        at[OUTPUT_STEP + half][-1].append(("output", NKV - 1, half))
    return first, at


FIRST_UNITS, UNITS_AT = schedule()
UNITS = FIRST_UNITS + [u for parts in UNITS_AT for units in parts for u in units]
ALL_BANKS = (6, 7, 5, 2, 3, 4, 0, 1)
UNIT_BANKS = ALL_BANKS[0:3]


def units_at(s, part=None):
    start = len(FIRST_UNITS) + sum(len(units) for parts in UNITS_AT[:s] for units in parts)
    ends = [start]
    for units in UNITS_AT[s]:
        ends.append(ends[-1] + len(units))
    return range(ends[0], ends[-1]) if part is None else range(ends[part], ends[part + 1])


def bank_of(n):
    return ALL_BANKS[n % 8] if n < len(FIRST_UNITS) else UNIT_BANKS[n % 3]


def user_before(n):
    return next((k for k in range(n - 1, max(-1, n - 17), -1) if bank_of(k) == bank_of(n)), None)


def ordinal(kind, n):
    return sum(u[0] == kind for u in UNITS[:n + 1])


def turned(g, j, half):
    return ordinal("turn", UNITS.index(("turn", g, j if j == REP else j // 2 * 2, half)))


def highs(n):
    return sum(1 if u[2] == REP else 2 for u in UNITS[:n + 1] if u[0] == "turn")


def mixed_of(m, ch):
    g, pair, qc, _ = STEPS[CHUNK_END[ch]]
    return m.mixed[:, g % NKV * REP // 2 + pair, qc * HALF:(qc + 1) * HALF]


class Core:

    def __init__(self, nc, ctx):
        self.nc, self.ctx = nc, ctx
        self.sems = []

    def sb(self, name, shape, dt=F32):
        return self.ctx.enter_context(self.nc.sbuf_tensor(name, shape, dt))

    def psum(self, name, shape, dt=F32):
        return self.ctx.enter_context(self.nc.psum_tensor(name, shape, dt))

    def sem(self, name):
        s = self.ctx.enter_context(self.nc.semaphore(name))
        self.sems.append(s)
        return s

    def clear_semaphores(self):
        numbers = [s.num for s in self.sems]
        self.nc.sync.sem_clear(range(min(numbers), max(numbers) + 1))
        self.nc.all_engine_barrier()


def first_constants(nc, m, d):
    with nc.Block() as block:
        @block.sync
        def _(sp):
            sp.dma_start(m.cos[:, :, :], d["cos"].rearrange("(t p) f -> p t f", p=P)).then_inc(m.s_load, 16)
            sp.dma_start(m.sin[:, :, :], d["sin"].rearrange("(t p) f -> p t f", p=P)).then_inc(m.s_load, 16)
            sp.wait_ge(m.s_load, 32)

        @block.gpsimd
        def _(pool):
            pool.memset(m.ident[:, :], 0.0).then_inc(m.s_set, 1)
            pool.memset(m.later[:, :], 0.0).then_inc(m.s_set, 1)
            pool.wait_ge(m.s_set, 2)
            pool.affine_select(out=m.ident[:, :], in_=m.ident[:, :], compare_op=ALU.not_equal, fill=1.0, base=0,
                               pattern=[[-1, P]], channel_multiplier=1).then_inc(m.s_set, 1)
            pool.affine_select(out=m.later[:, :], in_=m.later[:, :], compare_op=ALU.is_ge, fill=FAR, base=0,
                               pattern=[[-1, P]], channel_multiplier=1).then_inc(m.s_set, 1)
            pool.wait_ge(m.s_set, 4)
            pool.tensor_copy(m.ident16[:, :], m.ident[:, :]).then_inc(m.s_set, 1)
            pool.tensor_copy(m.later16[:, :], m.later[:, :]).then_inc(m.s_set, 1)
            pool.wait_ge(m.s_set, 6)

        @block.vector
        def _(dve):
            dve.memset(m.eps[:, :], EPS).then_inc(m.s_ones, 1)
            dve.wait_ge(m.s_ones, 1)
    m.clear_semaphores()


def decoder_constants(nc, m):
    with nc.Block() as block:
        @block.vector
        def _(dve):
            dve.memset(m.ones[:, :], 1.0).then_inc(m.s_ones, 1)
            for q in m.q_shift:
                dve.memset(q[MROW:KROWS, :, :].bitcast(F32), 0.0).then_inc(m.s_ones, 1)
            for k in m.k_rest:
                dve.memset(k[MROW:KROWS, :].bitcast(F32), 0.0).then_inc(m.s_ones, 1)
            dve.wait_ge(m.s_ones, 5)
            for k in m.k_rest:
                dve.memset(k[MROW:MROW + 1, :].bitcast(F32), 1.0).then_inc(m.s_ones, 1)
            for e in range(EXPERTS):
                dve.memset(m.expert_no[:, :, e:e + 1], float(e)).then_inc(m.s_ones, 1)
            dve.wait_ge(m.s_ones, 7 + EXPERTS)
    m.clear_semaphores()


def load_expert(sp, m, d, layer, e):
    i = e % WRING
    sp.dma_start(m.wgu[:, i, 0:FF], d["wg"][layer, e]).then_inc(m.s_expert[i], 16)
    sp.dma_start(m.wgu[:, i, FF:2 * FF], d["wu"][layer, e]).then_inc(m.s_expert[i], 16)
    sp.dma_start(m.wd[:, i, :, :], d["wd"][layer, e].rearrange("(j p) c -> p j c", p=P)).then_inc(m.s_expert[i], 16)


def attention_block(nc, m, d, layer):
    scores, heads = m.pair_bank, m.bank[4]
    with nc.Block() as block:
        @block.sync
        def _(sp):
            sp.dma_start(m.ln1[:, :], d["ln1_w"][layer].rearrange("(c o) -> c o", o=1)).then_inc(m.s_load, 16)
            sp.dma_start(m.wqkv[:, :, 0:REP * HD], d["wq"][layer].rearrange("c (g n) -> c g n", g=NKV)).then_inc(m.s_load, 16)
            sp.dma_start(m.wqkv[:, :, REP * HD:ROT], d["wk"][layer].rearrange("c (g n) -> c g n", g=NKV)).then_inc(m.s_load, 16)
            sp.dma_start(m.wqkv[:, :, ROT:GW], d["wv"][layer].rearrange("c (g n) -> c g n", g=NKV)).then_inc(m.s_load, 16)
            sp.dma_start(m.wo[:, :, :], d["wo"][layer].rearrange("(j p) c -> p j c", p=P)).then_inc(m.s_load_wo, 16)
            sp.dma_start(m.ln2[:, :], d["ln2_w"][layer].rearrange("(c o) -> c o", o=1)).then_inc(m.s_load_moe, 16)
            sp.dma_start(m.wr[:, :], d["wr"][layer]).then_inc(m.s_load_moe, 16)
            for e in range(WRING):
                load_expert(sp, m, d, layer, e)
            for g in range(GROUPS):
                sp.wait_ge(m.s_maxrow, g + 1)
                sp.dma_start(m.scratch[g % 2], m.maxrow[g % 2][:, :].bitcast(F32)).then_inc(m.s_scratch[g % 2], 16)
                sp.wait_ge(m.s_scratch[g % 2], 16 * (g // 2 + 1))
                if g >= 2:
                    sp.wait_ge(m.s_pv, (g - 1) * STEPS_PER_GROUP)
                sp.dma_start(m.q_shift[g % 2][MROW:MROW + 1, :, :].rearrange("o h (b c) -> o (h b) c", c=P).bitcast(F32),
                             m.scratch[g % 2].unsqueeze(0)).then_inc(m.s_shift[g % 2], 16)
            sp.wait_ge(m.s_load_moe, 2 * 16)
            for e in range(WRING):
                sp.wait_ge(m.s_expert[e], 3 * 16)

        @block.vector
        def _(dve):
            def squares(b, to):
                dve.tensor_tensor(to, m.x[:, b, :, :], m.x[:, b, :, :], ALU.mult).then_inc(m.s_norm_v, 1)
                dve.wait_ge(m.s_norm_v, 3 * b + 1)
                dve.reduce_sum(m.stat[:, 0, b, :], to, AX.X).then_inc(m.s_norm_v, 1)

            def normal(b):
                dve.wait_ge(m.s_norm_a, 2 * (b + 1))
                dve.tensor_tensor(m.square[:, :, :], m.x[:, b, :, :], m.stat[:, 2, b, :].unsqueeze(2).broadcast_to([P, TT, P]),
                                  ALU.mult).then_inc(m.s_norm_v, 1)

            squares(0, m.square[:, :, :])
            normal(0)
            squares(1, m.mixed[:, 0, :].rearrange("p (t c) -> p t c", c=C))
            dve.wait_ge(m.s_norm_v, 5)

            def unit(n):
                kind, g = UNITS[n][0:2]
                buf = g % 2
                if kind == "project":
                    tt = UNITS[n][2]
                    if tt % 2 == 0:
                        return
                    dve.wait_ge(m.s_raw, g * TT + tt + 1)
                    a = slice(tt - 1, tt + 1)
                    r = slice((tt - 1) % RAW, (tt - 1) % RAW + 2)
                    dve.tensor_tensor(m.rotated[:, a, :, :], m.raw[:, r, :, :],
                                      m.cos[:, a, :].unsqueeze(2).broadcast_to([P, 2, REP + 1, HD]),
                                      ALU.mult).then_inc(m.s_cos, 1)
                    i = g * TT // 2 + tt // 2 + 1
                    dve.wait_ge(m.s_sin, i)
                    dve.wait_ge(m.s_cos, i)
                    dve.tensor_tensor(m.rotated[:, a, :, :], m.rotated[:, a, :, :], m.swapped[:, r, :, :],
                                      ALU.add).then_inc(m.s_rotated, 1)
                elif kind == "turn":
                    j, half = UNITS[n][2:4]
                    cols = slice(half * HALF, (half + 1) * HALF)
                    if j == REP:
                        dve.wait_ge(m.s_high, highs(n))
                        dve.tensor_tensor(m.k_rest[buf][0:HD, cols], m.bank[bank_of(n)][0:HD, :],
                                          m.k_twice[buf][0:HD, cols].bitcast(F32), ALU.subtract).then_inc(m.s_low, 1)
                    else:
                        for i in range(2):
                            dve.wait_ge(m.s_high, highs(n) - 1 + i)
                            dve.tensor_tensor(m.q_full[buf][HD:P, j + i, cols], m.bank[bank_of(n)][i * HD:(i + 1) * HD, :],
                                              m.q_full[buf][0:HD, j + i, cols].bitcast(F32),
                                              ALU.subtract).then_inc(m.s_low if i else m.s_low0, 1)
                elif kind == "coarse":
                    j, qb, k0, keys = UNITS[n][2:6]
                    dve.wait_ge(m.s_unit, n + 1)
                    if g >= 2 and j == 0 and qb == 0 and k0 == 0:
                        dve.wait_ge(m.s_maxrow, g - 1)
                    to = m.maxima if k0 == 0 else m.maxima2
                    dve.reduce_max(to[buf][:, j, qb:qb + 1], m.bank[bank_of(n)][:, 0:keys], AX.X).then_inc(m.s_max, 1)
                elif kind == "norm":
                    if UNITS[n][2] == 0:
                        normal(1)
                elif kind == "output":
                    dve.wait_ge(m.s_unit, n + 1)
                    a = slice(UNITS[n][2] * TT // 2, (UNITS[n][2] + 1) * TT // 2)
                    dve.tensor_tensor(m.x[:, 0, a, :], m.bank[bank_of(n)][:, :].rearrange("p (t c) -> p t c", c=C),
                                      m.x[:, 0, a, :], ALU.add).then_inc(m.s_sum, 1)
                elif kind == "maxima":
                    dve.wait_ge(m.s_max, ordinal("coarse", n))
                    dve.tensor_tensor(m.maxima[buf][:, :, TT // 2:TT], m.maxima[buf][:, :, TT // 2:TT],
                                      m.maxima2[buf][:, :, TT // 2:TT], ALU.max).then_inc(m.s_rowmax, 1)

            def add(s):
                ch = chunk_of(s)
                dve.wait_ge(m.s_masked if is_diagonal(s) else m.s_probs, masks_until(s) if is_diagonal(s) else s + 1)
                dve.wait_ge(m.s_pv, s - STEPS[s][3] + 1)
                if STEPS[s][3] > 1:
                    dve.wait_ge(m.s_add_v, adds_until(s - 1))
                to = m.prob_sum[ch % 2][:, 0, first_query(s):]
                dve.tensor_tensor(to, to, m.probs[s % PROBS][:, 0, first_query(s):], ALU.add).then_inc(m.s_add_v, 1)

            for n in range(len(FIRST_UNITS)):
                unit(n)
            for s in range(ALL_STEPS):
                if 0 <= s - ADD_LAG < len(STEPS) and STEPS[s - ADD_LAG][3] > 0:
                    add(s - ADD_LAG)
                for n in units_at(s):
                    unit(n)
            for i in range(2):
                dve.wait_ge(m.s_wo, i + 1)
                a = slice(i * TT // 2, (i + 1) * TT // 2)
                dve.tensor_tensor(m.x[:, 1, a, :], m.bank[i][:, :].rearrange("p (t c) -> p t c", c=C), m.x[:, 1, a, :],
                                  ALU.add).then_inc(m.s_sum, 1)
            dve.wait_ge(m.s_sum, 4)
            dve.tensor_scalar(m.x[:, :, :, :], m.x[:, :, :, :], -LIMIT, LIMIT, ALU.max, ALU.min).then_inc(m.s_sum, 1)
            dve.wait_ge(m.s_sum, 5)

        @block.gpsimd
        def _(pool):
            def swap(n):
                kind, g, tt = UNITS[n][0:3]
                if tt % 2 == 0:
                    return
                a = slice(tt - 1, tt + 1)
                r = slice((tt - 1) % RAW, (tt - 1) % RAW + 2)
                i = g * TT // 2 + tt // 2
                pool.wait_ge(m.s_raw, g * TT + tt + 1)
                if i >= RAW // 2:
                    pool.wait_ge(m.s_rotated, i + 1 - RAW // 2)
                for f in range(2):
                    pool.tensor_tensor(m.swapped[:, r, :, f * 32:f * 32 + 32], m.raw[:, r, :, 32 - f * 32:64 - f * 32],
                                       m.sin[:, a, f * 32:f * 32 + 32].unsqueeze(2).broadcast_to([P, 2, REP + 1, 32]),
                                       ALU.mult).then_inc(m.s_sin if f else m.s_sin0, 1)

            def mask(s):
                ch, q0 = chunk_of(s), first_query(s)
                pool.wait_ge(m.s_probs, s + 1)
                v = (m.probs[s % PROBS] if STEPS[s][3] else m.prob_sum[ch % 2])[:, :, q0:q0 + P]
                pool.affine_select(out=v, in_=v, compare_op=ALU.is_ge, fill=0.0, base=0, pattern=[[0, 2], [1, P]],
                                   channel_multiplier=-1).then_inc(m.s_masked, 1)

            def add(s):
                ch = chunk_of(s)
                pool.wait_ge(m.s_masked if is_diagonal(s) else m.s_probs, masks_until(s) if is_diagonal(s) else s + 1)
                pool.wait_ge(m.s_pv, s - STEPS[s][3] + 1)
                if STEPS[s][3] > 1:
                    pool.wait_ge(m.s_add_p, adds_until(s - 1))
                to = m.prob_sum[ch % 2][:, 1, first_query(s):]
                pool.tensor_tensor(to, to, m.probs[s % PROBS][:, 1, first_query(s):], ALU.add).then_inc(m.s_add_p, 1)

            def store(ch):
                pool.wait_ge(m.s_recip, ch + 1)
                pool.wait_ge(m.s_taken, ch + 1)
                to = mixed_of(m, ch)
                pool.tensor_tensor(to, to, m.recip[:, :], ALU.mult).then_inc(m.s_stored, 1)

            def unit(n):
                if UNITS[n][0] == "project":
                    swap(n)
                if UNITS[n][0] == "denominators":
                    store(UNITS[n][2])

            for n in range(len(FIRST_UNITS)):
                unit(n)
            for s in range(ALL_STEPS):
                if s < len(STEPS) and is_diagonal(s):
                    mask(s)
                if 0 <= s - ADD_LAG < len(STEPS) and STEPS[s - ADD_LAG][3] > 0:
                    add(s - ADD_LAG)
                for n in units_at(s):
                    unit(n)

        @block.scalar
        def _(act):
            act.preload_act_table_set("natural_log_exp_and_others")
            def root(b):
                act.wait_ge(m.s_norm_v, 3 * b + 2)
                act.activation(m.stat[:, 1, b, :], m.stat[:, 0, b, :], ACT.Ln, bias=m.eps[:, 0:1], scale=1.0 / C).then_inc(m.s_norm_a, 1)
                act.wait_ge(m.s_norm_a, 2 * b + 1)
                act.activation(m.stat[:, 2, b, :], m.stat[:, 1, b, :], ACT.Exp, scale=-0.5).then_inc(m.s_norm_a, 1)

            root(0)
            act.wait_ge(m.s_load, 4 * 16)
            for i in range(2):
                act.wait_ge(m.s_turn_x, i + 1)
                act.mul(m.hT[:, i * HALF:(i + 1) * HALF], m.bank[i][:, :], m.ln1[:, 0:1]).then_inc(m.s_hT, 1)
            root(1)

            def unit(n):
                kind, g = UNITS[n][0:2]
                buf = g % 2
                if kind == "project":
                    tt = UNITS[n][2]
                    act.wait_ge(m.s_unit, n + 1)
                    if g >= 2:
                        act.wait_ge(m.s_pv, (g - 1) * STEPS_PER_GROUP)
                    act.copy(m.values[buf][:, tt, :], m.bank[bank_of(n)][:, ROT:GW]).then_inc(m.s_value, 1)
                    before = (g * TT + tt - RAW) // 2 + 1
                    if before > 0:
                        act.wait_ge(m.s_cos, before)
                        act.wait_ge(m.s_sin, before)
                    act.copy(m.raw[:, tt % RAW, :, :], m.bank[bank_of(n)][:, 0:ROT].rearrange("p (h e) -> p h e", e=HD)).then_inc(m.s_raw, 1)
                elif kind == "turn":
                    j, half = UNITS[n][2:4]
                    cols = slice(half * HALF, (half + 1) * HALF)
                    act.wait_ge(m.s_unit, n + 1)
                    if g >= 2:
                        act.wait_ge(m.s_pv, (g - 1) * STEPS_PER_GROUP)
                    if j == REP:
                        act.copy(m.k_twice[buf][HD:P, cols], m.bank[bank_of(n)][0:HD, :]).then_inc(m.s_high0, 1)
                        act.copy(m.k_twice[buf][0:HD, cols], m.bank[bank_of(n)][0:HD, :]).then_inc(m.s_high, 1)
                    else:
                        for i in range(2):
                            act.copy(m.q_full[buf][0:HD, j + i, cols], m.bank[bank_of(n)][i * HD:(i + 1) * HD, :]).then_inc(m.s_high, 1)
                        act.wait_ge(m.s_high, highs(n))
                        act.copy(m.q_shift[buf][0:HD, j:j + 2, cols], m.q_full[buf][0:HD, j:j + 2, cols]).then_inc(m.s_second, 1)
                elif kind == "denominators":
                    ch = UNITS[n][2]
                    act.wait_ge(m.s_unit, n + 1)
                    if ch:
                        act.wait_ge(m.s_stored, ch)
                    act.activation(m.recip[:, :], m.bank[bank_of(n)][:, :], ACT.Ln).then_inc(m.s_logden, 1)
                    act.wait_ge(m.s_logden, ch + 1)
                    act.activation(m.recip[:, :], m.recip[:, :], ACT.Exp, scale=-1.0).then_inc(m.s_recip, 1)
                elif kind == "norm":
                    half = UNITS[n][2]
                    act.wait_ge(m.s_unit, n + 1)
                    act.mul(m.hT[:, half * HALF:(half + 1) * HALF], m.bank[bank_of(n)][:, :], m.ln1[:, 0:1]).then_inc(m.s_hT, 1)
                elif kind == "maxima":
                    act.wait_ge(m.s_unit, n + 1)
                    if g >= 2:
                        act.wait_ge(m.s_shift[buf], 16 * (g // 2))
                    act.mul(m.maxrow[buf][:, :], m.bank[bank_of(n)][0:REP * TT, 0:P], -1.0).then_inc(m.s_maxrow, 1)

            def take(ch):
                act.wait_ge(m.s_pv, CHUNK_END[ch] + 1)
                if ch == BATCH_CHUNKS:
                    act.wait_ge(m.s_sum, 2)
                act.copy(mixed_of(m, ch), heads[:, :]).then_inc(m.s_taken, 1)

            def exponentials(s):
                ch, q0 = chunk_of(s), first_score(s)
                act.wait_ge(m.s_scores, s + 1)
                if STEPS[s][3] == 0:
                    to = m.prob_sum[ch % 2]
                    if ch >= 2:
                        act.wait_ge(m.s_unit, UNITS.index(("denominators", STEPS[CHUNK_END[ch - 2]][0], ch - 2)) + 1)
                else:
                    to = m.probs[s % PROBS]
                    if s >= PROBS:
                        act.wait_ge(m.s_pv, s - PROBS + 1)
                        act.wait_ge(m.s_add_v, adds_until(s - PROBS))
                        act.wait_ge(m.s_add_p, adds_until(s - PROBS))
                act.activation(to[:, :, q0:HALF], scores[s % 2][:, :].rearrange("p (k q) -> p k q", k=2)[:, :, q0:HALF],
                               ACT.Exp, scale=1.0 / math.sqrt(HD)).then_inc(m.s_probs, 1)

            for n in range(len(FIRST_UNITS)):
                unit(n)
            for s in range(ALL_STEPS):
                if s < len(STEPS):
                    exponentials(s)
                for n in units_at(s):
                    unit(n)
                if s - MIX_LAG in CHUNK_END:
                    take(CHUNK_END.index(s - MIX_LAG))

        @block.tensor
        def _(pe):
            pe.wait_ge(m.s_norm_v, 3)
            for tt in range(TT):
                mm = pe.transpose(m.bank[tt // 4][:, (tt % 4) * P:(tt % 4 + 1) * P], m.square[:, tt, :], m.ident[:, :])
                if tt % 4 == 3:
                    mm.then_inc(m.s_turn_x, 1)

            def released(n):
                kind = UNITS[n][0]
                if kind == "norm":
                    pe.wait_ge(m.s_hT, 2 + ordinal(kind, n))
                else:
                    sem = {"project": m.s_raw, "turn": m.s_low, "coarse": m.s_max, "maxima": m.s_maxrow, "output": m.s_sum,
                           "denominators": m.s_logden}[kind]
                    pe.wait_ge(sem, ordinal(kind, n))

            def output(to, b, tt):
                for j in range(NH // 2):
                    mm = pe.matmul(to[:, (tt % 4) * C:(tt % 4 + 1) * C], m.mixed[:, j, tt * P:(tt + 1) * P],
                                   m.wo[:, j, :], start=(j == 0), stop=(j == NH // 2 - 1))
                return mm

            def unit(n):
                kind, g = UNITS[n][0:2]
                buf, to, before = g % 2, m.bank[bank_of(n)], user_before(n)
                if before is not None:
                    released(before)
                if kind == "project":
                    tt = UNITS[n][2]
                    if g % NKV == 0:
                        pe.wait_ge(m.s_hT, 2 * (g // NKV) + tt // 4 + 1)
                    mm = pe.matmul(to[:, 0:GW], m.hT[:, tt * P:(tt + 1) * P], m.wqkv[:, g % NKV, :], start=True, stop=True)
                    mm.then_inc(m.s_unit, 1)
                elif kind == "turn":
                    j, half = UNITS[n][2:4]
                    pe.wait_ge(m.s_rotated, (g * TT + half * 4) // 2 + 2)
                    heads_here = slice(j, j + (1 if j == REP else 2))
                    for i in range(4):
                        rows = m.rotated[:, half * 4 + i, heads_here, :].rearrange("p h e -> p (h e)")
                        mm = pe.transpose(to[0:rows.shape[1], i * P:(i + 1) * P], rows, m.ident[:, :])
                    mm.then_inc(m.s_unit, 1)
                elif kind == "coarse":
                    j, qb, k0, keys = UNITS[n][2:6]
                    if k0 == 0:
                        pe.wait_ge(m.s_low, max(turned(g, REP, qb // 4), turned(g, j, qb // 4)))
                    diagonal = k0 + keys == (qb + 1) * P
                    mm = pe.matmul(to[:, 0:keys], m.q_full[buf][:, j, qb * P:(qb + 1) * P], m.k_twice[buf][:, k0:k0 + keys],
                                   start=True, stop=not diagonal)
                    if diagonal:
                        mm = pe.matmul(to[:, keys - P:keys], m.ident16[:, :], m.later16[:, :], start=False, stop=True)
                    mm.then_inc(m.s_unit, 1)
                elif kind == "norm":
                    half = UNITS[n][2]
                    pe.wait_ge(m.s_norm_v, 6)
                    for i in range(4):
                        mm = pe.transpose(to[:, i * P:(i + 1) * P], m.square[:, half * 4 + i, :], m.ident[:, :])
                    mm.then_inc(m.s_unit, 1)
                elif kind == "output":
                    pe.wait_ge(m.s_load_wo, 16)
                    pe.wait_ge(m.s_stored, BATCH_CHUNKS)
                    for tt in range(UNITS[n][2] * TT // 2, (UNITS[n][2] + 1) * TT // 2):
                        mm = output(to, 0, tt)
                    mm.then_inc(m.s_unit, 1)
                elif kind == "denominators":
                    ch = UNITS[n][2]
                    pe.wait_ge(m.s_add_v, adds_until(CHUNK_END[ch]))
                    pe.wait_ge(m.s_add_p, adds_until(CHUNK_END[ch]))
                    for i in range(2):
                        mm = pe.matmul(to[i * HD:(i + 1) * HD, :], m.ones[:, :], m.prob_sum[ch % 2][:, i, :], start=True, stop=True)
                    mm.then_inc(m.s_unit, 1)
                else:
                    pe.wait_ge(m.s_rowmax, g + 1)
                    mm = pe.transpose(to[0:REP * TT, 0:P], m.maxima[buf][:, :, :], m.ident[:, :])
                    mm.then_inc(m.s_unit, 1)

            def score(s, i):
                g, pair, qc, kt = STEPS[s]
                buf, q0 = g % 2, first_score(s)
                if s % STEPS_PER_GROUP == 0 and i == 0:
                    pe.wait_ge(m.s_low, turned(g, 2, 1))
                    pe.wait_ge(m.s_value, TT * (g + 1))
                    pe.wait_ge(m.s_second, REP * (g + 1))
                    pe.wait_ge(m.s_shift[buf], 16 * (g // 2 + 1))
                if s >= 2 and i == 0:
                    pe.wait_ge(m.s_probs, s - 1)
                cols = slice(qc * HALF + q0, (qc + 1) * HALF)
                keys = slice(kt * P, (kt + 1) * P)
                to = scores[s % 2][:, i * HALF + q0:(i + 1) * HALF]
                pe.matmul(to, m.k_twice[buf][:, keys], m.q_full[buf][:, 2 * pair + i, cols], start=True, stop=False)
                mm = pe.matmul(to, m.k_rest[buf][:, keys], m.q_shift[buf][:, 2 * pair + i, cols], start=False, stop=True)
                if i == 1:
                    mm.then_inc(m.s_scores, 1)

            def mix(s):
                g, pair, qc, kt = STEPS[s]
                ch, q0 = chunk_of(s), first_query(s)
                if is_diagonal(s):
                    pe.wait_ge(m.s_masked, masks_until(s))
                else:
                    pe.wait_ge(m.s_probs, s + 1)
                if kt == 0 and ch:
                    pe.wait_ge(m.s_taken, ch)
                probs = m.probs[s % PROBS] if kt else m.prob_sum[ch % 2]
                for i in range(2):
                    mm = pe.matmul(heads[i * HD:(i + 1) * HD, q0:HALF], m.values[g % 2][:, kt, :], probs[:, i, q0:HALF],
                                   start=(kt == 0), stop=(s == CHUNK_END[ch]))
                mm.then_inc(m.s_pv, 1)

            for n in range(len(FIRST_UNITS)):
                unit(n)
            for s in range(ALL_STEPS):
                for part in range(PARTS):
                    if part < 2 and s < len(STEPS):
                        score(s, part)
                    if part == 2 and 0 <= s - MIX_LAG < len(STEPS):
                        mix(s - MIX_LAG)
                    for n in units_at(s, part):
                        unit(n)

            pe.wait_ge(m.s_stored, CHUNKS)
            pe.wait_ge(m.s_probs, len(STEPS))
            for tt in range(TT):
                mm = output(m.bank[tt // 4], 1, tt)
                if tt % 4 == 3:
                    mm.then_inc(m.s_wo, 1)
    m.clear_semaphores()


def moe_block(nc, m, d, layer):
    halves = 2 * BATCH
    parts = EXPERTS * BATCH * FCH
    with nc.Block() as block:
        @block.sync
        def _(sp):
            for e in range(WRING, EXPERTS):
                sp.wait_ge(m.s_down_unit, BATCH * FCH * (e - WRING + 1))
                load_expert(sp, m, d, layer, e)

        @block.gpsimd
        def _(pool):
            for e in range(EXPERTS):
                w = e % WRING
                if e >= WRING:
                    pool.wait_ge(m.s_expert[w], 3 * 16)
                    pool.wait_ge(m.s_up, BATCH * FCH * (e - WRING + 1))
                pool.tensor_copy(m.w_hi[:, w, :], m.wgu[:, w, :]).then_inc(m.s_w_hi, 1)
                pool.wait_ge(m.s_w_hi, e + 1)
                pool.tensor_tensor(m.w_lo[:, w, :], m.wgu[:, w, :], m.w_hi[:, w, :].bitcast(F32), ALU.subtract).then_inc(m.s_w_lo, 1)

        @block.vector
        def _(dve):
            for b in range(BATCH):
                dve.tensor_tensor(m.normal[:, b, :, :], m.x[:, b, :, :], m.x[:, b, :, :], ALU.mult).then_inc(m.s_norm_v, 1)
                dve.wait_ge(m.s_norm_v, 3 * b + 1)
                dve.reduce_sum(m.stat[:, 0, b, :], m.normal[:, b, :, :], AX.X).then_inc(m.s_norm_v, 1)
                dve.wait_ge(m.s_norm_a, 2 * (b + 1))
                dve.tensor_tensor(m.normal[:, b, :, :], m.x[:, b, :, :], m.stat[:, 2, b, :].unsqueeze(2).broadcast_to([P, TT, P]),
                                  ALU.mult).then_inc(m.s_norm_v, 1)
            for i in range(halves):
                t = slice(i * HALF, (i + 1) * HALF)
                dve.wait_ge(m.s_h_hi, i + 1)
                dve.tensor_tensor(m.h_lo[:, t], m.h[:, t], m.h_hi[:, t].bitcast(F32), ALU.subtract).then_inc(m.s_h_lo, 1)

            pick, k = m.pick, 0

            def wide(a):
                return a.unsqueeze(2).broadcast_to([P, BATCH * TT, EXPERTS])

            def then(ins):
                nonlocal k
                k += 1
                ins.then_inc(m.s_pick, 1)
                dve.wait_ge(m.s_pick, k)

            def hot(values, to, largest, first):
                then(dve.reduce_max(largest, values, AX.X))
                then(dve.tensor_tensor(to, values, wide(largest), ALU.is_equal))
                then(dve.tensor_scalar(m.rank[:, :, :], m.expert_no[:, :, :], -1.0, float(EXPERTS), ALU.mult, ALU.add))
                then(dve.tensor_tensor(m.rank[:, :, :], m.rank[:, :, :], to, ALU.mult))
                then(dve.reduce_max(first, m.rank[:, :, :], AX.X))
                then(dve.tensor_tensor(to, m.rank[:, :, :], wide(first), ALU.is_equal))

            def shares():
                dve.wait_ge(m.s_routed, 1)
                hot(pick[:, 1, :, :], pick[:, 2, :, :], m.top[:, 1, :], m.top[:, 2, :])
                then(dve.scalar_tensor_tensor(pick[:, 3, :, :], pick[:, 1, :, :], 1.0, pick[:, 2, :, :], ALU.add, ALU.mult))
                then(dve.tensor_tensor(pick[:, 3, :, :], pick[:, 1, :, :], pick[:, 3, :, :], ALU.subtract))
                hot(pick[:, 3, :, :], pick[:, 4, :, :], m.top[:, 3, :], m.top[:, 4, :])
                then(dve.tensor_tensor(pick[:, 4, :, :], pick[:, 4, :, :], pick[:, 2, :, :], ALU.add))
                then(dve.tensor_tensor(pick[:, 4, :, :], pick[:, 4, :, :], pick[:, 1, :, :], ALU.mult))
                then(dve.reduce_sum(m.top[:, 5, :], pick[:, 4, :, :], AX.X))
                then(dve.reciprocal(m.top[:, 6, :], m.top[:, 5, :]))
                then(dve.tensor_tensor(m.share[:, :, :], pick[:, 4, :, :], wide(m.top[:, 6, :]), ALU.mult))

            dve.wait_ge(m.s_router, 1)
            logits = m.bank[4][:, 0:BATCH * TT * EXPERTS].rearrange("p (t e) -> p t e", e=EXPERTS)
            then(dve.reduce_max(m.top[:, 0, :], logits, AX.X))
            then(dve.tensor_tensor(pick[:, 0, :, :], logits, wide(m.top[:, 0, :]), ALU.subtract))

            def gated(i):
                dve.wait_ge(m.s_silu, i + 1)
                dve.wait_ge(m.s_up, i + 1)
                if i >= 2:
                    dve.wait_ge(m.s_down_unit, i - 1)
                dve.tensor_tensor(m.act_in[i % 2][:, :], m.up_bank[:, :], m.silu[i % 2][:, :], ALU.mult).then_inc(m.s_gated, 1)

            def weigh(n):
                e, b = divmod(n, BATCH)
                dve.wait_ge(m.s_down_unit, FCH * (n + 1))
                if n >= BATCH:
                    dve.wait_ge(m.s_weighed, TT * (n - 1))
                for tt in range(TT):
                    dve.scalar_tensor_tensor(m.moe[:, b, tt, :],
                                             m.down_bank[n % 2][:, tt * C:(tt + 1) * C],
                                             m.share[:, b * TT + tt, e:e + 1], m.moe[:, b, tt, :] if e else m.x[:, b, tt, :],
                                             ALU.mult, ALU.add).then_inc(m.s_weighed, 1)

            for n in range(EXPERTS * BATCH):
                for f in range(FCH):
                    gated(n * FCH + f)
                    if f == 0 and n:
                        weigh(n - 1)
                if n == 0:
                    shares()
            weigh(EXPERTS * BATCH - 1)
            dve.wait_ge(m.s_weighed, TT * EXPERTS * BATCH)
            dve.tensor_scalar(m.x[:, :, :, :], m.moe[:, :, :, :], -LIMIT, LIMIT, ALU.max, ALU.min).then_inc(m.s_sum, 1)
            dve.wait_ge(m.s_sum, 1)

        @block.scalar
        def _(act):
            act.preload_act_table_set("natural_log_exp_and_others")
            for b in range(BATCH):
                act.wait_ge(m.s_norm_v, 3 * b + 2)
                act.activation(m.stat[:, 1, b, :], m.stat[:, 0, b, :], ACT.Ln, bias=m.eps[:, 0:1], scale=1.0 / C).then_inc(m.s_norm_a, 1)
                act.wait_ge(m.s_norm_a, 2 * b + 1)
                act.activation(m.stat[:, 2, b, :], m.stat[:, 1, b, :], ACT.Exp, scale=-0.5).then_inc(m.s_norm_a, 1)
            for i in range(halves):
                t = slice(i * HALF, (i + 1) * HALF)
                act.wait_ge(m.s_turn_x, i + 1)
                act.mul(m.h[:, t], m.bank[i][:, :], m.ln2[:, 0:1]).then_inc(m.s_hT, 1)
                act.wait_ge(m.s_hT, i + 1)
                act.copy(m.h_hi[:, t], m.h[:, t]).then_inc(m.s_h_hi, 1)
            act.wait_ge(m.s_pick, 2)
            act.activation(m.pick[:, 1, :, :], m.pick[:, 0, :, :], ACT.Exp).then_inc(m.s_routed, 1)
            for i in range(parts):
                act.wait_ge(m.s_gate, i + 1)
                if i >= 2:
                    act.wait_ge(m.s_gated, i - 1)
                act.activation(m.silu[i % 2][:, :], m.gate_bank[:, :], ACT.Silu).then_inc(m.s_silu, 1)

        @block.tensor
        def _(pe):
            for i in range(halves):
                if i % 2 == 0:
                    pe.wait_ge(m.s_norm_v, 3 * (i // 2 + 1))
                for tt in range(4):
                    mm = pe.transpose(m.bank[i][:, tt * P:(tt + 1) * P], m.normal[:, i // 2, i % 2 * 4 + tt, :], m.ident[:, :])
                mm.then_inc(m.s_turn_x, 1)
            for tt in range(BATCH * TT):
                if tt % 4 == 0:
                    pe.wait_ge(m.s_hT, tt // 4 + 1)
                mm = pe.matmul(m.bank[4][:, tt * EXPERTS:(tt + 1) * EXPERTS], m.h[:, tt * P:(tt + 1) * P], m.wr[:, :],
                               start=True, stop=True)
            mm.then_inc(m.s_router, 1)

            def product(bank, w, column, b):
                cols = slice(column, column + P)
                terms = ((m.w_hi, m.h_hi), (m.w_hi, m.h_lo), (m.w_lo, m.h_hi))
                for x, (weight, h) in enumerate(terms):
                    for half in range(2):
                        t = slice(half * HALF, (half + 1) * HALF)
                        source = slice(b * T + half * HALF, b * T + (half + 1) * HALF)
                        mm = pe.matmul(bank[:, t], weight[:, w, cols], h[:, source], start=(x == 0), stop=(x == len(terms) - 1))
                return mm

            def hidden(i):
                n, f = divmod(i, FCH)
                e, b = divmod(n, BATCH)
                w = e % WRING
                if i % (BATCH * FCH) == 0:
                    pe.wait_ge(m.s_w_lo, e + 1)
                if i % FCH == 0 and e == 0:
                    pe.wait_ge(m.s_h_lo, 2 * (b + 1))
                if i >= 1:
                    pe.wait_ge(m.s_silu, i)
                product(m.gate_bank, w, f * P, b).then_inc(m.s_gate, 1)
                if i >= 1:
                    pe.wait_ge(m.s_gated, i)
                product(m.up_bank, w, FF + f * P, b).then_inc(m.s_up, 1)

            def down(i):
                n, f = divmod(i, FCH)
                pe.wait_ge(m.s_gated, i + 1)
                if f == 0 and n == 1:
                    pe.wait_ge(m.s_pick, 2)
                if f == 0 and n >= 2:
                    pe.wait_ge(m.s_weighed, TT * (n - 1))
                for tt in range(TT):
                    mm = pe.matmul(m.down_bank[n % 2][:, tt * C:(tt + 1) * C], m.act_in[i % 2][:, tt * P:(tt + 1) * P],
                                   m.wd[:, n // BATCH % WRING, f, :], start=(f == 0 and tt % 4 == 0), stop=(f == FCH - 1),
                                   skip_group_check=True)
                mm.then_inc(m.s_down_unit, 1)

            for i in range(parts):
                hidden(i)
                if i:
                    down(i - 1)
            down(parts - 1)
    m.clear_semaphores()


def decoder_tensors(m):
    m.q_full = [m.sb(f"q_full{i}", [P, REP, T], F32R) for i in range(2)]
    parts = m.q_full[0][:, :, :].rearrange("p h t -> p (h t)")
    m.h_hi, m.h_lo = parts[:, 0:BATCH * T], parts[:, BATCH * T:2 * BATCH * T]
    parts = m.q_full[1][:, :, :].rearrange("p h t -> p (h t)")
    m.w_hi, m.w_lo = (parts[:, i * WRING * 2 * FF:(i + 1) * WRING * 2 * FF].rearrange("p (w n) -> p w n", w=WRING) for i in range(2))
    m.q_shift = [m.sb(f"q_shift{i}", [KROWS, REP, T], F32R) for i in range(2)]
    m.k_twice = [m.sb(f"k_twice{i}", [P, T], F32R) for i in range(2)]
    m.k_rest = [m.sb(f"k_rest{i}", [KROWS, T], F32R) for i in range(2)]
    m.values = [m.sb(f"values{i}", [P, TT, HD]) for i in range(2)]
    m.ones = m.sb("ones", [P, HD])
    m.raw = m.sb("raw", [P, RAW, REP + 1, HD])
    m.swapped = m.sb("swapped", [P, RAW, REP + 1, HD])
    m.rotated = m.sb("rotated", [P, TT, REP + 1, HD])
    m.probs = [m.sb(f"probs{i}", [P, 2, HALF]) for i in range(PROBS)]
    m.prob_sum = [m.sb(f"prob_sum{i}", [P, 2, HALF]) for i in range(2)]
    m.mixed = m.sb("mixed", [P, NH // 2, T])
    m.silu = [m.mixed[:, i, :] for i in range(2)]
    m.act_in = [m.mixed[:, 2 + i, :] for i in range(2)]
    m.moe = m.mixed[:, 4:6, :].rearrange("p b (t c) -> p b t c", c=C)
    m.normal = m.moe
    m.h = m.mixed[:, 6:8, :].rearrange("p b t -> p (b t)")
    m.x, m.square = m.sb("x", [P, BATCH, TT, C]), m.sb("square", [P, TT, C])
    m.recip = m.sb("recip", [P, HALF])
    m.maxima = [m.sb(f"maxima{i}", [P, REP, TT]) for i in range(2)]
    m.maxima2 = [m.sb(f"maxima2{i}", [P, REP, TT]) for i in range(2)]
    m.maxrow = [m.sb(f"maxrow{i}", [REP * TT, P], F32R) for i in range(2)]
    m.hT = m.sb("hT", [C, T])
    m.stat = m.sb("stat", [P, 3, BATCH, TT])
    m.ln1, m.ln2 = m.sb("ln1", [C, 1]), m.sb("ln2", [C, 1])
    m.wqkv = m.sb("wqkv", [C, NKV, GW])
    m.wo = m.sb("wo", [P, NH // 2, C])
    m.wr = m.sb("wr", [C, EXPERTS])
    m.wgu = m.sb("wgu", [C, WRING, 2 * FF])
    m.wd = m.sb("wd", [P, WRING, FCH, C])
    m.expert_no = m.sb("expert_no", [P, BATCH * TT, EXPERTS])
    room, at = m.probs[0][:, :, :].rearrange("p k n -> p (k n)"), 0
    for name, kinds in (("rank", 1), ("share", 1), ("pick", 5)):
        n = kinds * BATCH * TT * EXPERTS
        part = room[:, at:at + n]
        if name == "pick":
            m.pick = part.rearrange("p (k t e) -> p k t e", k=kinds, e=EXPERTS)
        elif name == "rank":
            m.rank = part.rearrange("p (t e) -> p t e", e=EXPERTS)
        else:
            m.share = part.rearrange("p (t e) -> p t e", e=EXPERTS)
        at += n
    m.top = room[:, at:at + 7 * BATCH * TT].rearrange("p (k t) -> p k t", k=7)



def branch_tensors(m):
    m.same_head = m.sb("same_head", [P, P])
    m.stacker = m.sb("stacker", [P, 4, P])
    m.head_mask = m.sb("head_mask", [P, 4])
    m.w_turned = m.sb("w_turned", [C, 4, C])
    m.b_col = m.sb("b_col", [P, 2])
    m.b_row = m.sb("b_row", [P, 2, C])
    m.temp_col, m.temp_row = m.sb("temp_col", [P, 1]), m.sb("temp_row", [P, AH])
    m.scale_work = m.sb("scale_work", [P, 4, 1 + AH])
    m.scale = m.sb("scale", [P, 1 + AH])
    m.shift = m.sb("shift", [P, AH])
    m.xT = m.sb("xT", [C, T])
    m.seqT = m.sb("seqT", [P, T])
    m.qk = [m.sb(f"qk{i}", [P, T]) for i in range(2)]
    m.qk_square = [m.sb(f"qk_square{i}", [P, T]) for i in range(2)]
    m.qk_norm = [m.sb(f"qk_norm{i}", [P, T]) for i in range(2)]
    m.q_stack = [m.sb(f"q_stack{i}", [P, T], F32R) for i in range(4)]
    m.key_stack = [m.sb(f"key_stack{i}", [P, T], F32R) for i in range(4)]


def recurrence_tensors(m):
    m.w_wide = m.sb("w_wide", [C, 4, STATES])
    m.b_wide = m.sb("b_wide", [P, 4, STATE_TILES])
    m.sum_rows = m.sb("sum_rows", [P, STATE_TILES, P])
    m.key_wide = [m.sb(f"key_wide{i}", [P, HALF]) for i in range(2)]
    m.decay = [m.sb(f"decay{i}", [P, HALF]) for i in range(2)]
    m.outer = [m.sb(f"outer{i}", [P, HALF]) for i in range(2)]
    m.read = [m.sb(f"read{i}", [P, HALF]) for i in range(2)]
    m.state = m.sb("state", [P, STATE_TILES, 2, HALF])


def attention_tensors(m):
    m.key_head = [m.sb(f"key_head{i}", [P, T], F32R) for i in range(AH // 2)]
    m.weights = [m.sb(f"weights{i}", [P, 2, HALF]) for i in range(4)]
    m.recip_a = [m.sb(f"recip_a{i}", [32, HALF]) for i in range(2)]
    m.mixedT = m.sb("mixedT", [P, T])
    m.v_wide = m.sb("v_wide", [P, TT, AH, 64])


def recurrence_block(nc, m, d):
    kinds = 4

    with nc.Block() as block:
        @block.sync
        def _(sp):
            sp.dma_start(m.w_wide[:, :, :], d["w_wide"].rearrange("k c n -> c k n")).then_inc(m.s_load, 16)
            sp.dma_start(m.b_wide[:, :, :], d["b_wide"].rearrange("k p j -> p k j")).then_inc(m.s_load, 16)
            sp.dma_start(m.sum_rows[:, :, :], d["sum_rows"].rearrange("j p n -> p j n")).then_inc(m.s_load, 16)
            sp.dma_start(m.same_head[:, :], d["same_head"]).then_inc(m.s_load_wo, 16)
            sp.dma_start(m.stacker[:, :, :], d["stacker"].rearrange("g p n -> p g n")).then_inc(m.s_load_wo, 16)
            sp.dma_start(m.head_mask[:, :], d["head_mask"]).then_inc(m.s_load_wo, 16)
            sp.dma_start(m.w_turned[:, :, :], d["w_turned"].rearrange("k c n -> c k n")).then_inc(m.s_load_wo, 16)
            sp.dma_start(m.b_col[:, :], d["b_col"]).then_inc(m.s_load_wo, 16)
            sp.dma_start(m.b_row[:, :, :], d["b_row"].unsqueeze(0).broadcast_to([P, 2, C])).then_inc(m.s_load_wo, 16)
            sp.dma_start(m.scale_work[:, 0, 0:1], d["temp_col"]).then_inc(m.s_load_moe, 16)
            sp.dma_start(m.scale_work[:, 0, 1:1 + AH], d["temp_row"].unsqueeze(0).broadcast_to([P, AH])).then_inc(m.s_load_moe, 16)
            sp.wait_ge(m.s_load_wo, 6 * 16)

        @block.tensor
        def _(pe):
            for tt in range(TT):
                mm = pe.transpose(m.bank[tt // 4][:, (tt % 4) * P:(tt % 4 + 1) * P], m.x[:, tt, :], m.ident[:, :])
                if tt % 4 == 3:
                    mm.then_inc(m.s_turn_x, 1)
            pe.wait_ge(m.s_load, 3 * 16)
            pe.wait_ge(m.s_hT, 2)

            def project(n):
                i, kind = divmod(n, kinds)
                half, j = divmod(i, STATE_TILES)
                if n >= 6:
                    sem = (m.s_key_wide, m.s_decay, m.s_outer, m.s_read)[(n - 6) % kinds]
                    pe.wait_ge(sem, (n - 6) // kinds + 1)
                pe.matmul(m.bank[n % 6][:, :], m.w_wide[:, kind, j * P:(j + 1) * P], m.xT[:, half * HALF:(half + 1) * HALF],
                          start=True, stop=True).then_inc(m.s_unit, 1)

            def gather(i):
                half, j = divmod(i, STATE_TILES)
                pe.wait_ge(m.s_read, i + 1)
                pe.matmul(m.bank[6 + half][:, :], m.sum_rows[:, j, :], m.read[i % 2][:, :],
                          start=(j == 0), stop=(j == STATE_TILES - 1)).then_inc(m.s_gathered, 1)

            for i in range(2 * STATE_TILES):
                for kind in range(kinds):
                    project(i * kinds + kind)
                if i:
                    gather(i - 1)
            gather(2 * STATE_TILES - 1)

        @block.scalar
        def _(act):
            for i in range(2):
                act.wait_ge(m.s_turn_x, i + 1)
                act.copy(m.xT[:, i * HALF:(i + 1) * HALF], m.bank[i][:, :]).then_inc(m.s_hT, 1)
            act.wait_ge(m.s_norm_v, 1)
            for i in range(2 * STATE_TILES):
                j = i % STATE_TILES
                act.wait_ge(m.s_unit, kinds * i + 1)
                if i >= 2:
                    act.wait_ge(m.s_outer, i - 1)
                act.activation(m.key_wide[i % 2][:, :], m.bank[(kinds * i) % 6][:, :], ACT.Identity,
                               bias=m.b_wide[:, 0, j:j + 1]).then_inc(m.s_key_wide, 1)
                act.wait_ge(m.s_unit, kinds * i + 2)
                if i >= 2:
                    act.wait_ge(m.s_state, i - 1)
                act.activation(m.decay[i % 2][:, :], m.bank[(kinds * i + 1) % 6][:, :], ACT.Sigmoid,
                               bias=m.b_wide[:, 1, j:j + 1], scale=-1.0).then_inc(m.s_decay, 1)
            for half in range(2):
                act.wait_ge(m.s_gathered, (half + 1) * STATE_TILES)
                act.copy(m.seqT[:, half * HALF:(half + 1) * HALF], m.bank[6 + half][:, :]).then_inc(m.s_hT, 1)
            act.wait_ge(m.s_scale, 2)
            act.activation(m.scale_work[:, 2, :], m.scale_work[:, 1, :], ACT.Exp, scale=-1.0).then_inc(m.s_norm_a, 1)
            act.wait_ge(m.s_norm_a, 1)
            act.activation(m.scale_work[:, 3, :], m.scale_work[:, 2, :], ACT.Ln, bias=1.0).then_inc(m.s_norm_a, 1)

        @block.vector
        def _(dve):
            dve.wait_ge(m.s_load, 3 * 16)
            dve.tensor_scalar(m.b_wide[:, 1, :], m.b_wide[:, 1, :], -1.0, None, ALU.mult).then_inc(m.s_norm_v, 1)
            dve.wait_ge(m.s_load_moe, 2 * 16)
            dve.tensor_scalar(m.scale_work[:, 1, :], m.scale_work[:, 0, :], -1.0, None, ALU.mult).then_inc(m.s_scale, 1)
            dve.wait_ge(m.s_scale, 1)
            dve.tensor_tensor(m.scale_work[:, 1, :], m.scale_work[:, 1, :], m.scale_work[:, 0, :], ALU.max).then_inc(m.s_scale, 1)

            def read_out(i):
                j = i % STATE_TILES
                dve.wait_ge(m.s_unit, kinds * i + 4)
                if i >= 2:
                    dve.wait_ge(m.s_gathered, i - 1)
                dve.scalar_tensor_tensor(m.read[i % 2][:, :], m.bank[(kinds * i + 3) % 6][:, :], m.b_wide[:, 3, j:j + 1],
                                         m.state[:, j, i // STATE_TILES, :], ALU.add, ALU.mult).then_inc(m.s_read, 1)

            for i in range(2 * STATE_TILES):
                half, j = divmod(i, STATE_TILES)
                dve.wait_ge(m.s_unit, kinds * i + 3)
                dve.wait_ge(m.s_key_wide, i + 1)
                if i >= 2:
                    dve.wait_ge(m.s_state, i - 1)
                dve.scalar_tensor_tensor(m.outer[i % 2][:, :], m.bank[(kinds * i + 2) % 6][:, :], m.b_wide[:, 2, j:j + 1],
                                         m.key_wide[i % 2][:, :], ALU.add, ALU.mult).then_inc(m.s_outer, 1)
                dve.wait_ge(m.s_decay, i + 1)
                dve.wait_ge(m.s_outer, i + 1)
                dve.tensor_tensor_scan(m.state[:, j, half, :], m.decay[i % 2][:, :], m.outer[i % 2][:, :],
                                       m.state[:, j, 0, HALF - 1:HALF] if half else 0.0,
                                       ALU.mult, ALU.add).then_inc(m.s_state, 1)
                dve.wait_ge(m.s_state, i + 1)
                read_out(i)
            dve.wait_ge(m.s_norm_a, 2)
            dve.scalar_tensor_tensor(m.scale[:, :], m.scale_work[:, 0, :], 0.0, m.scale_work[:, 3, :], ALU.max,
                                     ALU.add).then_inc(m.s_scale, 1)
            dve.wait_ge(m.s_scale, 3)
            dve.tensor_scalar(m.shift[:, :], m.scale[:, 1:1 + AH], -TALL, 0.0, ALU.add, ALU.max).then_inc(m.s_scale, 1)
            dve.wait_ge(m.s_scale, 4)
            dve.tensor_scalar(m.shift[:, :], m.shift[:, :], -1.0, None, ALU.mult).then_inc(m.s_scale, 1)
            dve.wait_ge(m.s_scale, 5)
    m.clear_semaphores()


def heads_block(nc, m):
    q, k = 0, 1
    with nc.Block() as block:
        @block.tensor
        def _(pe):
            for i in (q, k):
                for half in range(2):
                    t = slice(half * HALF, (half + 1) * HALF)
                    mm = pe.matmul(m.pair_bank[i][:, t], m.w_turned[:, i, :], m.seqT[:, t], start=True, stop=True)
                mm.then_inc(m.s_unit, 1)
            for tt in range(TT):
                mm = pe.matmul(m.pair_bank[2][:, tt * C:(tt + 1) * C], m.xT[:, tt * P:(tt + 1) * P], m.w_turned[:, 2, :],
                               start=True, stop=True)
            mm.then_inc(m.s_unit, 1)
            for i in (q, k):
                pe.wait_ge(m.s_square, i + 1)
                if i == k:
                    pe.wait_ge(m.s_value, 5)
                for half in range(2):
                    t = slice(half * HALF, (half + 1) * HALF)
                    mm = pe.matmul(m.pair_bank[3 - i][:, t], m.same_head[:, :], m.qk_square[i][:, t], start=True, stop=True)
                mm.then_inc(m.s_sumsq, 1)
            for n in range(8):
                i, g = divmod(n, 4)
                pe.wait_ge(m.s_unit_length, i + 1)
                if n >= 2:
                    pe.wait_ge(m.s_low, n - 1)
                for half in range(2):
                    t = slice(half * HALF, (half + 1) * HALF)
                    mm = pe.matmul(m.pair_bank[n % 2][:, t], m.stacker[:, g, :], m.qk[i][:, t], start=True, stop=True)
                mm.then_inc(m.s_stacked, 1)

        @block.scalar
        def _(act):
            for i in (q, k):
                act.wait_ge(m.s_unit, i + 1)
                act.activation(m.qk[i][:, :], m.pair_bank[i][:, :], ACT.Identity, bias=m.b_col[:, i:i + 1]).then_inc(m.s_qk, 1)
            for i in (q, k):
                act.wait_ge(m.s_sumsq, i + 1)
                act.activation(m.qk_norm[i][:, :], m.pair_bank[3 - i][:, :], ACT.Sqrt).then_inc(m.s_norm_a, 1)
            for n in range(8):
                act.wait_ge(m.s_stacked, n + 1)
                to = (m.q_stack if n < 4 else m.key_stack)[n % 4]
                act.copy(to[:, :], m.pair_bank[n % 2][:, :]).then_inc(m.s_high, 1)

        @block.vector
        def _(dve):
            dve.memset(m.v_wide[:, :, :, :], 0.0).then_inc(m.s_value, 1)
            dve.wait_ge(m.s_value, 1)
            v_wide = m.v_wide[:, :, :, :].rearrange("p t (g j) e -> p t g j e", j=4)
            dve.wait_ge(m.s_unit, 3)
            for j in range(4):
                cols = m.pair_bank[2][:, :].rearrange("p (t g n) -> p t g n", t=TT, g=4)[:, :, :, 8 * j:8 * j + 8]
                bias = m.b_row[:, 0, :].rearrange("p (g n) -> p g n", g=4)[:, :, 8 * j:8 * j + 8]
                dve.tensor_tensor(v_wide[:, :, :, j, 8 * j:8 * j + 8], cols,
                                  bias.unsqueeze(1).broadcast_to([P, TT, 4, 8]), ALU.add).then_inc(m.s_value, 1)
            for j in range(4):
                dve.memset(v_wide[:, :, :, j, 32 + 8 * j:40 + 8 * j], 1.0).then_inc(m.s_ones, 1)
            for i in (q, k):
                dve.wait_ge(m.s_qk, i + 1)
                dve.tensor_tensor(m.qk_square[i][:, :], m.qk[i][:, :], m.qk[i][:, :], ALU.mult).then_inc(m.s_square, 1)
            for i in (q, k):
                dve.wait_ge(m.s_norm_a, i + 1)
                dve.tensor_scalar(m.qk_norm[i][:, :], m.qk_norm[i][:, :], 1e-12, None, ALU.max).then_inc(m.s_norm_v, 1)
                dve.wait_ge(m.s_norm_v, 2 * i + 1)
                dve.reciprocal(m.qk_square[i][:, :], m.qk_norm[i][:, :]).then_inc(m.s_norm_v, 1)
                dve.wait_ge(m.s_norm_v, 2 * i + 2)
                if i == q:
                    dve.scalar_tensor_tensor(m.qk[i][:, :], m.qk[i][:, :], m.scale[:, 0:1], m.qk_square[i][:, :],
                                             ALU.mult, ALU.mult).then_inc(m.s_unit_length, 1)
                else:
                    dve.tensor_tensor(m.qk[i][:, :], m.qk[i][:, :], m.qk_square[i][:, :], ALU.mult).then_inc(m.s_unit_length, 1)
            for n in range(8):
                dve.wait_ge(m.s_high, n + 1)
                to = (m.q_stack if n < 4 else m.key_stack)[n % 4]
                parts = ((32, 64), (96, 128)) if n < 4 else ((64, 128),)
                for x, (a, b) in enumerate(parts):
                    dve.tensor_tensor(to[a:b, :], m.pair_bank[n % 2][a:b, :], to[a:b, :].bitcast(F32), ALU.subtract)\
                       .then_inc(m.s_low if x == len(parts) - 1 else m.s_low0, 1)
            dve.wait_ge(m.s_low, 8)
            dve.wait_ge(m.s_ones, 4)
    m.clear_semaphores()


def full_attention_steps():
    return [(gp, qc, j, 2 * kp, side) for gp in range(2) for qc in range(2) for j in range(4)
            for kp in range(TT // 2) for side in range(2)]


def full_attention_block(nc, m):
    steps = full_attention_steps()
    per_chunk = len(steps) // 4
    s_tile = m.pair_bank[0:3]
    heads_per_pair = AH // 2
    with nc.Block() as block:
        @block.vector
        def _(dve):
            def key_heads(gp):
                for j in range(4):
                    for side in range(2):
                        n = j * 2 + side
                        if gp:
                            dve.wait_ge(m.s_scores, per_chunk + (j + 1) * TT - 1 + side)
                        dve.tensor_scalar(m.key_head[n][:, :], m.key_stack[2 * gp + side][:, :].bitcast(F32),
                                          m.head_mask[:, j:j + 1], None, ALU.mult).then_inc(m.s_key_head, 1)

            def store(ch):
                gp, qc = divmod(ch, 2)
                o = m.bank[6 + ch % 2]
                dve.wait_ge(m.s_pv, (ch + 1) * per_chunk // 2)
                for side in range(2):
                    n = 2 * ch + side
                    if ch:
                        dve.wait_ge(m.s_stored, n - 1)
                    dve.reciprocal(m.recip_a[side][:, :], o[64 * side + 32:64 * side + 64, :]).then_inc(m.s_recip, 1)
                    dve.wait_ge(m.s_recip, n + 1)
                    g = 2 * gp + side
                    dve.tensor_tensor(m.mixedT[32 * g:32 * g + 32, qc * HALF:(qc + 1) * HALF], o[64 * side:64 * side + 32, :],
                                      m.recip_a[side][:, :], ALU.mult).then_inc(m.s_stored, 1)

            dve.tensor_tensor(m.total[:, :, :], m.total[:, :, :], m.b_row[:, 1, :].unsqueeze(1).broadcast_to([P, TT, C]),
                              ALU.add).then_inc(m.s_sum, 1)
            key_heads(0)
            store(0)
            key_heads(1)
            store(1)
            store(2)
            store(3)
            dve.wait_ge(m.s_sum, 1)
            dve.wait_ge(m.s_wo, 1)
            dve.tensor_tensor(m.total[:, :, :], m.pair_bank[0][:, :].rearrange("p (t c) -> p t c", c=C), m.total[:, :, :],
                              ALU.add).then_inc(m.s_sum, 1)
            dve.wait_ge(m.s_sum, 2)

        @block.scalar
        def _(act):
            for s, (gp, qc, j, kb, side) in enumerate(steps):
                head = 4 * (2 * gp + side) + j
                act.wait_ge(m.s_scores, s + 1)
                if s >= 4:
                    act.wait_ge(m.s_pv, (s - 4) // 2 + 1)
                act.activation(m.weights[s % 4][:, :, :], s_tile[s % 3][:, :].rearrange("p (k q) -> p k q", k=2),
                               ACT.Exp, bias=m.shift[:, head:head + 1]).then_inc(m.s_probs, 1)

        @block.tensor
        def _(pe):
            def score(s):
                gp, qc, j, kb, side = steps[s]
                n = j * 2 + side
                if kb == 0 and qc == 0:
                    pe.wait_ge(m.s_key_head, gp * heads_per_pair + n + 1)
                if s >= 3:
                    pe.wait_ge(m.s_probs, s - 2)
                for i in range(2):
                    mm = pe.matmul(s_tile[s % 3][:, i * HALF:(i + 1) * HALF], m.key_head[n][:, (kb + i) * P:(kb + i + 1) * P],
                                   m.q_stack[2 * gp + side][:, qc * HALF:(qc + 1) * HALF], start=True, stop=True)
                mm.then_inc(m.s_scores, 1)

            def mix(pair):
                gp, qc, j, kb, _ = steps[2 * pair]
                ch = 2 * gp + qc
                pe.wait_ge(m.s_probs, 2 * pair + 2)
                if j == 0 and kb == 0 and ch >= 2:
                    pe.wait_ge(m.s_stored, 2 * (ch - 1))
                for i in range(2):
                    for side in range(2):
                        head = 4 * (2 * gp + side) + j
                        mm = pe.matmul(m.bank[6 + ch % 2][64 * side:64 * side + 64, :], m.v_wide[:, kb + i, head, :],
                                       m.weights[(2 * pair + side) % 4][:, i, :],
                                       start=(j == 0 and kb + i == 0), stop=(j == 3 and kb + i == TT - 1))
                mm.then_inc(m.s_pv, 1)

            for pair in range(len(steps) // 2):
                score(2 * pair)
                score(2 * pair + 1)
                if pair:
                    mix(pair - 1)
            mix(len(steps) // 2 - 1)
            pe.wait_ge(m.s_stored, 8)
            pe.wait_ge(m.s_probs, len(steps))
            for tt in range(TT):
                mm = pe.matmul(m.pair_bank[0][:, tt * C:(tt + 1) * C], m.mixedT[:, tt * P:(tt + 1) * P], m.w_turned[:, 3, :],
                               start=True, stop=True)
            mm.then_inc(m.s_wo, 1)
    m.clear_semaphores()


def semaphores(m):
    m.s_load = m.sem("load")
    m.s_key_wide = m.sem("key_wide")
    m.s_decay = m.sem("decay")
    m.s_outer = m.sem("outer")
    m.s_read = m.sem("read")
    m.s_gathered = m.sem("gathered")
    m.s_state = m.sem("state")
    m.s_scale = m.sem("scale")
    m.s_square = m.sem("square")
    m.s_qk = m.sem("qk")
    m.s_sumsq = m.sem("sumsq")
    m.s_unit_length = m.sem("unit_length")
    m.s_stacked = m.sem("stacked")
    m.s_key_head = m.sem("key_head")
    m.s_load_wo = m.sem("load_wo")
    m.s_load_moe = m.sem("load_moe")
    m.s_set = m.sem("set")
    m.s_ones = m.sem("ones")
    m.s_norm_v = m.sem("norm_v")
    m.s_norm_a = m.sem("norm_a")
    m.s_turn_x = m.sem("turn_x")
    m.s_hT = m.sem("hT")
    m.s_maxrow = m.sem("maxrow")
    m.s_pv = m.sem("pv")
    m.s_raw = m.sem("raw")
    m.s_cos = m.sem("cos")
    m.s_sin0 = m.sem("sin0")
    m.s_sin = m.sem("sin")
    m.s_rotated = m.sem("rotated")
    m.s_high = m.sem("high")
    m.s_high0 = m.sem("high0")
    m.s_second = m.sem("second")
    m.s_taken = m.sem("taken")
    m.s_add_v = m.sem("add_v")
    m.s_add_p = m.sem("add_p")
    m.s_low0 = m.sem("low0")
    m.s_low = m.sem("low")
    m.s_value = m.sem("value")
    m.s_max = m.sem("max")
    m.s_rowmax = m.sem("rowmax")
    m.s_unit = m.sem("unit")
    m.s_probs = m.sem("probs")
    m.s_scores = m.sem("scores")
    m.s_masked = m.sem("masked")
    m.s_recip = m.sem("recip")
    m.s_logden = m.sem("logden")
    m.s_stored = m.sem("stored")
    m.s_wo = m.sem("wo")
    m.s_sum = m.sem("sum")
    m.s_router = m.sem("router")
    m.s_routed = m.sem("routed")
    m.s_pick = m.sem("pick")
    m.s_silu = m.sem("silu")
    m.s_gate = m.sem("gate")
    m.s_w_hi = m.sem("w_hi")
    m.s_w_lo = m.sem("w_lo")
    m.s_h_hi = m.sem("h_hi")
    m.s_h_lo = m.sem("h_lo")
    m.s_up = m.sem("up")
    m.s_gated = m.sem("gated")
    m.s_down_unit = m.sem("down_unit")
    m.s_weighed = m.sem("weighed")
    m.s_shift = [m.sem(f"shift{i}") for i in range(2)]
    m.s_scratch = [m.sem(f"scratch{i}") for i in range(2)]
    m.s_expert = [m.sem(f"expert{i}") for i in range(WRING)]


def input_block(nc, m, d, b):
    with nc.Block() as block:
        @block.sync
        def _(sp):
            sp.dma_start(m.total[:, :, :], d["x"][b].rearrange("(t p) c -> p t c", p=P)).then_inc(m.s_load, 16)
            sp.wait_ge(m.s_load, 16)

        @block.vector
        def _(dve):
            dve.wait_ge(m.s_load, 16)
            for tt in range(TT):
                dve.bn_stats(m.bn[:, tt, :], m.total[:, tt, :]).then_inc(m.s_norm_v, 1)
            dve.wait_ge(m.s_norm_v, TT)
            for tt in range(TT):
                dve.bn_aggr(m.moments[:, tt, 0:2], m.bn[:, tt, :]).then_inc(m.s_norm_v, 1)
            dve.wait_ge(m.s_norm_v, 2 * TT)
            dve.tensor_tensor(m.square[:, :, :], m.total[:, :, :], m.moments[:, :, 0:1].broadcast_to([P, TT, C]),
                              ALU.subtract).then_inc(m.s_norm_v, 1)
            dve.wait_ge(m.s_norm_a, 2)
            dve.wait_ge(m.s_norm_v, 2 * TT + 1)
            dve.tensor_tensor(m.x[:, :, :], m.square[:, :, :], m.moments[:, :, 2:3].broadcast_to([P, TT, C]),
                              ALU.mult).then_inc(m.s_norm_v, 1)
            dve.wait_ge(m.s_norm_v, 2 * TT + 2)

        @block.scalar
        def _(act):
            act.wait_ge(m.s_norm_v, 2 * TT)
            act.activation(m.moments[:, :, 3:4], m.moments[:, :, 1:2], ACT.Ln, bias=m.eps[:, 0:1]).then_inc(m.s_norm_a, 1)
            act.wait_ge(m.s_norm_a, 1)
            act.activation(m.moments[:, :, 2:3], m.moments[:, :, 3:4], ACT.Exp, scale=-0.5).then_inc(m.s_norm_a, 1)
            act.wait_ge(m.s_norm_a, 2)
    m.clear_semaphores()


def leave_block(nc, m, b):
    with nc.Block() as block:
        @block.sync
        def _(sp):
            sp.dma_start(m.sums[b].rearrange("(t p) c -> p t c", p=P), m.total[:, :, :]).then_inc(m.s_load, 16)
            sp.dma_start(m.normed[b].rearrange("(t p) c -> p t c", p=P), m.x[:, :, :]).then_inc(m.s_load, 16)
            sp.wait_ge(m.s_load, 32)
    m.clear_semaphores()


def decoder_input_block(nc, m):
    with nc.Block() as block:
        @block.sync
        def _(sp):
            for b in range(BATCH):
                sp.dma_start(m.x[:, b, :, :], m.normed[b].rearrange("(t p) c -> p t c", p=P)).then_inc(m.s_load, 16)
            sp.wait_ge(m.s_load, 16 * BATCH)
    m.clear_semaphores()


def output_block(nc, m, out):
    total = m.mixed[:, 0:2, :].rearrange("p b (t c) -> p b t c", c=C)
    with nc.Block() as block:
        @block.vector
        def _(dve):
            for b in range(BATCH):
                dve.wait_ge(m.s_shift[b], 16)
                dve.tensor_tensor(total[:, b, :, :], total[:, b, :, :], m.x[:, b, :, :], ALU.add).then_inc(m.s_sum, 1)

        @block.sync
        def _(sp):
            for b in range(BATCH):
                sp.dma_start(total[:, b, :, :], m.sums[b].rearrange("(t p) c -> p t c", p=P)).then_inc(m.s_shift[b], 16)
            for b in range(BATCH):
                sp.wait_ge(m.s_sum, b + 1)
                sp.dma_start(out[b].rearrange("(t p) c -> p t c", p=P), total[:, b, :, :]).then_inc(m.s_load, 16)
            sp.wait_ge(m.s_load, 16 * BATCH)
    m.clear_semaphores()


def build_program(nc, d, out):
    with ExitStack() as ctx:
        m = Core(nc, ctx)
        semaphores(m)
        m.sums, m.normed = (nc.dram_tensor(n, (BATCH, T, C), F32, kind="Internal").ap() for n in ("sums", "normed"))
        m.scratch = [nc.dram_tensor(f"maxima_turned{i}", (REP * TT, P), F32, kind="Internal").ap() for i in range(2)]
        banks = m.psum("banks", [P, 8, HALF])
        m.bank = [banks[:, i, :] for i in range(8)]
        m.pair_bank = [banks[:, 2 * i:2 * i + 2, :].rearrange("p k n -> p (k n)") for i in range(4)]
        m.gate_bank, m.up_bank = m.pair_bank[0:2]
        m.down_bank = [m.pair_bank[3], m.pair_bank[2]]
        m.ident, m.ident16 = m.sb("ident", [P, P]), m.sb("ident16", [P, P], BF16)
        m.later16 = m.sb("later16", [P, P], BF16)
        m.cos, m.sin = m.sb("cos", [P, TT, HD]), m.sb("sin", [P, TT, HD])
        m.eps = m.sb("eps", [P, 1])
        with ExitStack() as m.ctx:
            m.later = m.sb("later", [P, P])
            first_constants(nc, m, d)
        with nc.Fori(0, BATCH) as b:
            with ExitStack() as m.ctx:
                m.total, m.x, m.square = (m.sb(n, [P, TT, C]) for n in ("total", "branch_x", "branch_square"))
                m.bn, m.moments = m.sb("bn", [P, TT, 6]), m.sb("moments", [P, TT, 4])
                input_block(nc, m, d, b)
                branch_tensors(m)
                outer = m.ctx
                with ExitStack() as m.ctx:
                    recurrence_tensors(m)
                    recurrence_block(nc, m, d)
                m.ctx = outer
                attention_tensors(m)
                heads_block(nc, m)
                full_attention_block(nc, m)
                leave_block(nc, m, b)
        with ExitStack() as m.ctx:
            decoder_tensors(m)
            decoder_constants(nc, m)
            decoder_input_block(nc, m)
            with nc.Fori(0, LAYERS) as layer:
                attention_block(nc, m, d, layer)
                moe_block(nc, m, d, layer)
            output_block(nc, m, out)


def rotary_tables():
    inverse = (np.float32(1.0) / (np.float32(10000.0) ** (np.arange(0, HD, 2, dtype=np.float32) / np.float32(HD)))).astype(np.float32)
    angles = np.arange(T, dtype=np.float32)[:, None] * inverse
    cos, sin = np.cos(angles), np.sin(angles)
    return np.concatenate([cos, cos], axis=1), np.concatenate([-sin, sin], axis=1)


def branch_constants():
    row = np.arange(P)
    state = np.arange(STATES)
    column = state // (AD * AD) * AD + state % AD
    sum_rows = (column[:, None] == row).astype(np.float32).reshape(STATE_TILES, P, P)
    same_head = (row[:, None] // AD == row // AD).astype(np.float32)
    stacker = np.stack([(row[:, None] == 32 * g + row % 32).astype(np.float32) for g in range(4)])
    head_mask = (row[:, None] % 32 // AD == np.arange(4)).astype(np.float32)
    return {"sum_rows": sum_rows, "same_head": same_head, "stacker": stacker, "head_mask": head_mask}


def laid_out(given):
    state = np.arange(STATES)
    head, d, e = state // (AD * AD), state // AD % AD, state % AD
    rows = [("Wsk", "bsk", head * AD + d), ("Wg", "bg", head), ("Wsv", "bsv", head * AD + e), ("Wsq", "bsq", head * AD + d)]
    return {
        "w_wide": np.stack([np.ascontiguousarray(given[w][i].T) for w, _, i in rows]),
        "b_wide": np.stack([np.ascontiguousarray(given[b][i].reshape(STATE_TILES, P).T) for _, b, i in rows]),
        "w_turned": np.stack([np.ascontiguousarray(given[w].T) for w in ("Wq", "Wk", "Wv", "Wo")]),
        "b_col": np.stack([given["bq"], given["bk"]], axis=1),
        "b_row": np.stack([given["bv"], given["bo"]]),
        "temp_row": given["temp"].reshape(AH),
        "temp_col": np.repeat(given["temp"].reshape(AH), AD).reshape(P, 1),
    }


DECODER = ("ln1_w", "ln2_w", "wq", "wk", "wv", "wo", "wr", "wg", "wu", "wd")


def arrays_of(inputs):
    given = {name: np.ascontiguousarray(inputs[full]) for name, full in _INS.items()}
    cos, sin = rotary_tables()
    return {"x": given["x"], "cos": cos, "sin": sin, **{n: given[n] for n in DECODER}, **branch_constants(), **laid_out(given)}


_INS = {
    "x": "L0_attn_x", "Wsq": "L0_attn_Wsq", "bsq": "L0_attn_bsq", "Wsk": "L0_attn_Wsk", "bsk": "L0_attn_bsk",
    "Wsv": "L0_attn_Wsv", "bsv": "L0_attn_bsv", "Wg": "L0_attn_Wg", "bg": "L0_attn_bg", "Wq": "L0_attn_Wq",
    "bq": "L0_attn_bq", "Wk": "L0_attn_Wk", "bk": "L0_attn_bk", "Wv": "L0_attn_Wv", "bv": "L0_attn_bv",
    "Wo": "L0_attn_Wo", "bo": "L0_attn_bo", "temp": "L0_attn_temp", "ln1_w": "L0_ffn_ln1_w",
    "ln2_w": "L0_ffn_ln2_w", "wq": "L0_ffn_wq", "wk": "L0_ffn_wk", "wv": "L0_ffn_wv", "wo": "L0_ffn_wo",
    "wr": "L0_ffn_wr", "wg": "L0_ffn_wg", "wu": "L0_ffn_wu", "wd": "L0_ffn_wd",
}


def kernel(**inputs):
    import numpy as _np
    import concourse.bacc as _bacc
    from concourse import mybir as _mybir
    from concourse.bass_utils import run_bass_kernel_spmd as _run

    nc = _bacc.Bacc("TRN2", target_bir_lowering=False, num_devices=1)
    arrays, dram = {}, {}
    for name, a in arrays_of(inputs).items():
        a = _np.ascontiguousarray(a)
        arrays[f"in_{name}_dram"] = a
        dram[name] = nc.dram_tensor(f"in_{name}_dram", a.shape, _mybir.dt.from_np(a.dtype), kind="ExternalInput").ap()
    out = nc.dram_tensor("out_0_dram", (BATCH, T, C), _mybir.dt.float32, kind="ExternalOutput").ap()
    build_program(nc, dram, out)
    r = _run(nc, [arrays], core_ids=[0])
    return r.results[0]["out_0_dram"]
```

```python
import math
from contextlib import ExitStack

import numpy as np

import concourse.bass as bass
import concourse.mybir as mybir

F32 = mybir.dt.float32
F32R = mybir.dt.float32r
BF16 = mybir.dt.bfloat16
ALU = mybir.AluOpType
ACT = mybir.ActivationFunctionType
AX = mybir.AxisListType

P = 128
BATCH, T, C = 2, 1024, 128
TT = T // P
HALF = 512
QUARTER = T // 4
LAYERS = 4
NH, NKV, HD = 16, 4, 64
REP = NH // NKV
GW = REP * HD + 2 * HD
ROT = REP * HD + HD
FF, EXPERTS = 256, 8
FCH = FF // P
EPS = 1e-5
RAW = 4
WRING = 4
AH, AD = 16, 8
STATES = AH * AD * AD
STATE_TILES = STATES // P
STACKS, GATES = 7, 3
TALL = 80.0
LIMIT = 100.0
FAR = -1e9
MROW = 64
KROWS = 96



GROUPS = BATCH * NKV


def attention_steps():
    return [(g, pair, qc, kt) for g in range(GROUPS) for pair in range(REP // 2) for qc in range(2)
            for kt in range(4 * (qc + 1))]


STEPS = attention_steps()
STEPS_PER_GROUP = len(STEPS) // GROUPS
CHUNK_END = [s for s, (_, _, qc, kt) in enumerate(STEPS) if kt == 4 * qc + 3]
CHUNKS = len(CHUNK_END)
BATCH_CHUNKS = CHUNKS // BATCH
MIX_LAG = 2
ADD_LAG = 2
DEN_LAG = ADD_LAG + 1
OUTPUT_STEP = len(STEPS) // BATCH + DEN_LAG
PROBS = 4
ALL_STEPS = len(STEPS) + DEN_LAG + 1


def is_diagonal(s):
    _, _, qc, kt = STEPS[s]
    return kt >= 4 * qc


def first_query(s):
    _, _, qc, kt = STEPS[s]
    return max(0, kt - 4 * qc) * P


def first_score(s):
    return min(first_query(s), HALF // 2)


def masks_until(s):
    return sum(is_diagonal(k) for k in range(s + 1))


def adds_until(s):
    return sum(STEPS[k][3] > 0 for k in range(s + 1))


def chunk_of(s):
    return sum(e < s for e in CHUNK_END)


def preparation_units(g, pair):
    def coarse(j, qbs):
        for qb in qbs:
            keys = (qb + 1) * P
            yield ("coarse", g, j, qb, 0, min(keys, HALF))
            if keys > HALF:
                yield ("coarse", g, j, qb, HALF, keys - HALF)

    def turns(quarters):
        return [("turn", g, 2 * pair, quarter) for quarter in quarters]

    early, late = range(TT // 2), range(TT // 2, TT)
    scores = [*coarse(2 * pair, early), *coarse(2 * pair + 1, early), *coarse(2 * pair, late), *coarse(2 * pair + 1, late)]
    if pair == 0:
        units = [("project", g, tt) for tt in range(TT)]
        units.insert(TT, ("turn", g, REP, 0))
        units += turns(range(2))
        for place, unit in zip((3,5,7), [("turn", g, REP, 1)] + turns((2, 3))):
            scores.insert(place, unit)
    else:
        units = turns(range(2))
        for place, unit in zip((5,7), turns((2, 3))):
            scores.insert(place, unit)
    return units + scores


PARTS = 3
UNIT_WEIGHT = {"norm": 1.5, "maxima": 0.5, "project": 1.0, "turn": 2.0, "coarse": 0.8}
WINDOWS = ((-18, -4), (-4, 6))


def schedule():
    first = preparation_units(0, 0) + [("maxima", 0, 0)]
    at = [[[] for _ in range(PARTS)] for _ in range(ALL_STEPS)]
    for g in range(GROUPS):
        for pair, (begin, end) in enumerate(WINDOWS):
            if g == 0 and pair == 0:
                continue
            units = preparation_units(g, pair)
            if g == NKV and pair == 0:
                units = [("norm", g, half) for half in range(2)] + units
            if (g, pair) != (0, 1):
                units.insert(1, ("maxima", g - 1 + pair, 1 - pair))
            start = g * STEPS_PER_GROUP
            slots = [(s, part) for s in range(max(start + begin, 0), start + end) for part in range(PARTS)]
            spans = [2 * (HALF - first_query(max(s - MIX_LAG, 0))) if part == 2 else HALF - first_score(s) for s, part in slots]
            scale = sum(UNIT_WEIGHT[u[0]] for u in units) / sum(spans)
            have, want = 0.0, 0.0
            for (s, part), span in zip(slots, spans):
                want += span * scale
                while units and have + UNIT_WEIGHT[units[0][0]] / 2 <= want:
                    have += UNIT_WEIGHT[units[0][0]]
                    at[s][part].append(units.pop(0))
            at[slots[-1][0]][-1] += units
    at[start + WINDOWS[1][1]][0].append(("maxima", GROUPS - 1, 1))
    for ch, s in enumerate(CHUNK_END):
        at[s + DEN_LAG][-1].append(("denominators", STEPS[s][0], ch))
    for half in range(2):
        at[OUTPUT_STEP + half][-1].append(("output", NKV - 1, half))
    return first, at


FIRST_UNITS, UNITS_AT = schedule()
UNITS = FIRST_UNITS + [u for parts in UNITS_AT for units in parts for u in units]
ALL_BANKS = (6, 7, 5, 2, 3, 4, 0, 1)
UNIT_BANKS = ALL_BANKS[0:3]


def units_at(s, part=None):
    start = len(FIRST_UNITS) + sum(len(units) for parts in UNITS_AT[:s] for units in parts)
    ends = [start]
    for units in UNITS_AT[s]:
        ends.append(ends[-1] + len(units))
    return range(ends[0], ends[-1]) if part is None else range(ends[part], ends[part + 1])


def bank_of(n):
    return ALL_BANKS[n % 8] if n < len(FIRST_UNITS) else UNIT_BANKS[n % 3]


def user_before(n):
    return next((k for k in range(n - 1, max(-1, n - 17), -1) if bank_of(k) == bank_of(n)), None)


def ordinal(kind, n):
    return sum(u[0] == kind for u in UNITS[:n + 1])


def turned(g, j, qb):
    return ordinal("turn", UNITS.index(("turn", g, j // 2 * 2, qb // 2) if j < REP else ("turn", g, REP, qb // 4)))


def mixed_of(m, ch):
    g, pair, qc, _ = STEPS[CHUNK_END[ch]]
    return m.mixed[:, g % NKV * REP // 2 + pair, qc * HALF:(qc + 1) * HALF]


class Core:

    def __init__(self, nc, ctx):
        self.nc, self.ctx = nc, ctx
        self.sems = []

    def sb(self, name, shape, dt=F32):
        return self.ctx.enter_context(self.nc.sbuf_tensor(name, shape, dt))

    def psum(self, name, shape, dt=F32):
        return self.ctx.enter_context(self.nc.psum_tensor(name, shape, dt))

    def sem(self, name):
        s = self.ctx.enter_context(self.nc.semaphore(name))
        self.sems.append(s)
        return s

    def clear_semaphores(self):
        numbers = [s.num for s in self.sems]
        self.nc.sync.sem_clear(range(min(numbers), max(numbers) + 1))
        self.nc.all_engine_barrier()


def first_constants(nc, m, d):
    with nc.Block() as block:
        @block.sync
        def _(sp):
            sp.dma_start(m.cos[:, :, :], d["cos"].rearrange("(t p) f -> p t f", p=P)).then_inc(m.s_load, 16)
            sp.dma_start(m.sin[:, :, :], d["sin"].rearrange("(t p) f -> p t f", p=P)).then_inc(m.s_load, 16)
            sp.wait_ge(m.s_load, 32)

        @block.gpsimd
        def _(pool):
            pool.memset(m.ident[:, :], 0.0).then_inc(m.s_set, 1)
            pool.memset(m.later[:, :], 0.0).then_inc(m.s_set, 1)
            pool.wait_ge(m.s_set, 2)
            pool.affine_select(out=m.ident[:, :], in_=m.ident[:, :], compare_op=ALU.not_equal, fill=1.0, base=0,
                               pattern=[[-1, P]], channel_multiplier=1).then_inc(m.s_set, 1)
            pool.affine_select(out=m.later[:, :], in_=m.later[:, :], compare_op=ALU.is_ge, fill=FAR, base=0,
                               pattern=[[-1, P]], channel_multiplier=1).then_inc(m.s_set, 1)
            pool.wait_ge(m.s_set, 4)
            pool.tensor_copy(m.ident16[:, :], m.ident[:, :]).then_inc(m.s_set, 1)
            pool.tensor_copy(m.later16[:, :], m.later[:, :]).then_inc(m.s_set, 1)
            pool.wait_ge(m.s_set, 6)

        @block.vector
        def _(dve):
            dve.memset(m.eps[:, :], EPS).then_inc(m.s_ones, 1)
            dve.wait_ge(m.s_ones, 1)
    m.clear_semaphores()


def decoder_start_block(nc, m):
    with nc.Block() as block:
        @block.sync
        def _(sp):
            for b in range(BATCH):
                sp.dma_start(m.x[:, b, :, :], m.normed[b].rearrange("(t p) c -> p t c", p=P)).then_inc(m.s_load, 16)
            sp.wait_ge(m.s_load, 16 * BATCH)

        @block.gpsimd
        def _(pool):
            pool.memset(m.q_shift[0][MROW:KROWS, :, :].bitcast(F32), 0.0).then_inc(m.s_set, 1)
            pool.wait_ge(m.s_set, 1)

        @block.vector
        def _(dve):
            dve.memset(m.ones[:, :], 1.0).then_inc(m.s_ones, 1)
            dve.memset(m.q_shift[1][MROW:KROWS, :, :].bitcast(F32), 0.0).then_inc(m.s_ones, 1)
            for k in m.k_rest:
                dve.memset(k[MROW:KROWS, :].bitcast(F32), 0.0).then_inc(m.s_ones, 1)
            dve.wait_ge(m.s_ones, 4)
            for k in m.k_rest:
                dve.memset(k[MROW:MROW + 1, :].bitcast(F32), 1.0).then_inc(m.s_ones, 1)
            for e in range(EXPERTS):
                dve.memset(m.expert_no[:, :, e:e + 1], float(e)).then_inc(m.s_ones, 1)
            dve.wait_ge(m.s_ones, 6 + EXPERTS)
    m.clear_semaphores()


def load_expert(sp, m, d, layer, e):
    i = e % WRING
    sp.dma_start(m.wgu[:, i, 0:FF], d["wg"][layer, e]).then_inc(m.s_expert[i], 16)
    sp.dma_start(m.wgu[:, i, FF:2 * FF], d["wu"][layer, e]).then_inc(m.s_expert[i], 16)
    sp.dma_start(m.wd[:, i, :, :], d["wd"][layer, e].rearrange("(j p) c -> p j c", p=P)).then_inc(m.s_expert[i], 16)


def attention_block(nc, m, d, layer):
    scores, heads = m.pair_bank, m.bank[4]
    with nc.Block() as block:
        @block.sync
        def _(sp):
            sp.dma_start(m.ln1[:, :], d["ln1_w"][layer].rearrange("(c o) -> c o", o=1)).then_inc(m.s_load, 16)
            sp.dma_start(m.wqkv[:, :, 0:REP * HD], d["wq"][layer].rearrange("c (g n) -> c g n", g=NKV)).then_inc(m.s_load, 16)
            sp.dma_start(m.wqkv[:, :, REP * HD:ROT], d["wk"][layer].rearrange("c (g n) -> c g n", g=NKV)).then_inc(m.s_load, 16)
            sp.dma_start(m.wqkv[:, :, ROT:GW], d["wv"][layer].rearrange("c (g n) -> c g n", g=NKV)).then_inc(m.s_load, 16)
            sp.dma_start(m.wo[:, :, :], d["wo"][layer].rearrange("(j p) c -> p j c", p=P)).then_inc(m.s_load_wo, 16)
            sp.dma_start(m.ln2[:, :], d["ln2_w"][layer].rearrange("(c o) -> c o", o=1)).then_inc(m.s_load_moe, 16)
            sp.dma_start(m.wr[:, :], d["wr"][layer]).then_inc(m.s_load_moe, 16)
            for e in range(WRING):
                load_expert(sp, m, d, layer, e)
            for x in range(2 * GROUPS):
                g, pair = divmod(x, 2)
                sp.wait_ge(m.s_maxrow, x + 1)
                sp.dma_start(m.scratch[pair], m.maxrow[pair][:, :].bitcast(F32)).then_inc(m.s_scratch[pair], 16)
                sp.wait_ge(m.s_scratch[pair], 16 * (g + 1))
                if g >= 2:
                    sp.wait_ge(m.s_pv, (g - 1) * STEPS_PER_GROUP)
                sp.dma_start(m.q_shift[g % 2][MROW:MROW + 1, 2 * pair:2 * pair + 2, :]
                             .rearrange("o h (b c) -> o (h b) c", c=P).bitcast(F32),
                             m.scratch[pair].unsqueeze(0)).then_inc(m.s_shift[pair], 16)
            sp.wait_ge(m.s_load_moe, 2 * 16)
            for e in range(WRING):
                sp.wait_ge(m.s_expert[e], 3 * 16)

        @block.vector
        def _(dve):
            def squares(b, to):
                dve.tensor_tensor(to, m.x[:, b, :, :], m.x[:, b, :, :], ALU.mult).then_inc(m.s_norm_v, 1)
                dve.wait_ge(m.s_norm_v, 3 * b + 1)
                dve.reduce_sum(m.stat[:, 0, b, :], to, AX.X).then_inc(m.s_norm_v, 1)

            def normal(b):
                dve.wait_ge(m.s_norm_a, 2 * (b + 1))
                dve.tensor_tensor(m.square[:, :, :], m.x[:, b, :, :], m.stat[:, 2, b, :].unsqueeze(2).broadcast_to([P, TT, P]),
                                  ALU.mult).then_inc(m.s_norm_v, 1)

            squares(0, m.square[:, :, :])
            normal(0)
            squares(1, m.mixed[:, 0, :].rearrange("p (t c) -> p t c", c=C))
            dve.wait_ge(m.s_norm_v, 5)

            def unit(n):
                kind, g = UNITS[n][0:2]
                buf = g % 2
                if kind == "project":
                    tt = UNITS[n][2]
                    if tt % 2 == 0:
                        return
                    dve.wait_ge(m.s_raw, g * TT + tt + 1)
                    a = slice(tt - 1, tt + 1)
                    r = slice((tt - 1) % RAW, (tt - 1) % RAW + 2)
                    dve.tensor_tensor(m.rotated[:, a, :, :], m.raw[:, r, :, :],
                                      m.cos[:, a, :].unsqueeze(2).broadcast_to([P, 2, REP + 1, HD]),
                                      ALU.mult).then_inc(m.s_cos, 1)
                    i = g * TT // 2 + tt // 2 + 1
                    dve.wait_ge(m.s_sin, i)
                    dve.wait_ge(m.s_cos, i)
                    dve.tensor_tensor(m.rotated[:, a, :, :], m.rotated[:, a, :, :], m.swapped[:, r, :, :],
                                      ALU.add).then_inc(m.s_rotated, 1)
                elif kind == "turn":
                    j, at = UNITS[n][2:4]
                    dve.wait_ge(m.s_high, ordinal("turn", n))
                    if j == REP:
                        cols = slice(at * HALF, (at + 1) * HALF)
                        dve.tensor_tensor(m.k_rest[buf][0:HD, cols], m.bank[bank_of(n)][0:HD, :],
                                          m.k_twice[buf][0:HD, cols].bitcast(F32), ALU.subtract).then_inc(m.s_low, 1)
                    else:
                        cols = slice(at * QUARTER, (at + 1) * QUARTER)
                        dve.tensor_tensor(m.q_full[buf][HD:P, j:j + 2, cols],
                                          m.bank[bank_of(n)][0:HD, :].rearrange("p (h t) -> p h t", h=2),
                                          m.q_full[buf][0:HD, j:j + 2, cols].bitcast(F32), ALU.subtract).then_inc(m.s_low, 1)
                elif kind == "coarse":
                    j, qb, k0, keys = UNITS[n][2:6]
                    dve.wait_ge(m.s_unit, n + 1)
                    if g >= 2 and j % 2 == 0 and qb == 0 and k0 == 0:
                        dve.wait_ge(m.s_maxrow, 2 * (g - 2) + j // 2 + 1)
                    to = m.maxima if k0 == 0 else m.maxima2
                    dve.reduce_max(to[buf][:, j, qb:qb + 1], m.bank[bank_of(n)][:, 0:keys], AX.X).then_inc(m.s_max, 1)
                    if j % 2 and k0 + keys == T:
                        dve.wait_ge(m.s_max, ordinal("coarse", n))
                        long = m.maxima[buf][:, j - 1:j + 1, TT // 2:TT]
                        dve.tensor_tensor(long, long, m.maxima2[buf][:, j - 1:j + 1, TT // 2:TT], ALU.max).then_inc(m.s_rowmax, 1)
                elif kind == "norm":
                    if UNITS[n][2] == 0:
                        normal(1)
                elif kind == "output":
                    dve.wait_ge(m.s_unit, n + 1)
                    a = slice(UNITS[n][2] * TT // 2, (UNITS[n][2] + 1) * TT // 2)
                    dve.tensor_tensor(m.x[:, 0, a, :], m.bank[bank_of(n)][:, :].rearrange("p (t c) -> p t c", c=C),
                                      m.x[:, 0, a, :], ALU.add).then_inc(m.s_sum, 1)

            def add(s):
                ch = chunk_of(s)
                dve.wait_ge(m.s_masked if is_diagonal(s) else m.s_probs, masks_until(s) if is_diagonal(s) else s + 1)
                dve.wait_ge(m.s_pv, s - STEPS[s][3] + 1)
                if STEPS[s][3] > 1:
                    dve.wait_ge(m.s_add_v, adds_until(s - 1))
                to = m.prob_sum[ch % 2][:, 0, first_query(s):]
                dve.tensor_tensor(to, to, m.probs[s % PROBS][:, 0, first_query(s):], ALU.add).then_inc(m.s_add_v, 1)

            for n in range(len(FIRST_UNITS)):
                unit(n)
            for s in range(ALL_STEPS):
                if 0 <= s - ADD_LAG < len(STEPS) and STEPS[s - ADD_LAG][3] > 0:
                    add(s - ADD_LAG)
                for n in units_at(s):
                    unit(n)
            for i in range(2):
                dve.wait_ge(m.s_wo, i + 1)
                a = slice(i * TT // 2, (i + 1) * TT // 2)
                dve.tensor_tensor(m.x[:, 1, a, :], m.bank[i][:, :].rearrange("p (t c) -> p t c", c=C), m.x[:, 1, a, :],
                                  ALU.add).then_inc(m.s_sum, 1)
            dve.wait_ge(m.s_sum, 4)
            dve.tensor_scalar(m.x[:, :, :, :], m.x[:, :, :, :], -LIMIT, LIMIT, ALU.max, ALU.min).then_inc(m.s_sum, 1)
            dve.wait_ge(m.s_sum, 5)

        @block.gpsimd
        def _(pool):
            def swap(n):
                kind, g, tt = UNITS[n][0:3]
                if tt % 2 == 0:
                    return
                a = slice(tt - 1, tt + 1)
                r = slice((tt - 1) % RAW, (tt - 1) % RAW + 2)
                i = g * TT // 2 + tt // 2
                pool.wait_ge(m.s_raw, g * TT + tt + 1)
                if i >= RAW // 2:
                    pool.wait_ge(m.s_rotated, i + 1 - RAW // 2)
                for f in range(2):
                    pool.tensor_tensor(m.swapped[:, r, :, f * 32:f * 32 + 32], m.raw[:, r, :, 32 - f * 32:64 - f * 32],
                                       m.sin[:, a, f * 32:f * 32 + 32].unsqueeze(2).broadcast_to([P, 2, REP + 1, 32]),
                                       ALU.mult).then_inc(m.s_sin if f else m.s_sin0, 1)

            def mask(s):
                ch, q0 = chunk_of(s), first_query(s)
                pool.wait_ge(m.s_probs, s + 1)
                v = (m.probs[s % PROBS] if STEPS[s][3] else m.prob_sum[ch % 2])[:, :, q0:q0 + P]
                pool.affine_select(out=v, in_=v, compare_op=ALU.is_ge, fill=0.0, base=0, pattern=[[0, 2], [1, P]],
                                   channel_multiplier=-1).then_inc(m.s_masked, 1)

            def add(s):
                ch = chunk_of(s)
                pool.wait_ge(m.s_masked if is_diagonal(s) else m.s_probs, masks_until(s) if is_diagonal(s) else s + 1)
                pool.wait_ge(m.s_pv, s - STEPS[s][3] + 1)
                if STEPS[s][3] > 1:
                    pool.wait_ge(m.s_add_p, adds_until(s - 1))
                to = m.prob_sum[ch % 2][:, 1, first_query(s):]
                pool.tensor_tensor(to, to, m.probs[s % PROBS][:, 1, first_query(s):], ALU.add).then_inc(m.s_add_p, 1)

            def store(ch):
                pool.wait_ge(m.s_recip, ch + 1)
                pool.wait_ge(m.s_taken, ch + 1)
                to = mixed_of(m, ch)
                pool.tensor_tensor(to, to, m.recip[:, :], ALU.mult).then_inc(m.s_stored, 1)

            def unit(n):
                if UNITS[n][0] == "project":
                    swap(n)
                if UNITS[n][0] == "denominators":
                    store(UNITS[n][2])

            for n in range(len(FIRST_UNITS)):
                unit(n)
            for s in range(ALL_STEPS):
                if s < len(STEPS) and is_diagonal(s):
                    mask(s)
                for n in units_at(s):
                    unit(n)
                if 0 <= s - ADD_LAG < len(STEPS) and STEPS[s - ADD_LAG][3] > 0:
                    add(s - ADD_LAG)

        @block.scalar
        def _(act):
            act.preload_act_table_set("natural_log_exp_and_others")
            def root(b):
                act.wait_ge(m.s_norm_v, 3 * b + 2)
                act.activation(m.stat[:, 1, b, :], m.stat[:, 0, b, :], ACT.Ln, bias=m.eps[:, 0:1], scale=1.0 / C).then_inc(m.s_norm_a, 1)
                act.wait_ge(m.s_norm_a, 2 * b + 1)
                act.activation(m.stat[:, 2, b, :], m.stat[:, 1, b, :], ACT.Exp, scale=-0.5).then_inc(m.s_norm_a, 1)

            root(0)
            act.wait_ge(m.s_load, 4 * 16)
            for i in range(2):
                act.wait_ge(m.s_turn_x, i + 1)
                act.mul(m.hT[:, i * HALF:(i + 1) * HALF], m.bank[i][:, :], m.ln1[:, 0:1]).then_inc(m.s_hT, 1)
            root(1)

            def unit(n):
                kind, g = UNITS[n][0:2]
                buf = g % 2
                if kind == "project":
                    tt = UNITS[n][2]
                    act.wait_ge(m.s_unit, n + 1)
                    if g >= 2:
                        act.wait_ge(m.s_pv, (g - 1) * STEPS_PER_GROUP)
                    act.copy(m.values[buf][:, tt, :], m.bank[bank_of(n)][:, ROT:GW]).then_inc(m.s_value, 1)
                    before = (g * TT + tt - RAW) // 2 + 1
                    if before > 0:
                        act.wait_ge(m.s_cos, before)
                        act.wait_ge(m.s_sin, before)
                    act.copy(m.raw[:, tt % RAW, :, :], m.bank[bank_of(n)][:, 0:ROT].rearrange("p (h e) -> p h e", e=HD)).then_inc(m.s_raw, 1)
                elif kind == "turn":
                    j, at = UNITS[n][2:4]
                    act.wait_ge(m.s_unit, n + 1)
                    if g >= 2:
                        act.wait_ge(m.s_pv, (g - 1) * STEPS_PER_GROUP)
                    if j == REP:
                        cols = slice(at * HALF, (at + 1) * HALF)
                        act.copy(m.k_twice[buf][0:HD, cols], m.bank[bank_of(n)][0:HD, :]).then_inc(m.s_high, 1)
                        act.wait_ge(m.s_high, ordinal("turn", n))
                        act.copy(m.k_twice[buf][HD:P, cols], m.k_twice[buf][0:HD, cols]).then_inc(m.s_second, 1)
                    else:
                        cols = slice(at * QUARTER, (at + 1) * QUARTER)
                        act.copy(m.q_full[buf][0:HD, j:j + 2, cols],
                                 m.bank[bank_of(n)][0:HD, :].rearrange("p (h t) -> p h t", h=2)).then_inc(m.s_high, 1)
                        act.wait_ge(m.s_high, ordinal("turn", n))
                        act.copy(m.q_shift[buf][0:HD, j:j + 2, cols], m.q_full[buf][0:HD, j:j + 2, cols]).then_inc(m.s_second, 1)
                elif kind == "denominators":
                    ch = UNITS[n][2]
                    act.wait_ge(m.s_unit, n + 1)
                    if ch:
                        act.wait_ge(m.s_stored, ch)
                    act.activation(m.recip[:, :], m.bank[bank_of(n)][:, :], ACT.Ln).then_inc(m.s_logden, 1)
                    act.wait_ge(m.s_logden, ch + 1)
                    act.activation(m.recip[:, :], m.recip[:, :], ACT.Exp, scale=-1.0).then_inc(m.s_recip, 1)
                elif kind == "norm":
                    half = UNITS[n][2]
                    act.wait_ge(m.s_unit, n + 1)
                    act.mul(m.hT[:, half * HALF:(half + 1) * HALF], m.bank[bank_of(n)][:, :], m.ln1[:, 0:1]).then_inc(m.s_hT, 1)
                elif kind == "maxima":
                    act.wait_ge(m.s_unit, n + 1)
                    pair = UNITS[n][2]
                    if g:
                        act.wait_ge(m.s_shift[pair], 16 * g)
                    act.mul(m.maxrow[pair][:, :], m.bank[bank_of(n)][0:2 * TT, 0:P], -1.0).then_inc(m.s_maxrow, 1)

            def take(ch):
                act.wait_ge(m.s_pv, CHUNK_END[ch] + 1)
                if ch == BATCH_CHUNKS:
                    act.wait_ge(m.s_sum, 2)
                act.copy(mixed_of(m, ch), heads[:, :]).then_inc(m.s_taken, 1)

            def exponentials(s):
                ch, q0 = chunk_of(s), first_score(s)
                act.wait_ge(m.s_scores, s + 1)
                if STEPS[s][3] == 0:
                    to = m.prob_sum[ch % 2]
                    if ch >= 2:
                        act.wait_ge(m.s_unit, UNITS.index(("denominators", STEPS[CHUNK_END[ch - 2]][0], ch - 2)) + 1)
                else:
                    to = m.probs[s % PROBS]
                    if s >= PROBS:
                        act.wait_ge(m.s_pv, s - PROBS + 1)
                        act.wait_ge(m.s_add_v, adds_until(s - PROBS))
                        act.wait_ge(m.s_add_p, adds_until(s - PROBS))
                act.activation(to[:, :, q0:HALF], scores[s % 2][:, :].rearrange("p (k q) -> p k q", k=2)[:, :, q0:HALF],
                               ACT.Exp, scale=1.0 / math.sqrt(HD)).then_inc(m.s_probs, 1)

            for n in range(len(FIRST_UNITS)):
                unit(n)
            for s in range(ALL_STEPS):
                if s < len(STEPS):
                    exponentials(s)
                for n in units_at(s):
                    unit(n)
                if s - MIX_LAG in CHUNK_END:
                    take(CHUNK_END.index(s - MIX_LAG))

        @block.tensor
        def _(pe):
            pe.wait_ge(m.s_norm_v, 3)
            for tt in range(TT):
                mm = pe.transpose(m.bank[tt // 4][:, (tt % 4) * P:(tt % 4 + 1) * P], m.square[:, tt, :], m.ident[:, :])
                if tt % 4 == 3:
                    mm.then_inc(m.s_turn_x, 1)

            def released(n):
                kind = UNITS[n][0]
                if kind == "norm":
                    pe.wait_ge(m.s_hT, 2 + ordinal(kind, n))
                else:
                    sem = {"project": m.s_raw, "turn": m.s_low, "coarse": m.s_max, "maxima": m.s_maxrow, "output": m.s_sum,
                           "denominators": m.s_logden}[kind]
                    pe.wait_ge(sem, ordinal(kind, n))

            def output(to, b, tt):
                for j in range(NH // 2):
                    mm = pe.matmul(to[:, (tt % 4) * C:(tt % 4 + 1) * C], m.mixed[:, j, tt * P:(tt + 1) * P],
                                   m.wo[:, j, :], start=(j == 0), stop=(j == NH // 2 - 1))
                return mm

            def unit(n):
                kind, g = UNITS[n][0:2]
                buf, to, before = g % 2, m.bank[bank_of(n)], user_before(n)
                if before is not None:
                    released(before)
                if kind == "project":
                    tt = UNITS[n][2]
                    if g % NKV == 0:
                        pe.wait_ge(m.s_hT, 2 * (g // NKV) + tt // 4 + 1)
                    mm = pe.matmul(to[:, 0:GW], m.hT[:, tt * P:(tt + 1) * P], m.wqkv[:, g % NKV, :], start=True, stop=True)
                    mm.then_inc(m.s_unit, 1)
                elif kind == "turn":
                    j, at = UNITS[n][2:4]
                    if j == REP:
                        pe.wait_ge(m.s_rotated, (g * TT + at * 4) // 2 + 2)
                        for i in range(4):
                            mm = pe.transpose(to[0:HD, i * P:(i + 1) * P], m.rotated[:, at * 4 + i, REP, :], m.ident[:, :])
                    else:
                        pe.wait_ge(m.s_rotated, g * TT // 2 + at + 1)
                        for i in range(2):
                            for k in range(2):
                                mm = pe.transpose(to[0:HD, (2 * i + k) * P:(2 * i + k + 1) * P],
                                                  m.rotated[:, at * 2 + k, j + i, :], m.ident[:, :])
                    mm.then_inc(m.s_unit, 1)
                elif kind == "coarse":
                    j, qb, k0, keys = UNITS[n][2:6]
                    if k0 == 0:
                        pe.wait_ge(m.s_low, max(turned(g, REP, qb), turned(g, j, qb)))
                        pe.wait_ge(m.s_second, turned(g, REP, qb))
                    diagonal = k0 + keys == (qb + 1) * P
                    mm = pe.matmul(to[:, 0:keys], m.q_full[buf][:, j, qb * P:(qb + 1) * P], m.k_twice[buf][:, k0:k0 + keys],
                                   start=True, stop=not diagonal)
                    if diagonal:
                        mm = pe.matmul(to[:, keys - P:keys], m.ident16[:, :], m.later16[:, :], start=False, stop=True)
                    mm.then_inc(m.s_unit, 1)
                elif kind == "norm":
                    half = UNITS[n][2]
                    pe.wait_ge(m.s_norm_v, 6)
                    for i in range(4):
                        mm = pe.transpose(to[:, i * P:(i + 1) * P], m.square[:, half * 4 + i, :], m.ident[:, :])
                    mm.then_inc(m.s_unit, 1)
                elif kind == "output":
                    pe.wait_ge(m.s_load_wo, 16)
                    pe.wait_ge(m.s_stored, BATCH_CHUNKS)
                    for tt in range(UNITS[n][2] * TT // 2, (UNITS[n][2] + 1) * TT // 2):
                        mm = output(to, 0, tt)
                    mm.then_inc(m.s_unit, 1)
                elif kind == "denominators":
                    ch = UNITS[n][2]
                    pe.wait_ge(m.s_add_v, adds_until(CHUNK_END[ch]))
                    pe.wait_ge(m.s_add_p, adds_until(CHUNK_END[ch]))
                    for i in range(2):
                        mm = pe.matmul(to[i * HD:(i + 1) * HD, :], m.ones[:, :], m.prob_sum[ch % 2][:, i, :], start=True, stop=True)
                    mm.then_inc(m.s_unit, 1)
                else:
                    pair = UNITS[n][2]
                    pe.wait_ge(m.s_rowmax, 2 * g + pair + 1)
                    mm = pe.transpose(to[0:2 * TT, 0:P], m.maxima[buf][:, 2 * pair:2 * pair + 2, :], m.ident[:, :])
                    mm.then_inc(m.s_unit, 1)

            def score(s, i):
                g, pair, qc, kt = STEPS[s]
                buf, q0 = g % 2, first_score(s)
                if qc == 0 and kt == 0 and i == 0:
                    prepared = max(turned(g, REP, TT - 1), turned(g, 2 * pair, TT - 1))
                    pe.wait_ge(m.s_low, prepared)
                    pe.wait_ge(m.s_second, prepared)
                    pe.wait_ge(m.s_value, TT * (g + 1))
                    pe.wait_ge(m.s_shift[pair], 16 * (g + 1))
                if s >= 2 and i == 0:
                    pe.wait_ge(m.s_probs, s - 1)
                cols = slice(qc * HALF + q0, (qc + 1) * HALF)
                keys = slice(kt * P, (kt + 1) * P)
                to = scores[s % 2][:, i * HALF + q0:(i + 1) * HALF]
                pe.matmul(to, m.k_twice[buf][:, keys], m.q_full[buf][:, 2 * pair + i, cols], start=True, stop=False)
                mm = pe.matmul(to, m.k_rest[buf][:, keys], m.q_shift[buf][:, 2 * pair + i, cols], start=False, stop=True)
                if i == 1:
                    mm.then_inc(m.s_scores, 1)

            def mix(s):
                g, pair, qc, kt = STEPS[s]
                ch, q0 = chunk_of(s), first_query(s)
                if is_diagonal(s):
                    pe.wait_ge(m.s_masked, masks_until(s))
                else:
                    pe.wait_ge(m.s_probs, s + 1)
                if kt == 0 and ch:
                    pe.wait_ge(m.s_taken, ch)
                probs = m.probs[s % PROBS] if kt else m.prob_sum[ch % 2]
                for i in range(2):
                    mm = pe.matmul(heads[i * HD:(i + 1) * HD, q0:HALF], m.values[g % 2][:, kt, :], probs[:, i, q0:HALF],
                                   start=(kt == 0), stop=(s == CHUNK_END[ch]))
                mm.then_inc(m.s_pv, 1)

            for n in range(len(FIRST_UNITS)):
                unit(n)
            for s in range(ALL_STEPS):
                for part in range(PARTS):
                    if part < 2 and s < len(STEPS):
                        score(s, part)
                    if part == 2 and 0 <= s - MIX_LAG < len(STEPS):
                        mix(s - MIX_LAG)
                    for n in units_at(s, part):
                        unit(n)

            pe.wait_ge(m.s_stored, CHUNKS)
            pe.wait_ge(m.s_probs, len(STEPS))
            for tt in range(TT):
                mm = output(m.bank[tt // 4], 1, tt)
                if tt % 4 == 3:
                    mm.then_inc(m.s_wo, 1)
    m.clear_semaphores()


def moe_block(nc, m, d, layer):
    halves = 2 * BATCH
    turn_bank = [m.bank[i] for i in (0, 1, 6, 7)]
    parts = EXPERTS * BATCH * FCH
    with nc.Block() as block:
        @block.sync
        def _(sp):
            for e in range(WRING, EXPERTS):
                sp.wait_ge(m.s_down_unit, BATCH * FCH * (e - WRING + 1))
                load_expert(sp, m, d, layer, e)

        @block.gpsimd
        def _(pool):
            for e in range(EXPERTS):
                w = e % WRING
                if e >= WRING:
                    pool.wait_ge(m.s_expert[w], 3 * 16)
                    pool.wait_ge(m.s_up, BATCH * FCH * (e - WRING + 1))
                if e:
                    pool.tensor_copy(m.w_hi[:, w, :], m.wgu[:, w, :]).then_inc(m.s_w_hi, 1)
                pool.wait_ge(m.s_w_hi, e + 1)
                pool.tensor_tensor(m.w_lo[:, w, :], m.wgu[:, w, :], m.w_hi[:, w, :].bitcast(F32), ALU.subtract).then_inc(m.s_w_lo, 1)

        @block.vector
        def _(dve):
            def gated(i):
                dve.wait_ge(m.s_silu, i + 1)
                dve.wait_ge(m.s_up, i + 1)
                if i >= 2:
                    dve.wait_ge(m.s_down_unit, i - 1)
                dve.tensor_tensor(m.act_in[i % 2][:, :], m.up_bank[:, :], m.silu[i % 2][:, :], ALU.mult).then_inc(m.s_gated, 1)

            for b in range(BATCH):
                dve.tensor_tensor(m.normal[:, b, :, :], m.x[:, b, :, :], m.x[:, b, :, :], ALU.mult).then_inc(m.s_norm_v, 1)
                dve.wait_ge(m.s_norm_v, 3 * b + 1)
                dve.reduce_sum(m.stat[:, 0, b, :], m.normal[:, b, :, :], AX.X).then_inc(m.s_norm_v, 1)
                dve.wait_ge(m.s_norm_a, 2 * (b + 1))
                dve.tensor_tensor(m.normal[:, b, :, :], m.x[:, b, :, :], m.stat[:, 2, b, :].unsqueeze(2).broadcast_to([P, TT, P]),
                                  ALU.mult).then_inc(m.s_norm_v, 1)
                if b == 1:
                    gated(0)
                for i in range(2 * b, 2 * b + 2):
                    t = slice(i * HALF, (i + 1) * HALF)
                    dve.wait_ge(m.s_h_hi, i + 1)
                    dve.tensor_tensor(m.h_lo[:, t], m.h[:, t], m.h_hi[:, t].bitcast(F32), ALU.subtract).then_inc(m.s_h_lo, 1)

            pick, k = m.pick, 0

            def wide(a):
                return a.unsqueeze(2).broadcast_to([P, BATCH * TT, EXPERTS])

            def then(ins):
                nonlocal k
                k += 1
                ins.then_inc(m.s_pick, 1)
                dve.wait_ge(m.s_pick, k)

            def hot(values, to, largest, first):
                then(dve.reduce_max(largest, values, AX.X))
                then(dve.tensor_tensor(to, values, wide(largest), ALU.is_equal))
                then(dve.tensor_scalar(m.rank[:, :, :], m.expert_no[:, :, :], -1.0, float(EXPERTS), ALU.mult, ALU.add))
                then(dve.tensor_tensor(m.rank[:, :, :], m.rank[:, :, :], to, ALU.mult))
                then(dve.reduce_max(first, m.rank[:, :, :], AX.X))
                then(dve.tensor_tensor(to, m.rank[:, :, :], wide(first), ALU.is_equal))

            def shares():
                dve.wait_ge(m.s_routed, 1)
                hot(pick[:, 1, :, :], pick[:, 2, :, :], m.top[:, 1, :], m.top[:, 2, :])
                then(dve.scalar_tensor_tensor(pick[:, 3, :, :], pick[:, 1, :, :], 1.0, pick[:, 2, :, :], ALU.add, ALU.mult))
                then(dve.tensor_tensor(pick[:, 3, :, :], pick[:, 1, :, :], pick[:, 3, :, :], ALU.subtract))
                hot(pick[:, 3, :, :], pick[:, 4, :, :], m.top[:, 3, :], m.top[:, 4, :])
                then(dve.tensor_tensor(pick[:, 4, :, :], pick[:, 4, :, :], pick[:, 2, :, :], ALU.add))
                then(dve.tensor_tensor(pick[:, 4, :, :], pick[:, 4, :, :], pick[:, 1, :, :], ALU.mult))
                then(dve.reduce_sum(m.top[:, 5, :], pick[:, 4, :, :], AX.X))
                then(dve.reciprocal(m.top[:, 6, :], m.top[:, 5, :]))
                then(dve.tensor_tensor(m.share[:, :, :], pick[:, 4, :, :], wide(m.top[:, 6, :]), ALU.mult))

            dve.wait_ge(m.s_router, 1)
            logits = m.bank[4][:, 0:BATCH * TT * EXPERTS].rearrange("p (t e) -> p t e", e=EXPERTS)
            then(dve.reduce_max(m.top[:, 0, :], logits, AX.X))
            then(dve.tensor_tensor(pick[:, 0, :, :], logits, wide(m.top[:, 0, :]), ALU.subtract))

            def weigh(n):
                e, b = divmod(n, BATCH)
                dve.wait_ge(m.s_down_unit, FCH * (n + 1))
                if n >= BATCH:
                    dve.wait_ge(m.s_weighed, TT * (n - 1))
                for tt in range(TT):
                    dve.scalar_tensor_tensor(m.moe[:, b, tt, :],
                                             m.down_bank[n % 2][:, tt * C:(tt + 1) * C],
                                             m.share[:, b * TT + tt, e:e + 1], m.moe[:, b, tt, :] if e else m.x[:, b, tt, :],
                                             ALU.mult, ALU.add).then_inc(m.s_weighed, 1)

            for n in range(EXPERTS * BATCH):
                for f in range(FCH):
                    if n or f:
                        gated(n * FCH + f)
                    if f == 0 and n:
                        weigh(n - 1)
                if n == 0:
                    shares()
            weigh(EXPERTS * BATCH - 1)
            dve.wait_ge(m.s_weighed, TT * EXPERTS * BATCH)
            dve.tensor_scalar(m.x[:, :, :, :], m.moe[:, :, :, :], -LIMIT, LIMIT, ALU.max, ALU.min).then_inc(m.s_sum, 1)
            dve.wait_ge(m.s_sum, 1)

        @block.scalar
        def _(act):
            act.preload_act_table_set("natural_log_exp_and_others")
            act.copy(m.w_hi[:, 0, :], m.wgu[:, 0, :]).then_inc(m.s_w_hi, 1)
            def silu(i):
                act.wait_ge(m.s_gate, i + 1)
                if i >= 2:
                    act.wait_ge(m.s_gated, i - 1)
                act.activation(m.silu[i % 2][:, :], m.gate_bank[:, :], ACT.Silu).then_inc(m.s_silu, 1)

            for b in range(BATCH):
                act.wait_ge(m.s_norm_v, 3 * b + 2)
                act.activation(m.stat[:, 1, b, :], m.stat[:, 0, b, :], ACT.Ln, bias=m.eps[:, 0:1], scale=1.0 / C).then_inc(m.s_norm_a, 1)
                act.wait_ge(m.s_norm_a, 2 * b + 1)
                act.activation(m.stat[:, 2, b, :], m.stat[:, 1, b, :], ACT.Exp, scale=-0.5).then_inc(m.s_norm_a, 1)
                if b == 1:
                    silu(0)
                for i in range(2 * b, 2 * b + 2):
                    t = slice(i * HALF, (i + 1) * HALF)
                    act.wait_ge(m.s_turn_x, i + 1)
                    act.mul(m.h[:, t], turn_bank[i][:, :], m.ln2[:, 0:1]).then_inc(m.s_hT, 1)
                    act.wait_ge(m.s_hT, i + 1)
                    act.copy(m.h_hi[:, t], m.h[:, t]).then_inc(m.s_h_hi, 1)
            silu(1)
            act.wait_ge(m.s_pick, 2)
            act.activation(m.pick[:, 1, :, :], m.pick[:, 0, :, :], ACT.Exp).then_inc(m.s_routed, 1)
            for i in range(2, parts):
                silu(i)

        @block.tensor
        def _(pe):
            def turn(b):
                pe.wait_ge(m.s_norm_v, 3 * (b + 1))
                for i in range(2 * b, 2 * b + 2):
                    for tt in range(4):
                        mm = pe.transpose(turn_bank[i][:, tt * P:(tt + 1) * P], m.normal[:, b, i % 2 * 4 + tt, :], m.ident[:, :])
                    mm.then_inc(m.s_turn_x, 1)

            def router():
                pe.wait_ge(m.s_hT, halves)
                for tt in range(BATCH * TT):
                    mm = pe.matmul(m.bank[4][:, tt * EXPERTS:(tt + 1) * EXPERTS], m.h[:, tt * P:(tt + 1) * P], m.wr[:, :],
                                   start=True, stop=True)
                mm.then_inc(m.s_router, 1)

            def product(bank, w, column, b):
                cols = slice(column, column + P)
                terms = ((m.w_hi, m.h_hi), (m.w_hi, m.h_lo), (m.w_lo, m.h_hi))
                for x, (weight, h) in enumerate(terms):
                    for half in range(2):
                        t = slice(half * HALF, (half + 1) * HALF)
                        source = slice(b * T + half * HALF, b * T + (half + 1) * HALF)
                        mm = pe.matmul(bank[:, t], weight[:, w, cols], h[:, source], start=(x == 0), stop=(x == len(terms) - 1))
                return mm

            def hidden(i):
                n, f = divmod(i, FCH)
                e, b = divmod(n, BATCH)
                w = e % WRING
                if i % (BATCH * FCH) == 0:
                    pe.wait_ge(m.s_w_lo, e + 1)
                if i % FCH == 0 and e == 0:
                    pe.wait_ge(m.s_h_lo, 2 * (b + 1))
                if i >= 1:
                    pe.wait_ge(m.s_silu, i)
                product(m.gate_bank, w, f * P, b).then_inc(m.s_gate, 1)
                if i >= 1:
                    pe.wait_ge(m.s_gated, i)
                product(m.up_bank, w, FF + f * P, b).then_inc(m.s_up, 1)

            def down(i):
                n, f = divmod(i, FCH)
                pe.wait_ge(m.s_gated, i + 1)
                if f == 0 and n == 1:
                    pe.wait_ge(m.s_pick, 2)
                if f == 0 and n >= 2:
                    pe.wait_ge(m.s_weighed, TT * (n - 1))
                for tt in range(TT):
                    mm = pe.matmul(m.down_bank[n % 2][:, tt * C:(tt + 1) * C], m.act_in[i % 2][:, tt * P:(tt + 1) * P],
                                   m.wd[:, n // BATCH % WRING, f, :], start=(f == 0 and tt % 4 == 0), stop=(f == FCH - 1),
                                   skip_group_check=True)
                mm.then_inc(m.s_down_unit, 1)

            turn(0)
            for i in range(parts):
                hidden(i)
                if i:
                    down(i - 1)
                else:
                    turn(1)
                    router()
            down(parts - 1)
    m.clear_semaphores()


def decoder_tensors(m):
    m.q_full = [m.sb(f"q_full{i}", [P, REP, T], F32R) for i in range(2)]
    parts = m.q_full[0][:, :, :].rearrange("p h t -> p (h t)")
    m.h_hi, m.h_lo = parts[:, 0:BATCH * T], parts[:, BATCH * T:2 * BATCH * T]
    parts = m.q_full[1][:, :, :].rearrange("p h t -> p (h t)")
    m.w_hi, m.w_lo = (parts[:, i * WRING * 2 * FF:(i + 1) * WRING * 2 * FF].rearrange("p (w n) -> p w n", w=WRING) for i in range(2))
    m.q_shift = [m.sb(f"q_shift{i}", [KROWS, REP, T], F32R) for i in range(2)]
    m.k_twice = [m.sb(f"k_twice{i}", [P, T], F32R) for i in range(2)]
    m.k_rest = [m.sb(f"k_rest{i}", [KROWS, T], F32R) for i in range(2)]
    m.values = [m.sb(f"values{i}", [P, TT, HD]) for i in range(2)]
    m.ones = m.sb("ones", [P, HD])
    m.raw = m.sb("raw", [P, RAW, REP + 1, HD])
    m.swapped = m.sb("swapped", [P, RAW, REP + 1, HD])
    m.rotated = m.sb("rotated", [P, TT, REP + 1, HD])
    m.probs = [m.sb(f"probs{i}", [P, 2, HALF]) for i in range(PROBS)]
    m.prob_sum = [m.sb(f"prob_sum{i}", [P, 2, HALF]) for i in range(2)]
    m.mixed = m.sb("mixed", [P, NH // 2, T])
    m.silu = [m.mixed[:, i, :] for i in range(2)]
    m.act_in = [m.mixed[:, 2 + i, :] for i in range(2)]
    m.moe = m.mixed[:, 4:6, :].rearrange("p b (t c) -> p b t c", c=C)
    m.normal = m.moe
    m.h = m.mixed[:, 6:8, :].rearrange("p b t -> p (b t)")
    m.x, m.square = m.sb("x", [P, BATCH, TT, C]), m.sb("square", [P, TT, C])
    m.recip = m.sb("recip", [P, HALF])
    m.maxima = [m.sb(f"maxima{i}", [P, REP, TT]) for i in range(2)]
    m.maxima2 = [m.sb(f"maxima2{i}", [P, REP, TT]) for i in range(2)]
    m.maxrow = [m.sb(f"maxrow{i}", [2 * TT, P], F32R) for i in range(2)]
    m.hT = m.sb("hT", [C, T])
    m.stat = m.sb("stat", [P, 3, BATCH, TT])
    m.ln1, m.ln2 = m.sb("ln1", [C, 1]), m.sb("ln2", [C, 1])
    m.wqkv = m.sb("wqkv", [C, NKV, GW])
    m.wo = m.sb("wo", [P, NH // 2, C])
    m.wr = m.sb("wr", [C, EXPERTS])
    m.wgu = m.sb("wgu", [C, WRING, 2 * FF])
    m.wd = m.sb("wd", [P, WRING, FCH, C])
    m.expert_no = m.sb("expert_no", [P, BATCH * TT, EXPERTS])
    room, at = m.probs[0][:, :, :].rearrange("p k n -> p (k n)"), 0
    for name, kinds in (("rank", 1), ("share", 1), ("pick", 5)):
        n = kinds * BATCH * TT * EXPERTS
        part = room[:, at:at + n]
        if name == "pick":
            m.pick = part.rearrange("p (k t e) -> p k t e", k=kinds, e=EXPERTS)
        elif name == "rank":
            m.rank = part.rearrange("p (t e) -> p t e", e=EXPERTS)
        else:
            m.share = part.rearrange("p (t e) -> p t e", e=EXPERTS)
        at += n
    m.top = room[:, at:at + 7 * BATCH * TT].rearrange("p (k t) -> p k t", k=7)



def branch_weights(m):
    m.w_twice = m.sb("w_twice", [C, STACKS, P])
    m.b_twice = m.sb("b_twice", [P, STACKS])
    m.widen = m.sb("widen", [P, 4 * STATE_TILES // 2, P], F32R)
    m.sum_rows = m.sb("sum_rows", [P, STATE_TILES, P])
    m.same_head = m.sb("same_head", [P, P])
    m.stacker = m.sb("stacker", [P, 4, P])
    m.head_mask = m.sb("head_mask", [P, 4])
    m.w_turned = m.sb("w_turned", [C, 4, C])
    m.b_col = m.sb("b_col", [P, 2])
    m.b_row = m.sb("b_row", [P, 2, C])
    m.temps = m.sb("temps", [P, 1 + AH])


def branch_weights_block(nc, m, d):
    with nc.Block() as block:
        @block.sync
        def _(sp):
            loads = ((m.w_twice[:, :, :], d["w_twice"].rearrange("k c n -> c k n")), (m.b_twice[:, :], d["b_twice"]),
                     (m.widen_loaded[:, :, :], d["widen"].rearrange("j p n -> p j n")),
                     (m.sum_rows[:, :, :], d["sum_rows"].rearrange("j p n -> p j n")), (m.same_head[:, :], d["same_head"]),
                     (m.stacker[:, :, :], d["stacker"].rearrange("g p n -> p g n")), (m.head_mask[:, :], d["head_mask"]),
                     (m.w_turned[:, :, :], d["w_turned"].rearrange("k c n -> c k n")), (m.b_col[:, :], d["b_col"]),
                     (m.b_row[:, :, :], d["b_row"].unsqueeze(0).broadcast_to([P, 2, C])), (m.temps[:, 0:1], d["temp_col"]),
                     (m.temps[:, 1:1 + AH], d["temp_row"].unsqueeze(0).broadcast_to([P, AH])))
            for to, source in loads:
                sp.dma_start(to, source).then_inc(m.s_load, 16)
            sp.wait_ge(m.s_load, 16 * len(loads))

        @block.vector
        def _(dve):
            dve.wait_ge(m.s_load, 16 * 12)
            dve.tensor_scalar(m.b_twice[:, GATES:GATES + 1], m.b_twice[:, GATES:GATES + 1], -1.0, None, ALU.mult).then_inc(m.s_norm_v, 1)
            dve.tensor_copy(m.widen[:, :, :], m.widen_loaded[:, :, :]).then_inc(m.s_norm_v, 1)
            dve.wait_ge(m.s_norm_v, 2)
    m.clear_semaphores()


def branch_tensors(m):
    m.scale_work = m.sb("scale_work", [P, 4, 1 + AH])
    m.scale = m.sb("scale", [P, 1 + AH])
    m.shift = m.sb("shift", [P, AH])
    m.xT = m.sb("xT", [C, T])
    m.seqT = m.sb("seqT", [P, T])
    m.qk = [m.sb(f"qk{i}", [P, T]) for i in range(2)]
    m.qk_square = [m.sb(f"qk_square{i}", [P, T]) for i in range(2)]
    m.qk_norm = [m.sb(f"qk_norm{i}", [P, T]) for i in range(2)]
    m.q_stack = [m.sb(f"q_stack{i}", [P, T], F32R) for i in range(4)]
    m.key_stack = [m.sb(f"key_stack{i}", [P, T], F32R) for i in range(4)]


def recurrence_tensors(m):
    m.stack = [m.sb(f"stack{i}", [P, T], F32R) for i in range(STACKS)]
    m.gates = m.sb("gates", [P, T])
    m.key_wide = [m.sb(f"key_wide{i}", [P, HALF]) for i in range(2)]
    m.decay = [m.sb(f"decay{i}", [P, HALF]) for i in range(2)]
    m.outer = [m.sb(f"outer{i}", [P, HALF]) for i in range(2)]
    m.read = [m.sb(f"read{i}", [P, HALF]) for i in range(2)]
    m.state = m.sb("state", [P, STATE_TILES, 2, HALF])


def attention_tensors(m):
    m.key_head = [m.sb(f"key_head{i}", [P, T], F32R) for i in range(AH // 2)]
    m.weights = [m.sb(f"weights{i}", [P, 2, HALF]) for i in range(4)]
    m.recip_a = [m.sb(f"recip_a{i}", [32, HALF]) for i in range(2)]
    m.mixedT = m.sb("mixedT", [P, T])
    m.v_wide = m.sb("v_wide", [P, TT, AH, 64])


def recurrence_block(nc, m, d):
    kinds = 4

    def source(j, kind):
        group = 2 * j // STATE_TILES
        if kind == 1:
            return GATES, STATE_TILES + j
        return 3 * group + (kind + 1) // 2 + (group and 1), (STATE_TILES // 2 if kind == 2 else 0) + j % (STATE_TILES // 2)

    with nc.Block() as block:
        @block.tensor
        def _(pe):
            for tt in range(TT):
                mm = pe.transpose(m.bank[tt // 4][:, (tt % 4) * P:(tt % 4 + 1) * P], m.x[:, tt, :], m.ident[:, :])
                if tt % 4 == 3:
                    mm.then_inc(m.s_turn_x, 1)
            pe.wait_ge(m.s_hT, 2)
            for n in range(STACKS):
                if n >= 4:
                    pe.wait_ge(m.s_low, n - 3)
                for half in range(2):
                    t = slice(half * HALF, (half + 1) * HALF)
                    mm = pe.matmul(m.pair_bank[(n + 1) % 4][:, t], m.w_twice[:, n, :], m.xT[:, t], start=True, stop=True)
                mm.then_inc(m.s_stacked, 1)
            pe.wait_ge(m.s_low, STACKS)

            def project(n):
                i, kind = divmod(n, kinds)
                half, j = divmod(i, STATE_TILES)
                if n >= 6:
                    sem = (m.s_key_wide, m.s_decay, m.s_outer, m.s_read)[(n - 6) % kinds]
                    pe.wait_ge(sem, (n - 6) // kinds + 1 + (sem is m.s_decay))
                stack, picker = source(j, kind)
                pe.matmul(m.bank[n % 6][:, :], m.widen[:, picker, :], m.stack[stack][:, half * HALF:(half + 1) * HALF],
                          start=True, stop=True).then_inc(m.s_unit, 1)

            def gather(i):
                half, j = divmod(i, STATE_TILES)
                pe.wait_ge(m.s_read, i + 1)
                pe.matmul(m.bank[6 + half][:, :], m.sum_rows[:, j, :], m.read[i % 2][:, :],
                          start=(j == 0), stop=(j == STATE_TILES - 1)).then_inc(m.s_gathered, 1)

            for i in range(2 * STATE_TILES):
                for kind in range(kinds):
                    project(i * kinds + kind)
                if i:
                    gather(i - 1)
            gather(2 * STATE_TILES - 1)

        @block.scalar
        def _(act):
            for i in range(2):
                act.wait_ge(m.s_turn_x, i + 1)
                act.copy(m.xT[:, i * HALF:(i + 1) * HALF], m.bank[i][:, :]).then_inc(m.s_hT, 1)
            for n in range(STACKS):
                act.wait_ge(m.s_stacked, n + 1)
                bank = m.pair_bank[(n + 1) % 4]
                if n == GATES:
                    act.activation(m.gates[:, :], bank[:, :], ACT.Sigmoid, bias=m.b_twice[:, n:n + 1], scale=-1.0).then_inc(m.s_decay, 1)
                    act.wait_ge(m.s_decay, 1)
                    act.copy(m.stack[n][:, :], m.gates[:, :]).then_inc(m.s_high, 1)
                else:
                    act.activation(m.stack[n][:, :], bank[:, :], ACT.Identity, bias=m.b_twice[:, n:n + 1]).then_inc(m.s_high, 1)
            for i in range(2 * STATE_TILES):
                act.wait_ge(m.s_unit, kinds * i + 1)
                if i >= 2:
                    act.wait_ge(m.s_outer, i - 1)
                act.copy(m.key_wide[i % 2][:, :], m.bank[(kinds * i) % 6][:, :]).then_inc(m.s_key_wide, 1)
                act.wait_ge(m.s_unit, kinds * i + 2)
                if i >= 2:
                    act.wait_ge(m.s_state, i - 1)
                act.copy(m.decay[i % 2][:, :], m.bank[(kinds * i + 1) % 6][:, :]).then_inc(m.s_decay, 1)
            for half in range(2):
                act.wait_ge(m.s_gathered, (half + 1) * STATE_TILES)
                act.copy(m.seqT[:, half * HALF:(half + 1) * HALF], m.bank[6 + half][:, :]).then_inc(m.s_hT, 1)
            act.wait_ge(m.s_scale, 2)
            act.activation(m.scale_work[:, 2, :], m.scale_work[:, 1, :], ACT.Exp, scale=-1.0).then_inc(m.s_norm_a, 1)
            act.wait_ge(m.s_norm_a, 1)
            act.activation(m.scale_work[:, 3, :], m.scale_work[:, 2, :], ACT.Ln, bias=1.0).then_inc(m.s_norm_a, 1)

        @block.vector
        def _(dve):
            dve.tensor_scalar(m.scale_work[:, 1, :], m.temps[:, :], -1.0, None, ALU.mult).then_inc(m.s_scale, 1)
            dve.wait_ge(m.s_scale, 1)
            dve.tensor_tensor(m.scale_work[:, 1, :], m.scale_work[:, 1, :], m.temps[:, :], ALU.max).then_inc(m.s_scale, 1)

            for n in range(STACKS):
                dve.wait_ge(m.s_high, n + 1)
                low = m.stack[n][P // 2:P, :]
                if n == GATES:
                    dve.tensor_tensor(low, m.gates[P // 2:P, :], low.bitcast(F32), ALU.subtract).then_inc(m.s_low, 1)
                else:
                    dve.scalar_tensor_tensor(low, m.pair_bank[(n + 1) % 4][P // 2:P, :], m.b_twice[P // 2:P, n:n + 1],
                                             low.bitcast(F32), ALU.add, ALU.subtract).then_inc(m.s_low, 1)

            def read_out(i):
                j = i % STATE_TILES
                dve.wait_ge(m.s_unit, kinds * i + 4)
                if i >= 2:
                    dve.wait_ge(m.s_gathered, i - 1)
                dve.tensor_tensor(m.read[i % 2][:, :], m.bank[(kinds * i + 3) % 6][:, :], m.state[:, j, i // STATE_TILES, :],
                                  ALU.mult).then_inc(m.s_read, 1)

            for i in range(2 * STATE_TILES):
                half, j = divmod(i, STATE_TILES)
                dve.wait_ge(m.s_unit, kinds * i + 3)
                dve.wait_ge(m.s_key_wide, i + 1)
                if i >= 2:
                    dve.wait_ge(m.s_state, i - 1)
                dve.tensor_tensor(m.outer[i % 2][:, :], m.bank[(kinds * i + 2) % 6][:, :], m.key_wide[i % 2][:, :],
                                  ALU.mult).then_inc(m.s_outer, 1)
                dve.wait_ge(m.s_decay, i + 2)
                dve.wait_ge(m.s_outer, i + 1)
                dve.tensor_tensor_scan(m.state[:, j, half, :], m.decay[i % 2][:, :], m.outer[i % 2][:, :],
                                       m.state[:, j, 0, HALF - 1:HALF] if half else 0.0,
                                       ALU.mult, ALU.add).then_inc(m.s_state, 1)
                dve.wait_ge(m.s_state, i + 1)
                read_out(i)
            dve.wait_ge(m.s_norm_a, 2)
            dve.scalar_tensor_tensor(m.scale[:, :], m.temps[:, :], 0.0, m.scale_work[:, 3, :], ALU.max,
                                     ALU.add).then_inc(m.s_scale, 1)
            dve.wait_ge(m.s_scale, 3)
            dve.tensor_scalar(m.shift[:, :], m.scale[:, 1:1 + AH], -TALL, 0.0, ALU.add, ALU.max).then_inc(m.s_scale, 1)
            dve.wait_ge(m.s_scale, 4)
            dve.tensor_scalar(m.shift[:, :], m.shift[:, :], -1.0, None, ALU.mult).then_inc(m.s_scale, 1)
            dve.wait_ge(m.s_scale, 5)
    m.clear_semaphores()


def heads_block(nc, m):
    q, k = 0, 1
    with nc.Block() as block:
        @block.tensor
        def _(pe):
            for i in (q, k):
                for half in range(2):
                    t = slice(half * HALF, (half + 1) * HALF)
                    mm = pe.matmul(m.pair_bank[i][:, t], m.w_turned[:, i, :], m.seqT[:, t], start=True, stop=True)
                mm.then_inc(m.s_unit, 1)
            for tt in range(TT):
                mm = pe.matmul(m.pair_bank[2][:, tt * C:(tt + 1) * C], m.xT[:, tt * P:(tt + 1) * P], m.w_turned[:, 2, :],
                               start=True, stop=True)
            mm.then_inc(m.s_unit, 1)
            for i in (q, k):
                pe.wait_ge(m.s_square, i + 1)
                if i == k:
                    pe.wait_ge(m.s_value, 4)
                for half in range(2):
                    t = slice(half * HALF, (half + 1) * HALF)
                    mm = pe.matmul(m.pair_bank[3 - i][:, t], m.same_head[:, :], m.qk_square[i][:, t], start=True, stop=True)
                mm.then_inc(m.s_sumsq, 1)
            for n in range(8):
                i, g = divmod(n, 4)
                pe.wait_ge(m.s_unit_length, i + 1)
                if n >= 4:
                    pe.wait_ge(m.s_low, n - 3)
                for half in range(2):
                    t = slice(half * HALF, (half + 1) * HALF)
                    mm = pe.matmul(m.pair_bank[n % 4][:, t], m.stacker[:, g, :], m.qk[i][:, t], start=True, stop=True)
                mm.then_inc(m.s_stacked, 1)

        @block.gpsimd
        def _(pool):
            pool.memset(m.v_wide[:, :, :, :], 0.0).then_inc(m.s_set, 1)

        @block.scalar
        def _(act):
            act.preload_act_table_set("natural_log_exp_and_others")
            for i in (q, k):
                act.wait_ge(m.s_unit, i + 1)
                act.activation(m.qk[i][:, :], m.pair_bank[i][:, :], ACT.Identity, bias=m.b_col[:, i:i + 1]).then_inc(m.s_qk, 1)
            for i in (q, k):
                act.wait_ge(m.s_norm_v, i + 1)
                act.activation(m.qk_norm[i][:, :], m.qk_norm[i][:, :], ACT.Ln).then_inc(m.s_norm_a, 1)
                act.wait_ge(m.s_norm_a, 2 * i + 1)
                act.activation(m.qk_norm[i][:, :], m.qk_norm[i][:, :], ACT.Exp, scale=-0.5).then_inc(m.s_norm_a, 1)
            for n in range(8):
                act.wait_ge(m.s_stacked, n + 1)
                to = (m.q_stack if n < 4 else m.key_stack)[n % 4]
                act.copy(to[:, :], m.pair_bank[n % 4][:, :]).then_inc(m.s_high, 1)

        @block.vector
        def _(dve):
            dve.wait_ge(m.s_set, 1)
            v_wide = m.v_wide[:, :, :, :].rearrange("p t (g j) e -> p t g j e", j=4)
            dve.wait_ge(m.s_unit, 3)
            for j in range(4):
                cols = m.pair_bank[2][:, :].rearrange("p (t g n) -> p t g n", t=TT, g=4)[:, :, :, 8 * j:8 * j + 8]
                bias = m.b_row[:, 0, :].rearrange("p (g n) -> p g n", g=4)[:, :, 8 * j:8 * j + 8]
                dve.tensor_tensor(v_wide[:, :, :, j, 8 * j:8 * j + 8], cols,
                                  bias.unsqueeze(1).broadcast_to([P, TT, 4, 8]), ALU.add).then_inc(m.s_value, 1)
            for j in range(4):
                dve.memset(v_wide[:, :, :, j, 32 + 8 * j:40 + 8 * j], 1.0).then_inc(m.s_ones, 1)
            for i in (q, k):
                dve.wait_ge(m.s_qk, i + 1)
                dve.tensor_tensor(m.qk_square[i][:, :], m.qk[i][:, :], m.qk[i][:, :], ALU.mult).then_inc(m.s_square, 1)
            for i in (q, k):
                dve.wait_ge(m.s_sumsq, i + 1)
                dve.tensor_scalar(m.qk_norm[i][:, :], m.pair_bank[3 - i][:, :], 1e-24, None, ALU.max).then_inc(m.s_norm_v, 1)
            for i in (q, k):
                dve.wait_ge(m.s_norm_a, 2 * i + 2)
                if i == q:
                    dve.scalar_tensor_tensor(m.qk[i][:, :], m.qk[i][:, :], m.scale[:, 0:1], m.qk_norm[i][:, :],
                                             ALU.mult, ALU.mult).then_inc(m.s_unit_length, 1)
                else:
                    dve.tensor_tensor(m.qk[i][:, :], m.qk[i][:, :], m.qk_norm[i][:, :], ALU.mult).then_inc(m.s_unit_length, 1)
            for n in range(8):
                dve.wait_ge(m.s_high, n + 1)
                to = (m.q_stack if n < 4 else m.key_stack)[n % 4]
                parts = ((32, 64), (96, 128)) if n < 4 else ((64, 128),)
                for x, (a, b) in enumerate(parts):
                    dve.tensor_tensor(to[a:b, :], m.pair_bank[n % 4][a:b, :], to[a:b, :].bitcast(F32), ALU.subtract)\
                       .then_inc(m.s_low if x == len(parts) - 1 else m.s_low0, 1)
            dve.wait_ge(m.s_low, 8)
            dve.wait_ge(m.s_ones, 4)
    m.clear_semaphores()


def full_attention_steps():
    return [(gp, qc, j, 2 * kp, side) for gp in range(2) for qc in range(2) for j in range(4)
            for kp in range(TT // 2) for side in range(2)]


def full_attention_block(nc, m):
    steps = full_attention_steps()
    per_chunk = len(steps) // 4
    s_tile = m.pair_bank[0:3]
    heads_per_pair = AH // 2
    with nc.Block() as block:
        @block.vector
        def _(dve):
            def key_heads(gp):
                for j in range(4):
                    for side in range(2):
                        n = j * 2 + side
                        if gp:
                            dve.wait_ge(m.s_scores, per_chunk + (j + 1) * TT - 1 + side)
                        dve.tensor_scalar(m.key_head[n][:, :], m.key_stack[2 * gp + side][:, :].bitcast(F32),
                                          m.head_mask[:, j:j + 1], None, ALU.mult).then_inc(m.s_key_head, 1)

            def store(ch):
                gp, qc = divmod(ch, 2)
                o = m.bank[6 + ch % 2]
                dve.wait_ge(m.s_pv, (ch + 1) * per_chunk // 2)
                for side in range(2):
                    n = 2 * ch + side
                    if ch:
                        dve.wait_ge(m.s_stored, n - 1)
                    dve.reciprocal(m.recip_a[side][:, :], o[64 * side + 32:64 * side + 64, :]).then_inc(m.s_recip, 1)
                    dve.wait_ge(m.s_recip, n + 1)
                    g = 2 * gp + side
                    dve.tensor_tensor(m.mixedT[32 * g:32 * g + 32, qc * HALF:(qc + 1) * HALF], o[64 * side:64 * side + 32, :],
                                      m.recip_a[side][:, :], ALU.mult).then_inc(m.s_stored, 1)

            dve.tensor_tensor(m.total[:, :, :], m.total[:, :, :], m.b_row[:, 1, :].unsqueeze(1).broadcast_to([P, TT, C]),
                              ALU.add).then_inc(m.s_sum, 1)
            key_heads(0)
            store(0)
            key_heads(1)
            store(1)
            store(2)
            store(3)
            dve.wait_ge(m.s_sum, 1)
            dve.wait_ge(m.s_wo, 1)
            dve.tensor_tensor(m.total[:, :, :], m.pair_bank[0][:, :].rearrange("p (t c) -> p t c", c=C), m.total[:, :, :],
                              ALU.add).then_inc(m.s_sum, 1)
            dve.wait_ge(m.s_sum, 2)

        @block.scalar
        def _(act):
            for s, (gp, qc, j, kb, side) in enumerate(steps):
                head = 4 * (2 * gp + side) + j
                act.wait_ge(m.s_scores, s + 1)
                if s >= 4:
                    act.wait_ge(m.s_pv, (s - 4) // 2 + 1)
                act.activation(m.weights[s % 4][:, :, :], s_tile[s % 3][:, :].rearrange("p (k q) -> p k q", k=2),
                               ACT.Exp, bias=m.shift[:, head:head + 1]).then_inc(m.s_probs, 1)

        @block.tensor
        def _(pe):
            def score(s):
                gp, qc, j, kb, side = steps[s]
                n = j * 2 + side
                if kb == 0 and qc == 0:
                    pe.wait_ge(m.s_key_head, gp * heads_per_pair + n + 1)
                if s >= 3:
                    pe.wait_ge(m.s_probs, s - 2)
                for i in range(2):
                    mm = pe.matmul(s_tile[s % 3][:, i * HALF:(i + 1) * HALF], m.key_head[n][:, (kb + i) * P:(kb + i + 1) * P],
                                   m.q_stack[2 * gp + side][:, qc * HALF:(qc + 1) * HALF], start=True, stop=True)
                mm.then_inc(m.s_scores, 1)

            def mix(pair):
                gp, qc, j, kb, _ = steps[2 * pair]
                ch = 2 * gp + qc
                pe.wait_ge(m.s_probs, 2 * pair + 2)
                if j == 0 and kb == 0 and ch >= 2:
                    pe.wait_ge(m.s_stored, 2 * (ch - 1))
                for i in range(2):
                    for side in range(2):
                        head = 4 * (2 * gp + side) + j
                        mm = pe.matmul(m.bank[6 + ch % 2][64 * side:64 * side + 64, :], m.v_wide[:, kb + i, head, :],
                                       m.weights[(2 * pair + side) % 4][:, i, :],
                                       start=(j == 0 and kb + i == 0), stop=(j == 3 and kb + i == TT - 1))
                mm.then_inc(m.s_pv, 1)

            for pair in range(len(steps) // 2):
                score(2 * pair)
                score(2 * pair + 1)
                if pair:
                    mix(pair - 1)
            mix(len(steps) // 2 - 1)
            pe.wait_ge(m.s_stored, 8)
            pe.wait_ge(m.s_probs, len(steps))
            for tt in range(TT):
                mm = pe.matmul(m.pair_bank[0][:, tt * C:(tt + 1) * C], m.mixedT[:, tt * P:(tt + 1) * P], m.w_turned[:, 3, :],
                               start=True, stop=True)
            mm.then_inc(m.s_wo, 1)
    m.clear_semaphores()


def semaphores(m):
    m.s_load = m.sem("load")
    m.s_key_wide = m.sem("key_wide")
    m.s_decay = m.sem("decay")
    m.s_outer = m.sem("outer")
    m.s_read = m.sem("read")
    m.s_gathered = m.sem("gathered")
    m.s_state = m.sem("state")
    m.s_scale = m.sem("scale")
    m.s_square = m.sem("square")
    m.s_qk = m.sem("qk")
    m.s_sumsq = m.sem("sumsq")
    m.s_unit_length = m.sem("unit_length")
    m.s_stacked = m.sem("stacked")
    m.s_key_head = m.sem("key_head")
    m.s_load_wo = m.sem("load_wo")
    m.s_load_moe = m.sem("load_moe")
    m.s_set = m.sem("set")
    m.s_ones = m.sem("ones")
    m.s_norm_v = m.sem("norm_v")
    m.s_norm_a = m.sem("norm_a")
    m.s_turn_x = m.sem("turn_x")
    m.s_hT = m.sem("hT")
    m.s_maxrow = m.sem("maxrow")
    m.s_pv = m.sem("pv")
    m.s_raw = m.sem("raw")
    m.s_cos = m.sem("cos")
    m.s_sin0 = m.sem("sin0")
    m.s_sin = m.sem("sin")
    m.s_rotated = m.sem("rotated")
    m.s_high = m.sem("high")
    m.s_second = m.sem("second")
    m.s_taken = m.sem("taken")
    m.s_add_v = m.sem("add_v")
    m.s_add_p = m.sem("add_p")
    m.s_low0 = m.sem("low0")
    m.s_low = m.sem("low")
    m.s_value = m.sem("value")
    m.s_max = m.sem("max")
    m.s_rowmax = m.sem("rowmax")
    m.s_unit = m.sem("unit")
    m.s_probs = m.sem("probs")
    m.s_scores = m.sem("scores")
    m.s_masked = m.sem("masked")
    m.s_recip = m.sem("recip")
    m.s_logden = m.sem("logden")
    m.s_stored = m.sem("stored")
    m.s_wo = m.sem("wo")
    m.s_sum = m.sem("sum")
    m.s_router = m.sem("router")
    m.s_routed = m.sem("routed")
    m.s_pick = m.sem("pick")
    m.s_silu = m.sem("silu")
    m.s_gate = m.sem("gate")
    m.s_w_hi = m.sem("w_hi")
    m.s_w_lo = m.sem("w_lo")
    m.s_h_hi = m.sem("h_hi")
    m.s_h_lo = m.sem("h_lo")
    m.s_up = m.sem("up")
    m.s_gated = m.sem("gated")
    m.s_down_unit = m.sem("down_unit")
    m.s_weighed = m.sem("weighed")
    m.s_shift = [m.sem(f"shift{i}") for i in range(2)]
    m.s_scratch = [m.sem(f"scratch{i}") for i in range(2)]
    m.s_expert = [m.sem(f"expert{i}") for i in range(WRING)]


def input_block(nc, m, d, b):
    with nc.Block() as block:
        @block.sync
        def _(sp):
            sp.dma_start(m.total[:, :, :], d["x"][b].rearrange("(t p) c -> p t c", p=P)).then_inc(m.s_load, 16)
            sp.wait_ge(m.s_load, 16)

        @block.vector
        def _(dve):
            dve.wait_ge(m.s_load, 16)
            for tt in range(TT):
                dve.bn_stats(m.bn[:, tt, :], m.total[:, tt, :]).then_inc(m.s_norm_v, 1)
            dve.wait_ge(m.s_norm_v, TT)
            for tt in range(TT):
                dve.bn_aggr(m.moments[:, tt, 0:2], m.bn[:, tt, :]).then_inc(m.s_norm_v, 1)
            dve.wait_ge(m.s_norm_v, 2 * TT)
            dve.tensor_tensor(m.square[:, :, :], m.total[:, :, :], m.moments[:, :, 0:1].broadcast_to([P, TT, C]),
                              ALU.subtract).then_inc(m.s_norm_v, 1)
            dve.wait_ge(m.s_norm_a, 2)
            dve.wait_ge(m.s_norm_v, 2 * TT + 1)
            dve.tensor_tensor(m.x[:, :, :], m.square[:, :, :], m.moments[:, :, 2:3].broadcast_to([P, TT, C]),
                              ALU.mult).then_inc(m.s_norm_v, 1)
            dve.wait_ge(m.s_norm_v, 2 * TT + 2)

        @block.scalar
        def _(act):
            act.wait_ge(m.s_norm_v, 2 * TT)
            act.activation(m.moments[:, :, 3:4], m.moments[:, :, 1:2], ACT.Ln, bias=m.eps[:, 0:1]).then_inc(m.s_norm_a, 1)
            act.wait_ge(m.s_norm_a, 1)
            act.activation(m.moments[:, :, 2:3], m.moments[:, :, 3:4], ACT.Exp, scale=-0.5).then_inc(m.s_norm_a, 1)
            act.wait_ge(m.s_norm_a, 2)
    m.clear_semaphores()


def leave_block(nc, m, b):
    with nc.Block() as block:
        @block.sync
        def _(sp):
            sp.dma_start(m.sums[b].rearrange("(t p) c -> p t c", p=P), m.total[:, :, :]).then_inc(m.s_load, 16)
            sp.dma_start(m.normed[b].rearrange("(t p) c -> p t c", p=P), m.x[:, :, :]).then_inc(m.s_load, 16)
            sp.wait_ge(m.s_load, 32)
    m.clear_semaphores()


def output_block(nc, m, out):
    total = m.mixed[:, 0:2, :].rearrange("p b (t c) -> p b t c", c=C)
    with nc.Block() as block:
        @block.vector
        def _(dve):
            for b in range(BATCH):
                dve.wait_ge(m.s_shift[b], 16)
                dve.tensor_tensor(total[:, b, :, :], total[:, b, :, :], m.x[:, b, :, :], ALU.add).then_inc(m.s_sum, 1)

        @block.sync
        def _(sp):
            for b in range(BATCH):
                sp.dma_start(total[:, b, :, :], m.sums[b].rearrange("(t p) c -> p t c", p=P)).then_inc(m.s_shift[b], 16)
            for b in range(BATCH):
                sp.wait_ge(m.s_sum, b + 1)
                sp.dma_start(out[b].rearrange("(t p) c -> p t c", p=P), total[:, b, :, :]).then_inc(m.s_load, 16)
            sp.wait_ge(m.s_load, 16 * BATCH)
    m.clear_semaphores()


def build_program(nc, d, out):
    with ExitStack() as ctx:
        m = Core(nc, ctx)
        semaphores(m)
        m.sums, m.normed = (nc.dram_tensor(n, (BATCH, T, C), F32, kind="Internal").ap() for n in ("sums", "normed"))
        m.scratch = [nc.dram_tensor(f"maxima_turned{i}", (2 * TT, P), F32, kind="Internal").ap() for i in range(2)]
        banks = m.psum("banks", [P, 8, HALF])
        m.bank = [banks[:, i, :] for i in range(8)]
        m.pair_bank = [banks[:, 2 * i:2 * i + 2, :].rearrange("p k n -> p (k n)") for i in range(4)]
        m.gate_bank, m.up_bank = m.pair_bank[0:2]
        m.down_bank = [m.pair_bank[3], m.pair_bank[2]]
        m.ident, m.ident16 = m.sb("ident", [P, P]), m.sb("ident16", [P, P], BF16)
        m.later16 = m.sb("later16", [P, P], BF16)
        m.cos, m.sin = m.sb("cos", [P, TT, HD]), m.sb("sin", [P, TT, HD])
        m.eps = m.sb("eps", [P, 1])
        with ExitStack() as m.ctx:
            m.later = m.sb("later", [P, P])
            first_constants(nc, m, d)
        with ExitStack() as branch:
            m.ctx = branch
            branch_weights(m)
            with ExitStack() as m.ctx:
                m.widen_loaded = m.sb("widen_loaded", [P, 4 * STATE_TILES // 2, P])
                branch_weights_block(nc, m, d)
            with nc.Fori(0, BATCH) as b, ExitStack() as m.ctx:
                m.total, m.x, m.square = (m.sb(n, [P, TT, C]) for n in ("total", "branch_x", "branch_square"))
                m.bn, m.moments = m.sb("bn", [P, TT, 6]), m.sb("moments", [P, TT, 4])
                input_block(nc, m, d, b)
                branch_tensors(m)
                outer = m.ctx
                with ExitStack() as m.ctx:
                    recurrence_tensors(m)
                    recurrence_block(nc, m, d)
                m.ctx = outer
                attention_tensors(m)
                heads_block(nc, m)
                full_attention_block(nc, m)
                leave_block(nc, m, b)
        with ExitStack() as m.ctx:
            decoder_tensors(m)
            decoder_start_block(nc, m)
            with nc.Fori(0, LAYERS) as layer:
                attention_block(nc, m, d, layer)
                moe_block(nc, m, d, layer)
            output_block(nc, m, out)


def rotary_tables():
    inverse = (np.float32(1.0) / (np.float32(10000.0) ** (np.arange(0, HD, 2, dtype=np.float32) / np.float32(HD)))).astype(np.float32)
    angles = np.arange(T, dtype=np.float32)[:, None] * inverse
    cos, sin = np.cos(angles), np.sin(angles)
    return np.concatenate([cos, cos], axis=1), np.concatenate([-sin, sin], axis=1)


def branch_constants():
    row = np.arange(P)
    state = np.arange(STATES)
    column = state // (AD * AD) * AD + state % AD
    sum_rows = (column[:, None] == row).astype(np.float32).reshape(STATE_TILES, P, P)
    same_head = (row[:, None] // AD == row // AD).astype(np.float32)
    head, d, e = state // (AD * AD), state // AD % AD, state % AD
    rows = [(head % 8 * AD + d)[:STATES // 2], (head % 8 * AD + e)[:STATES // 2], head]
    widen = np.concatenate([r.reshape(-1, 1, P) == row[:, None] % (P // 2) for r in rows]).astype(np.float32)
    stacker = np.stack([(row[:, None] == 32 * g + row % 32).astype(np.float32) for g in range(4)])
    head_mask = (row[:, None] % 32 // AD == np.arange(4)).astype(np.float32)
    return {"sum_rows": sum_rows, "widen": widen, "same_head": same_head, "stacker": stacker, "head_mask": head_mask}


def laid_out(given):
    half = np.arange(P) % (P // 2)
    kinds = [("Wsk", "bsk"), ("Wsv", "bsv"), ("Wsq", "bsq")]
    rows = [(*k, half) for k in kinds] + [("Wg", "bg", half % AH)] + [(*k, P // 2 + half) for k in kinds]
    return {
        "w_twice": np.stack([np.ascontiguousarray(given[w][i].T) for w, _, i in rows]),
        "b_twice": np.stack([given[b][i] for _, b, i in rows], axis=1),
        "w_turned": np.stack([np.ascontiguousarray(given[w].T) for w in ("Wq", "Wk", "Wv", "Wo")]),
        "b_col": np.stack([given["bq"], given["bk"]], axis=1),
        "b_row": np.stack([given["bv"], given["bo"]]),
        "temp_row": given["temp"].reshape(AH),
        "temp_col": np.repeat(given["temp"].reshape(AH), AD).reshape(P, 1),
    }


DECODER = ("ln1_w", "ln2_w", "wq", "wk", "wv", "wo", "wr", "wg", "wu", "wd")


def arrays_of(inputs):
    given = {name: np.ascontiguousarray(inputs[full]) for name, full in _INS.items()}
    cos, sin = rotary_tables()
    return {"x": given["x"], "cos": cos, "sin": sin, **{n: given[n] for n in DECODER}, **branch_constants(), **laid_out(given)}


_INS = {
    "x": "L0_attn_x", "Wsq": "L0_attn_Wsq", "bsq": "L0_attn_bsq", "Wsk": "L0_attn_Wsk", "bsk": "L0_attn_bsk",
    "Wsv": "L0_attn_Wsv", "bsv": "L0_attn_bsv", "Wg": "L0_attn_Wg", "bg": "L0_attn_bg", "Wq": "L0_attn_Wq",
    "bq": "L0_attn_bq", "Wk": "L0_attn_Wk", "bk": "L0_attn_bk", "Wv": "L0_attn_Wv", "bv": "L0_attn_bv",
    "Wo": "L0_attn_Wo", "bo": "L0_attn_bo", "temp": "L0_attn_temp", "ln1_w": "L0_ffn_ln1_w",
    "ln2_w": "L0_ffn_ln2_w", "wq": "L0_ffn_wq", "wk": "L0_ffn_wk", "wv": "L0_ffn_wv", "wo": "L0_ffn_wo",
    "wr": "L0_ffn_wr", "wg": "L0_ffn_wg", "wu": "L0_ffn_wu", "wd": "L0_ffn_wd",
}


def kernel(**inputs):
    import numpy as _np
    import concourse.bacc as _bacc
    from concourse import mybir as _mybir
    from concourse.bass_utils import run_bass_kernel_spmd as _run

    nc = _bacc.Bacc("TRN2", target_bir_lowering=False, num_devices=1)
    arrays, dram = {}, {}
    for name, a in arrays_of(inputs).items():
        a = _np.ascontiguousarray(a)
        arrays[f"in_{name}_dram"] = a
        dram[name] = nc.dram_tensor(f"in_{name}_dram", a.shape, _mybir.dt.from_np(a.dtype), kind="ExternalInput").ap()
    out = nc.dram_tensor("out_0_dram", (BATCH, T, C), _mybir.dt.float32, kind="ExternalOutput").ap()
    build_program(nc, dram, out)
    r = _run(nc, [arrays], core_ids=[0])
    return r.results[0]["out_0_dram"]
```
